# Optimizing a Trainium2 kernel written in Bass

```python
import numpy as np
import jax
import jax.numpy as jnp

def _softmax(x, axis=-1):
    return jax.nn.softmax(x, axis=axis)

def _gelu(x):
    return jax.nn.gelu(x, approximate=True)

def _silu(x):
    return jax.nn.silu(x)

def _sigmoid(x):
    return jax.nn.sigmoid(x)

def _layernorm(x, axis=-1, eps=1e-05):
    m = jnp.mean(x, axis=axis, keepdims=True)
    v = jnp.var(x, axis=axis, keepdims=True)
    return (x - m) / jnp.sqrt(v + eps)

def _scatter_add(tgt, idx, src, axis=0):
    return tgt.at[idx].add(src)

def _segment_sum(src, seg, n):
    return jax.ops.segment_sum(src, seg, n)
kernel_name = 'mk_flamingo_gated_d1_seqx_r4_c52442'

def setup_inputs(seed: int=0):
    np.random.seed(seed)
    _w = jnp.asarray

    def _rec_inputs():
        import jax
        import jax.numpy as jnp
        _rk = jax.random.key(seed)
        x = -0.000125 + 0.9999 * jax.random.normal(jax.random.fold_in(_rk, 1), (2, 512, 1024), jnp.float32)
        _lenS = 512 - jax.random.randint(jax.random.fold_in(_rk, 7), (2,), 0, max(1, 512 // 4) + 1, jnp.int32)
        _lenS2 = 1024 - jax.random.randint(jax.random.fold_in(_rk, 8), (2,), 0, max(1, 1024 // 4) + 1, jnp.int32)
        _ctx_4096P = jax.random.normal(jax.random.fold_in(_rk, 11), (2, 16, 1024), jnp.float32)
        _ctx_4096c = jax.random.dirichlet(jax.random.fold_in(_rk, 511), 0.3 * jnp.ones((16,), jnp.float32), (2, 1024))
        _ctx_4096t = jnp.einsum('bsk,bkd->bsd', _ctx_4096c, _ctx_4096P)
        _ctx_4096t = _ctx_4096t * jax.lax.rsqrt(jnp.mean(jnp.square(_ctx_4096t)) + 1e-12) * 0.953939
        ctx_4096 = -5.72187e-05 + 0.999849 * (_ctx_4096t + 0.3 * jax.random.normal(jax.random.fold_in(_rk, 611), (2, 1024, 1024), jnp.float32))
        _g = jax.random.normal(jax.random.fold_in(_rk, 9001), (2, 1), jnp.float32)
        _g = jnp.sign(_g) * jnp.maximum(jnp.abs(_g), 1.0) + (_g == 0) * 1.0
        g_xattn = _g[0]
        g_ffn = _g[1]
        return (x, ctx_4096, g_xattn, g_ffn)
    x, ctx_4096, g_xattn, g_ffn = _rec_inputs()

    def _L0_xattn_setup():
        import jax, jax.numpy as jnp
        import numpy as np
        QMIN = 0.0
        QMAX = 255.0

        def fake_quant(x, scale, zp):
            s = scale.reshape(())
            z = zp.reshape(())
            q = jnp.clip(jnp.round(x / s + z), QMIN, QMAX)
            return (q - z) * s
        key = jax.random.key(seed)
        k1, k2 = jax.random.split(key)
        B, M, K, N = (4, 512, 1024, 1024)
        x1 = jax.random.normal(k1, (B, M, K), dtype=jnp.float32)
        x2 = jax.random.normal(k2, (B, K, N), dtype=jnp.float32)
        x1_scale = jnp.full((1,), 8.0 / 255.0, dtype=jnp.float32)
        x1_zp = jnp.full((1,), 128.0, dtype=jnp.float32)
        x2_scale = jnp.full((1,), 8.0 / 255.0, dtype=jnp.float32)
        x2_zp = jnp.full((1,), 128.0, dtype=jnp.float32)
        return {'x1': x1, 'x2': x2, 'x1_scale': x1_scale, 'x1_zp': x1_zp, 'x2_scale': x2_scale, 'x2_zp': x2_zp}
    _L0_xattn_all = _L0_xattn_setup()
    _L0_xattn_in = {k: v for k, v in _L0_xattn_all.items() if k in ('x1_scale', 'x1_zp', 'x2_scale', 'x2_zp')}
    del _L0_xattn_all

    def _L0_ffn_setup():
        import jax, jax.numpy as jnp
        import numpy as np
        DIM = 1024
        INTER = 256
        E = 16
        GROUPS = 4
        LIM = 2
        K = 2
        SHARED_INTER = 2 * INTER
        SCALE = 1.0
        key = jax.random.key(seed)
        ks = jax.random.split(key, 16)

        def n(k, shape, s=0.02):
            return jax.random.normal(k, shape, jnp.float32) * s
        return {'x': jax.random.normal(ks[0], (1, 512, DIM), jnp.float32), 'router_w': n(ks[1], (DIM, E)), 'router_b': n(ks[2], (E,)), 'router_bias': n(ks[3], (E,), 1.0), 'ew1': n(ks[4], (E, DIM, INTER)), 'eb1': n(ks[5], (E, INTER)), 'ew2': n(ks[6], (E, DIM, INTER)), 'eb2': n(ks[7], (E, INTER)), 'ew3': n(ks[8], (E, INTER, DIM)), 'eb3': n(ks[9], (E, DIM)), 'sw1': n(ks[10], (DIM, SHARED_INTER)), 'sb1': n(ks[11], (SHARED_INTER,)), 'sw2': n(ks[12], (DIM, SHARED_INTER)), 'sb2': n(ks[13], (SHARED_INTER,)), 'sw3': n(ks[14], (SHARED_INTER, DIM)), 'sb3': n(ks[15], (DIM,))}
    _L0_ffn_all = _L0_ffn_setup()
    _L0_ffn_in = {k: v for k, v in _L0_ffn_all.items() if k in ('router_w', 'router_b', 'router_bias', 'ew1', 'eb1', 'ew2', 'eb2', 'ew3', 'eb3', 'sw1', 'sb1', 'sw2', 'sb2', 'sw3', 'sb3')}
    del _L0_ffn_all
    return {'x': x, 'ctx_4096': ctx_4096, 'g_xattn': g_xattn, 'g_ffn': g_ffn, 'L0_xattn_x1_scale': _L0_xattn_in['x1_scale'], 'L0_xattn_x1_zp': _L0_xattn_in['x1_zp'], 'L0_xattn_x2_scale': _L0_xattn_in['x2_scale'], 'L0_xattn_x2_zp': _L0_xattn_in['x2_zp'], 'L0_ffn_router_w': _L0_ffn_in['router_w'], 'L0_ffn_router_b': _L0_ffn_in['router_b'], 'L0_ffn_router_bias': _L0_ffn_in['router_bias'], 'L0_ffn_ew1': _L0_ffn_in['ew1'], 'L0_ffn_eb1': _L0_ffn_in['eb1'], 'L0_ffn_ew2': _L0_ffn_in['ew2'], 'L0_ffn_eb2': _L0_ffn_in['eb2'], 'L0_ffn_ew3': _L0_ffn_in['ew3'], 'L0_ffn_eb3': _L0_ffn_in['eb3'], 'L0_ffn_sw1': _L0_ffn_in['sw1'], 'L0_ffn_sb1': _L0_ffn_in['sb1'], 'L0_ffn_sw2': _L0_ffn_in['sw2'], 'L0_ffn_sb2': _L0_ffn_in['sb2'], 'L0_ffn_sw3': _L0_ffn_in['sw3'], 'L0_ffn_sb3': _L0_ffn_in['sb3']}

def reference(x, ctx_4096, g_xattn, g_ffn, L0_xattn_x1_scale, L0_xattn_x1_zp, L0_xattn_x2_scale, L0_xattn_x2_zp, L0_ffn_router_w, L0_ffn_router_b, L0_ffn_router_bias, L0_ffn_ew1, L0_ffn_eb1, L0_ffn_ew2, L0_ffn_eb2, L0_ffn_ew3, L0_ffn_eb3, L0_ffn_sw1, L0_ffn_sb1, L0_ffn_sw2, L0_ffn_sb2, L0_ffn_sw3, L0_ffn_sb3):
    import jax
    import jax.numpy as jnp

    def _L0_xattn_ref(x1, x2, x1_scale, x1_zp, x2_scale, x2_zp):
        import jax, jax.numpy as jnp
        import numpy as np
        QMIN = 0.0
        QMAX = 255.0

        def fake_quant(x, scale, zp):
            s = scale.reshape(())
            z = zp.reshape(())
            q = jnp.clip(jnp.round(x / s + z), QMIN, QMAX)
            return (q - z) * s
        q1 = fake_quant(x1, x1_scale, x1_zp)
        q2 = fake_quant(x2, x2_scale, x2_zp)
        return jnp.matmul(q1, q2)

    def _L0_ffn_ref(x, router_w, router_b, router_bias, ew1, eb1, ew2, eb2, ew3, eb3, sw1, sb1, sw2, sb2, sw3, sb3):
        import jax, jax.numpy as jnp
        import numpy as np
        DIM = 1024
        INTER = 256
        E = 16
        GROUPS = 4
        LIM = 2
        K = 2
        SHARED_INTER = 2 * INTER
        SCALE = 1.0
        shape = x.shape
        xt = x.reshape(-1, DIM)
        T = xt.shape[0]
        logits = xt @ router_w + router_b
        scores = jax.nn.softmax(logits.astype(jnp.float32), axis=-1) + router_bias
        g = scores.reshape(T, GROUPS, E // GROUPS)
        _, gidx = jax.lax.top_k(g.max(axis=-1), LIM)
        keep = jnp.zeros((T, GROUPS), bool).at[jnp.arange(T)[:, None], gidx].set(True)
        masked = jnp.where(keep[:, :, None], g, -jnp.inf).reshape(T, E)
        _, idx = jax.lax.top_k(masked, K)
        vals = (jnp.take_along_axis(scores, idx, axis=1) * SCALE).astype(x.dtype)
        gate = jnp.zeros((T, E), x.dtype).at[jnp.arange(T)[:, None], idx].add(vals)

        def step(y, p):
            w1, b1, w2, b2, w3, b3, ge = p
            h = jax.nn.silu(xt @ w1 + b1) * (xt @ w2 + b2)
            return (y + ge[:, None] * (h @ w3 + b3), None)
        y, _ = jax.lax.scan(step, jnp.zeros_like(xt), (ew1, eb1, ew2, eb2, ew3, eb3, gate.T))
        z = jax.nn.silu(xt @ sw1 + sb1) * (xt @ sw2 + sb2) @ sw3 + sb3
        return (y + z).reshape(shape)
    x = x + jnp.tanh(g_xattn[0]) * _L0_xattn_ref(_layernorm(x, axis=-1), ctx_4096, L0_xattn_x1_scale, L0_xattn_x1_zp, L0_xattn_x2_scale, L0_xattn_x2_zp)
    x = x + jnp.tanh(g_ffn[0]) * _L0_ffn_ref(_layernorm(x, axis=-1), L0_ffn_router_w, L0_ffn_router_b, L0_ffn_router_bias, L0_ffn_ew1, L0_ffn_eb1, L0_ffn_ew2, L0_ffn_eb2, L0_ffn_ew3, L0_ffn_eb3, L0_ffn_sw1, L0_ffn_sb1, L0_ffn_sw2, L0_ffn_sb2, L0_ffn_sw3, L0_ffn_sb3)
    return x

_drawn_inputs = setup_inputs


def setup_inputs(seed=0):
    import zlib

    import numpy as np

    out = dict(_drawn_inputs(seed))
    spreads = {}
    factors = {'L0_ffn_router_w': 66.565,
     'L0_ffn_router_b': 200.0,
     'L0_ffn_router_bias': 6.017,
     'L0_ffn_ew1': 6.415,
     'L0_ffn_eb1': 8.0,
     'L0_ffn_ew2': 6.174,
     'L0_ffn_eb2': 8.0,
     'L0_ffn_ew3': 6.13,
     'L0_ffn_eb3': 64.0,
     'L0_ffn_sw1': 8.0,
     'L0_ffn_sb1': 64.0,
     'L0_ffn_sw2': 8.0,
     'L0_ffn_sb2': 64.0,
     'L0_ffn_sw3': 8.0,
     'L0_ffn_sb3': 200.0}
    for name, (base, spread) in spreads.items():
        noise = np.random.default_rng([zlib.crc32(name.encode()), seed]).standard_normal(out[name].shape)
        drawn = base * np.exp(spread * noise) if base else spread * noise
        out[name] = jnp.asarray(drawn.astype(out[name].dtype))
    for name, factor in factors.items():
        out[name] = (out[name] * factor).astype(out[name].dtype)
    return out
```

```python
import concourse.bass as bass
from concourse import mybir
from contextlib import ExitStack

F32, F16, BF16, I32 = mybir.dt.float32, mybir.dt.float16, mybir.dt.bfloat16, mybir.dt.int32
ALU = mybir.AluOpType
ACT = mybir.ActivationFunctionType
AX = mybir.AxisListType.X

P = 128
B, S, D = 2, 512, 1024
KC = D // P
NT = B * S // P
TB = NT // B
E, INTER = 16, 256
GROUPS = 4
SI = 2 * INTER
SC = SI // P
HC = INTER // P
TOPK = 2
MAXT = E + (TOPK * NT * P - E) // P
MINT = TOPK * NT
STEPS = MAXT + 1
COLS = STEPS + 4

QMAX = 255.0
HALF = 128.0
ROUND = 12582912.0
XS = 16.0
WS = 16.0
HS = 0.25
UPS = XS * WS
DNS = HS * WS
SELV = 4.0
EPS = 1e-5
BIG = 1e30


def build(nc, x, ctx_in, g_xattn, g_ffn, x1_scale, x1_zp, x2_scale, x2_zp, router_w, router_b, router_bias,
          ew1, eb1, ew2, eb2, ew3, eb3, sw1, sb1, sw2, sb2, sw3, sb3, out):
    x_t = x.rearrange("b (t p) d -> (b t) p d", p=P)
    out_t = out.rearrange("b (t p) d -> (b t) p d", p=P)
    split_dram = nc.dram_tensor("split_dram", [NT * P, 2 * D], F16, kind="Internal").ap()
    slots_dram = nc.dram_tensor("slots_dram", [MAXT * P, D], F32, kind="Internal").ap()

    es = ExitStack()
    with es:
        def sb(name, shape, dt):
            return es.enter_context(nc.sbuf_tensor(name, shape, dt))

        sems = {}

        def sem(name):
            sems[name] = es.enter_context(nc.semaphore(name))
            return sems[name]

        X = sb("X", [P, NT, D], F32)
        areaT = sb("areaT", [P, 8192], F32)
        area2 = sb("area2", [P, 4096], F32)
        ring = sb("ring", [P, 4, D], F32)
        rows = sb("rows", [P, 2, D], F32)
        areaQ = sb("areaQ", [P, 3072], F32)
        wrow = sb("wrow", [P, 2, 2 * D], F16)
        areaW = sb("areaW", [P, 8192], F32)
        SW3 = sb("SW3", [P, 2, SC, D], F16)
        areaH = sb("areaH", [P, 2048], F32)
        SA = sb("SA", [P, 2, S], F32)

        def view(area, lo, n, dt, pat=None, **kw):
            v = area[:, lo:lo + n]
            if dt is not F32:
                v = v.bitcast(dt)
            return v.rearrange(pat, **kw) if pat else v

        XT = view(areaT, 0, 8192, F16, "p (h k t) -> p h k t", h=2, k=KC)
        Q2 = view(area2, 0, 4096, BF16, "p (k n) -> p k n", k=KC)
        Q1T = view(areaQ, 0, 2048, BF16, "p (j k t) -> p j k t", j=TB, k=KC)
        CT = view(areaQ, 2048, 1024, F32)
        SW = view(areaW, 0, 8192, F16, "p (h k n) -> p h k n", h=2, k=KC)
        HT = view(areaH, 0, 2048, F16, "p (h c t) -> p h c t", h=2, c=SC)
        bias32 = areaH[0:64, 0:1536]
        W12F = view(areaT, 0, 4096, F32, "p (k n) -> p k n", k=KC)
        W3S = [view(areaT, 4096 + 2048 * i, 2048, F16, "p (h c n) -> p h c n", h=2, c=HC) for i in range(2)]
        W3F = wrow[:, :, :].rearrange("p a n -> p (a n)").bitcast(F32).rearrange("p (c n) -> p c n", c=HC)
        W12S = [view(areaW, 4096 * i, 4096, F16, "p (h k n) -> p h k n", h=2, k=KC) for i in range(2)]
        XG = [view(area2, 1024 * i, 1024, F16, "p (h n) -> p h n", h=2) for i in range(2)]
        XGT = [view(area2, 2048 + 1024 * i, 1024, F16, "p (h k t) -> p h k t", h=2, k=KC) for i in range(2)]
        HF = [view(areaH, 256 * i, 256, F32) for i in range(2)]
        HSP = [view(areaH, 512 + 256 * i, 256, F16, "p (h n) -> p h n", h=2) for i in range(2)]
        HTS = [view(areaH, 1024 + 256 * i, 256, F16, "p (h c t) -> p h c t", h=2, c=HC) for i in range(2)]

        BS = sb("BS", [64, SI + D], F16)
        SEL = sb("SEL", [64, 3, P], F16)
        SELQ = sb("SELQ", [64, COLS], F32)
        RW32 = sb("RW32", [P, KC, E], F32)
        RW = sb("RW", [P, KC, 2, E], F16)
        rb = sb("rb", [P, 2, E], F32)
        sbT = sb("sbT", [P, 2, SC], F32)
        sc6 = sb("sc6", [P, 8], F32)
        cf = sb("cf", [P, 16], F32)
        stats = sb("stats", [P, NT, 12], F32)
        mv = sb("mv", [P, NT, 2], F32)
        lnA = sb("lnA", [P, NT], F32)
        lnB = sb("lnB", [P, NT], F32)
        lnR = sb("lnR", [P, NT], F32)
        lnV = sb("lnV", [P, NT], F32)
        mhalf = sb("mhalf", [P, TB], F32)
        r1 = sb("r1", [P, TB], F32)
        idf = sb("idf", [P, P], F32)
        idh = sb("idh", [P, P], F16)
        onesb = sb("onesb", [P, P], BF16)
        onesh = sb("onesh", [P, P], F16)
        tri = sb("tri", [P, P], F16)
        iota = sb("iota", [P, P], F32)
        pcol = sb("pcol", [P, 8], F32)
        desc = sb("desc", [P, E], F32)
        TI = sb("TI", [P, COLS], I32)
        tok1 = sb("tok1", [P, 2], I32)
        EL = sb("EL", [P, COLS], I32)
        LC = sb("LC", [P, COLS], I32)
        ntiles = sb("ntiles", [P, 1], I32)
        PI = sb("PI", [P, 2 * NT], I32)
        CV = sb("CV", [P, 2, NT], F32)

        PS = es.enter_context(nc.psum_tensor("PS", [P, 8, 512], F32))

        def bank16(b):
            return PS[:, b, :].bitcast(F16).rearrange("p (k t) -> p k t", k=KC)

        ofs = [0]

        def small(n, pat=None, dt=F32, **kw):
            lo = ofs[0]
            ofs[0] += n
            assert ofs[0] <= 3072
            return view(areaQ, lo, n, dt, pat, **kw)

        TE = "p (t e) -> p t e"
        lg = small(P, TE, t=NT)
        sco = small(P, TE, t=NT)
        t1 = small(P, TE, t=NT)
        t2 = small(P, TE, t=NT)
        oh = [small(P, TE, t=NT) for _ in range(2)]
        gm = small(NT * GROUPS, "p (t g) -> p t g", t=NT)
        gt = small(NT * GROUPS, "p (t g) -> p t g", t=NT)
        go = [small(NT * GROUPS, "p (t g) -> p t g", t=NT) for _ in range(2)]
        m8 = small(NT)
        Mh = small(P // 2, TE, dt=F16, t=NT)
        run = small((NT + 1) * E, "p (t e) -> p t e", t=NT + 1)
        sA = small(8 + E)
        sB = small(8 + E)
        ntl = small(E)
        base = small(E)
        pos = small(2 * NT, "p (j t) -> p j t", j=2)
        aa = small(2 * NT, "p (j t) -> p j t", j=2)
        bb = small(2 * NT, "p (j t) -> p j t", j=2)
        big = small(1024)
        GE = big[:, 0:2 * NT * 33].rearrange("p (j t a) -> p j t a", j=2, a=33)
        OB = view(areaQ, ofs[0] - 1024, 1024, F16, "p (j t s) -> p j t s", j=2, t=NT)
        OA = SA[:, 0, 0:256].bitcast(F16).rearrange("p (j t a) -> p j t a", j=2, a=32)
        ECM = SA[:, 1, :]

        x_in = [sem(f"x_in{i}") for i in range(NT)]
        ring_in = [sem(f"ring_in{i}") for i in range(4)]
        sw1_in = [sem(f"sw1_in{i}") for i in range(4)]
        small_in, bias_in = sem("small_in"), sem("bias_in")
        consts, ident_rdy, v_chain = sem("consts"), sem("ident_rdy"), sem("v_chain")
        coef1, tanh_rdy, mv_rdy, rstd_rdy = sem("coef1"), sem("tanh_rdy"), sem("mv_rdy"), sem("rstd_rdy")
        var_eps = sem("var_eps")
        y_relu, y_rnd, q1_T, q1_rdy = sem("y_relu"), sem("y_rnd"), sem("q1_T"), sem("q1_rdy")
        c_relu, c_rnd, q2_rdy = sem("c_relu"), sem("c_rnd"), sem("q2_rdy")
        sw_hi, sw_lo = sem("sw_hi"), sem("sw_lo")
        r1_done, r1_read, col_done, col_read = sem("r1_done"), sem("r1_read"), sem("col_done"), sem("col_read")
        at_done, at_read = sem("at_done"), sem("at_read")
        ln_xs, ln_hi, ln_lo = sem("ln_xs"), sem("ln_hi"), sem("ln_lo")
        split_out = [sem("split_out0"), sem("split_out1")]
        tk_T, tk_hi, tk_lo = sem("tk_T"), sem("tk_hi"), sem("tk_lo")
        rw_hi, rw_lo, bs_zero, bs_hi, bs_lo = sem("rw_hi"), sem("rw_lo"), sem("bs_zero"), sem("bs_hi"), sem("bs_lo")
        su_done, su_silu, su_hf, su_hi, su_lo = sem("su_done"), sem("su_silu"), sem("su_hf"), sem("su_hi"), sem("su_lo")
        sd_done, sd_read = sem("sd_done"), sem("sd_read")
        lg_done, lg_read, lg_sub, lg_exp = sem("lg_done"), sem("lg_read"), sem("lg_sub"), sem("lg_exp")
        m_rdy, rank_done, rank_read = sem("m_rdy"), sem("rank_done"), sem("rank_read")
        lc_rdy, zero_rdy, zero_out = sem("lc_rdy"), sem("zero_rdy"), sem("zero_out")
        el_rdy, slot_rdy, ti_done, ti_rdy = sem("el_rdy"), sem("slot_rdy"), sem("ti_done"), sem("ti_rdy")
        gathers, tok_rdy, tok_in = sem("gathers"), sem("tok_rdy"), [sem("tok_in0"), sem("tok_in1")]
        w12_in, w3_in = sem("w12_in"), sem("w3_in")
        w12_hi, w12_lo, w3_hi, w3_lo = sem("w12_hi"), sem("w12_lo"), sem("w3_hi"), sem("w3_lo")
        sel_rdy = sem("sel_rdy")
        xg_T, xg_hi, xg_lo = sem("xg_T"), sem("xg_hi"), sem("xg_lo")
        up_done, h_silu, h_prod, h_hi, h_lo = sem("up_done"), sem("h_silu"), sem("h_prod"), sem("h_hi"), sem("h_lo")
        hT_done, hT_rdy, dn_done, y_rdy = sem("hT_done"), sem("hT_rdy"), sem("dn_done"), sem("y_rdy")
        y_out = [sem("y_out0"), sem("y_out1")]
        slot_in = [sem(f"slot_in{i}") for i in range(4)]
        fin_half, fin_rdy, out_done = sem("fin_half"), sem("fin_rdy"), sem("out_done")

        block = es.enter_context(nc.Block())

        CHUNKS = ([("ctx", 0, k) for k in range(KC)] + [("sw", 0, k) for k in range(KC)]
                  + [("ctx", 1, k) for k in range(KC)] + [("sw3", 0, c) for c in range(SC)])
        RING_AT = {c: r for r, c in enumerate(CHUNKS)}

        def arrived(eng, r):
            eng.wait_ge(ring_in[r % 4], 16 * (r // 4 + 1))

        def consumed(r):
            kind, b, k = CHUNKS[r]
            if kind == "ctx":
                return q2_rdy, b * KC + k + 1
            return sw_lo, (k if kind == "sw" else KC + k) + 1

        def tile_count(eng):
            return eng.value_load(ntiles[0:1, 0:1], min_val=MINT, max_val=MAXT)

        def loads_before(eng, t):
            return eng.value_load(LC[0:1, bass.ds(t, 1)], min_val=1, max_val=MAXT)

        @block.sync
        def _(sp):
            for n, v in enumerate((x1_scale, x1_zp, x2_scale, x2_zp, g_xattn, g_ffn)):
                sp.dma_start(sc6[:, n:n + 1], v.partition_broadcast(P)).then_inc(small_in, 16)
            for i in range(TB):
                sp.dma_start(X[:, i, :], x_t[i]).then_inc(x_in[i], 16)

            def load_chunk(r):
                kind, b, k = CHUNKS[r]
                if r >= 4:
                    sp.wait_ge(*consumed(r - 4))
                rs = slice(k * P, (k + 1) * P)
                if kind == "ctx":
                    sp.dma_start(ring[:, r % 4, :], ctx_in[b, rs, :]).then_inc(ring_in[r % 4], 16)
                elif kind == "sw3":
                    sp.dma_start(ring[:, r % 4, :], sw3[rs, :]).then_inc(ring_in[r % 4], 16)
                else:
                    sp.dma_start(ring[:, r % 4, :].rearrange("p (w n) -> p w n", w=2)[:, 0, :], sw1[rs, :])\
                        .then_inc(sw1_in[r % 4], 16)
                    sp.dma_start(ring[:, r % 4, SI:2 * SI], sw2[rs, :]).then_inc(ring_in[r % 4], 16)

            for r in range(KC):
                load_chunk(r)
            sp.wait_ge(bs_zero, 1)
            for q in (0, 32):
                sp.dma_start(areaH[q:q + E, 0:INTER], eb1[:, :]).then_inc(bias_in, 16)
                sp.dma_start(areaH[q:q + E, INTER:SI], eb2[:, :]).then_inc(bias_in, 16)
                sp.dma_start(areaH[q:q + E, SI:SI + D], eb3[:, :]).then_inc(bias_in, 16)
                sp.dma_start(areaH[q + E:q + E + 1, SI:SI + D], sb3.rearrange("(a n) -> a n", a=1)).then_inc(bias_in, 16)
            sp.dma_start(rb[:, 0, :], router_b.partition_broadcast(P)).then_inc(bias_in, 16)
            sp.dma_start(rb[:, 1, :], router_bias.partition_broadcast(P)).then_inc(bias_in, 16)
            sp.dma_start(RW32[:, :, :], router_w.rearrange("(k p) e -> p k e", p=P)).then_inc(bias_in, 16)
            with nc.allow_non_contiguous_dma(reason="bias vectors laid along the partitions"):
                sp.dma_start(sbT[:, 0, :], sb1.rearrange("(c p) -> p c", p=P)).then_inc(bias_in, 16)
                sp.dma_start(sbT[:, 1, :], sb2.rearrange("(c p) -> p c", p=P)).then_inc(bias_in, 16)
            for r in range(KC, 2 * KC):
                load_chunk(r)
            for i in range(TB, NT):
                sp.dma_start(X[:, i, :], x_t[i]).then_inc(x_in[i], 16)

            def store_split(i):
                sp.wait_ge(ln_hi, i + 1)
                sp.wait_ge(ln_lo, i + 1)
                sp.dma_start(split_dram[i * P:(i + 1) * P, :], wrow[:, i % 2, :]).then_inc(split_out[i % 2], 16)

            for i in range(TB):
                store_split(i)
            for r in range(2 * KC, len(CHUNKS)):
                load_chunk(r)
            for i in range(TB, NT):
                store_split(i)

            def expert_of(t):
                return sp.value_load(EL[0:1, bass.ds(t, 1)], min_val=0, max_val=E - 1)

            def load_up(e):
                for w, lo in ((ew1, 0), (ew2, INTER)):
                    sp.dma_start(W12F[:, :, lo:lo + INTER],
                                 w[bass.ds(e, 1), :, :].rearrange("o (k p) n -> p (o k) n", p=P)).then_inc(w12_in, 16)

            def load_down(e):
                sp.dma_start(W3F[:, :, :],
                             ew3[bass.ds(e, 1), :, :].rearrange("o (c p) n -> p (o c) n", p=P)).then_inc(w3_in, 16)

            sp.wait_ge(zero_rdy, 1)
            sp.dma_start(slots_dram[MINT * P:, :].rearrange("(a p) d -> p a d", p=P),
                         XGT[1].rearrange("p h k t -> p (h k t)").bitcast(F32).unsqueeze(1)
                         .to_broadcast([P, MAXT - MINT, D])).then_inc(zero_out, 16)
            sp.wait_ge(el_rdy, 1)
            sp.wait_ge(su_done, 2 * SC)
            load_up(expert_of(0))
            sp.wait_ge(split_out[0], 16 * NT // 2)
            sp.wait_ge(split_out[1], 16 * NT // 2)
            load_down(expert_of(0))
            sp.wait_ge(w12_lo, 4)
            load_up(expert_of(1))
            sp.wait_ge(zero_out, 16)

            for s in y_out:
                sp.sem_inc(s, 16)
            sp.wait_ge(lc_rdy, 1)
            n = tile_count(sp)

            def step(a, j):
                loads = [loads_before(sp, a + k) for k in range(3)]
                e_up, e_down = expert_of(a + 2), expert_of(a + 1)
                with sp.If(loads[2] > loads[1]):
                    sp.wait_ge(w12_lo, 4 * loads[1])
                    load_up(e_up)
                with sp.If(loads[1] > loads[0]):
                    sp.wait_ge(w3_lo, 2 * loads[0])
                    load_down(e_down)
                if not (isinstance(a, int) and a == 0):
                    sp.wait_ge(y_rdy, a)
                    sp.dma_start(slots_dram[bass.ds((a - 1) * P, P), :], rows[:, 1 - j, :]).then_inc(y_out[1 - j], 16)

            step(0, 0)
            step(1, 1)
            with sp.Fori(1, MINT // 2) as it:
                step(2 * it, 0)
                step(2 * it + 1, 1)
            with sp.Fori(MINT // 2, STEPS // 2) as it:
                with sp.If(2 * it <= n):
                    step(2 * it, 0)
                with sp.If(2 * it + 1 <= n):
                    step(2 * it + 1, 1)

            for i in range(NT):
                sp.wait_ge(fin_rdy, i + 1)
                sp.dma_start(out_t[i], X[:, i, :]).then_inc(out_done, 16)
            sp.wait_ge(out_done, 16 * NT)

        @block.gpsimd
        def _(pool):
            nc.gpsimd.memset(idf[:, :], 0.0).then_inc(consts, 1)
            nc.gpsimd.memset(idh[:, :], 0.0).then_inc(consts, 1)
            nc.gpsimd.memset(tri[:, :], 1.0).then_inc(consts, 1)
            nc.gpsimd.memset(onesb[:, :], 1.0).then_inc(consts, 1)
            nc.gpsimd.memset(onesh[:, :], 1.0).then_inc(consts, 1)
            nc.gpsimd.iota(iota[:, :], pattern=[[1, P]], base=0, channel_multiplier=0,
                           allow_small_or_imprecise_dtypes=True).then_inc(consts, 1)
            nc.gpsimd.iota(pcol[:, :], pattern=[[P, 8]], base=0, channel_multiplier=1,
                           allow_small_or_imprecise_dtypes=True).then_inc(consts, 1)
            nc.gpsimd.iota(desc[:, :], pattern=[[-1, E]], base=E, channel_multiplier=0,
                           allow_small_or_imprecise_dtypes=True).then_inc(consts, 1)
            nc.gpsimd.memset(TI[:, :], 0).then_inc(consts, 1)
            nc.gpsimd.memset(mhalf[:, :], -0.5).then_inc(consts, 1)
            pool.wait_ge(consts, 10)
            for m in (idf, idh):
                nc.gpsimd.affine_select(out=m[:, :], in_=m[:, :], compare_op=ALU.not_equal, fill=1.0, base=0,
                                        pattern=[[-1, P]], channel_multiplier=1).then_inc(ident_rdy, 1)
            nc.gpsimd.affine_select(out=tri[:, :], in_=tri[:, :], compare_op=ALU.is_gt, fill=0.0, base=0,
                                    pattern=[[1, P]], channel_multiplier=-1).then_inc(ident_rdy, 1)

            powers = [0]

            def rstd(lo, n, tiles):
                pool.wait_ge(mv_rdy, tiles)
                nc.gpsimd.tensor_scalar(lnV[:, lo:lo + n], mv[:, lo:lo + n, 1], EPS, 1.0, ALU.add, ALU.mult)\
                    .then_inc(var_eps, 1)
                powers[0] += 1
                pool.wait_ge(var_eps, powers[0])
                nc.gpsimd.tensor_tensor(lnR[:, lo:lo + n], lnV[:, lo:lo + n], mhalf[:, 0:n], ALU.pow)\
                    .then_inc(rstd_rdy, 1)

            for b in range(B):
                rstd(b * TB, TB, (TB, 3 * TB)[b])
                for k in range(KC):
                    n = b * KC + k
                    pool.wait_ge(c_rnd, n + 1)
                    if b and k == 0:
                        pool.wait_ge(at_done, TB)
                    nc.gpsimd.tensor_scalar(Q2[:, k, :], ring[:, RING_AT["ctx", b, k] % 4, :],
                                            -(ROUND + HALF), 1.0, ALU.add, ALU.mult).then_inc(q2_rdy, 1)
                if b == 0:
                    rstd(0, 2, TB + 2)
                    rstd(2, 2, TB + 4)
                else:
                    rstd(TB, TB, 4 * TB)

            def gather(t, j):
                pool.wait_ge(tok_rdy, t + 1)
                pool.sem_inc(gathers, 1)
                pool.indirect_dma_start(out=XG[j].rearrange("p h n -> p (h n)"), out_offset=None,
                                        in_=split_dram[:, :],
                                        in_offset=bass.IndirectOffsetOnAxis(tok1[:, j:j + 1], 0)).then_inc(tok_in[j], 16)

            pool.wait_ge(at_done, NT)
            nc.gpsimd.memset(XGT[1].rearrange("p h k t -> p (h k t)").bitcast(F32), 0.0).then_inc(zero_rdy, 1)
            pool.wait_ge(split_out[0], 16 * NT // 2)
            pool.wait_ge(split_out[1], 16 * NT // 2)
            gather(0, 0)
            gather(1, 1)

            def step(a, j):
                gather(a + 2, j)

            pool.wait_ge(lc_rdy, 1)
            n = tile_count(pool)
            step(0, 0)
            step(1, 1)
            with pool.Fori(1, MINT // 2) as it:
                step(2 * it, 0)
                step(2 * it + 1, 1)
            with pool.Fori(MINT // 2, STEPS // 2) as it:
                with pool.If(2 * it <= n):
                    step(2 * it, 0)
                with pool.If(2 * it + 1 <= n):
                    step(2 * it + 1, 1)
            pool.wait_ge(tok_in[0], 16 * ((n >> 1) + 2))
            pool.sem_inc(gathers, 1)
            pool.wait_ge(tok_in[1], 16 * (((n + 1) >> 1) + 1))
            pool.sem_inc(gathers, 1)

            pool.wait_ge(y_out[0], 16 * (((n + 1) >> 1) + 1))
            pool.sem_inc(gathers, 1)
            pool.wait_ge(y_out[1], 16 * ((n >> 1) + 1))
            pool.sem_inc(gathers, 1)
            for i in range(NT):
                for c in range(2):
                    r = 2 * (i % 2) + c
                    if i >= 2:
                        pool.wait_ge(fin_half if c == 0 else fin_rdy, i - 1)
                    pool.indirect_dma_start(out=ring[:, r, :], out_offset=None, in_=slots_dram[:, :],
                                            in_offset=bass.IndirectOffsetOnAxis(PI[:, c * NT + i:c * NT + i + 1], 0)).then_inc(slot_in[r], 16)

        def yout_before(a, j):
            return 8 * a if j == 0 else 8 * a + 8

        @block.scalar
        def _(act):
            act.wait_ge(small_in, 96)
            nc.scalar.activation(cf[:, 0:2], sc6[:, 4:6], ACT.Tanh).then_inc(tanh_rdy, 1)

            def relu_x(i):
                act.wait_ge(coef1, i // TB + 1)
                if i >= 2:
                    act.wait_ge(q1_T, 2 * (i - 1))
                if i in (TB, TB + 1):
                    act.wait_ge(ln_lo, i - 1)
                nc.scalar.activation(rows[:, i % 2, :], X[:, i, :], ACT.Relu, bias=lnB[:, i:i + 1],
                                     scale=lnA[:, i:i + 1]).then_inc(y_relu, 1)

            def evac_q1(i):
                for h in range(2):
                    act.wait_ge(q1_T, 2 * i + h + 1)
                    nc.scalar.activation(Q1T[:, i % TB, h * 4:h * 4 + 4, :].rearrange("p k t -> p (k t)"),
                                         PS[:, 2 + h, :], ACT.Identity, bias=cf[:, 10:11]).then_inc(q1_rdy, 1)

            def relu_ctx(b, k):
                r = RING_AT["ctx", b, k]
                arrived(act, r)
                nc.scalar.activation(ring[:, r % 4, :], ring[:, r % 4, :], ACT.Relu, bias=sc6[:, 3:4],
                                     scale=cf[:, 2:3]).then_inc(c_relu, 1)

            def hi_chunk(kind, k):
                r = RING_AT[kind, 0, k]
                arrived(act, r)
                if kind == "sw":
                    act.wait_ge(sw1_in[r % 4], 16 * (k // 4 + 1))
                dst = SW[:, 0, k, :] if kind == "sw" else SW3[:, 0, k, :]
                nc.scalar.activation(dst, ring[:, r % 4, :], ACT.Copy, scale=WS).then_inc(sw_hi, 1)

            def ln_hi_row(i):
                act.wait_ge(ln_xs, i + 1)
                if i >= 2:
                    act.wait_ge(split_out[i % 2], 16 * (i // 2))
                nc.scalar.activation(wrow[:, i % 2, 0:D], rows[:, i % 2, :], ACT.Copy).then_inc(ln_hi, 1)

            def tk_lo_evac(i):
                act.wait_ge(tk_T, 2 * i + 2)
                nc.scalar.activation(XT[:, 1, :, i * P:(i + 1) * P], bank16(3), ACT.Copy).then_inc(tk_lo, 1)

            def su_act(u):
                act.wait_ge(su_done, u + 1)
                if u >= 2:
                    act.wait_ge(su_lo, u - 1)
                nc.scalar.activation(SA[:, u % 2, :], PS[:, 4 + 2 * (u % 2), :], ACT.Silu,
                                     bias=sbT[:, 0, u % SC:u % SC + 1], scale=1.0 / UPS).then_inc(su_silu, 1)
                act.wait_ge(su_hf, u + 1)
                if u == SC:
                    act.wait_ge(sd_done, TB)
                nc.scalar.activation(HT[:, 0, u % SC, :], SA[:, u % 2, :], ACT.Copy, scale=HS / UPS).then_inc(su_hi, 1)

            def small_work():
                act.wait_ge(bias_in, 16 * 13)
                nc.scalar.activation(BS[:, 0:SI], areaH[0:64, 0:SI], ACT.Copy, scale=UPS / SELV).then_inc(bs_hi, 1)
                nc.scalar.activation(BS[:, SI:], areaH[0:64, SI:SI + D], ACT.Copy, scale=DNS / SELV).then_inc(bs_hi, 1)
                nc.scalar.activation(RW[:, :, 0, :], RW32[:, :, :], ACT.Copy, scale=WS).then_inc(rw_hi, 1)

            act.wait_ge(tanh_rdy, 2)
            for i in range(TB):
                relu_x(i)
                relu_ctx(0, i)
                evac_q1(i)
            for k in range(TB, KC):
                relu_ctx(0, k)
            small_work()
            for k in range(KC):
                hi_chunk("sw", k)
            for i in range(TB):
                ln_hi_row(i)
                if i:
                    tk_lo_evac(i - 1)
            tk_lo_evac(TB - 1)
            act.wait_ge(bs_lo, 2)
            relu_x(TB)
            relu_x(TB + 1)
            for c in range(SC):
                relu_ctx(1, 2 * c)
                relu_ctx(1, 2 * c + 1)
                su_act(c)
                if c == 1:
                    for i in range(TB, NT):
                        evac_q1(i)
                        if i + 2 < NT:
                            relu_x(i + 2)
            for c in range(SC):
                hi_chunk("sw3", c)
            for i in range(TB, NT):
                ln_hi_row(i)
                if i > TB:
                    tk_lo_evac(i - 1)
            tk_lo_evac(NT - 1)
            act.wait_ge(lg_sub, 1)
            nc.scalar.activation(t1[:, :, :], lg[:, :, :], ACT.Exp).then_inc(lg_exp, 1)
            for c in range(SC):
                su_act(SC + c)

            def split_up(loads, j):
                act.wait_ge(w12_in, 32 * loads)
                for q in range(4):
                    nc.scalar.activation(W12S[j][:, 0, 2 * q:2 * q + 2, :], W12F[:, 2 * q:2 * q + 2, :], ACT.Copy,
                                         scale=WS).then_inc(w12_hi, 1)

            def select(t, j):
                nc.scalar.activation(SEL[:, j, :], SELQ[:, bass.ds(t, 1)].to_broadcast([64, P]), ACT.Copy)\
                    .then_inc(sel_rdy, 1)

            def tokens_low(t, j):
                act.wait_ge(xg_T, 2 * t + 2)
                nc.scalar.activation(XGT[j][:, 1, :, :], bank16(3), ACT.Copy).then_inc(xg_lo, 1)

            def tokens_of(t, j):
                nc.scalar.activation(tok1[:, j:j + 1], TI[:, bass.ds(t, 1)], ACT.Copy).then_inc(tok_rdy, 1)

            act.sem_inc(w12_hi, 4)
            act.sem_inc(w3_hi, 2)
            act.wait_ge(ti_rdy, 1)
            tokens_of(0, 0)
            tokens_of(1, 1)
            split_up(1, 0)
            act.wait_ge(el_rdy, 1)
            select(0, 0)
            tokens_low(0, 0)

            def split_down(loads, j):
                act.wait_ge(w3_in, 16 * loads)
                for q in range(HC):
                    nc.scalar.activation(W3S[j][:, 0, q, :], W3F[:, q, :], ACT.Copy, scale=WS).then_inc(w3_hi, 1)

            act.wait_ge(lc_rdy, 1)
            n = tile_count(act)

            def step(a, j):
                first = isinstance(a, int) and a == 0
                loads, loads_next = loads_before(act, a), loads_before(act, a + 1)
                loads_last = 0 if first else loads_before(act, a - 1)
                act.wait_ge(xg_T, 2 * a + 2)
                tokens_of(a + 2, j)
                if first:
                    act.wait_ge(zero_out, 16)
                tokens_low(a + 1, 1 - j)
                if first:
                    split_up(2, 1)
                else:
                    with act.If(loads_next > loads):
                        split_up(loads_next, 1 - j)
                act.wait_ge(up_done, a + 1)
                nc.scalar.activation(HF[j], PS[:, 4 + j, 0:INTER], ACT.Silu, scale=1.0 / UPS).then_inc(h_silu, 1)
                act.wait_ge(h_prod, a + 1)
                nc.scalar.activation(HSP[j][:, 0, :], HF[j], ACT.Copy, scale=HS / UPS).then_inc(h_hi, 1)
                if first:
                    split_down(1, 0)
                else:
                    with act.If(loads > loads_last):
                        split_down(loads, j)
                if not first:
                    act.wait_ge(dn_done, a)
                    if not (isinstance(a, int) and a < 3):
                        act.wait_ge(y_out[1 - j], yout_before(a, j))
                    nc.scalar.activation(rows[:, 1 - j, :].rearrange("p (h n) -> p h n", h=2), PS[:, 0:2, :],
                                         ACT.Copy, scale=1.0 / DNS).then_inc(y_rdy, 1)
                select(a + 1, 1 - j)

            step(0, 0)
            step(1, 1)
            with act.Fori(1, MINT // 2) as it:
                step(2 * it, 0)
                step(2 * it + 1, 1)
            with act.Fori(MINT // 2, STEPS // 2) as it:
                with act.If(2 * it <= n):
                    step(2 * it, 0)
                with act.If(2 * it + 1 <= n):
                    step(2 * it + 1, 1)

        @block.vector
        def _(dve):
            chain = [0]

            def link(ins):
                chain[0] += 1
                ins.then_inc(v_chain, 1)
                dve.wait_ge(v_chain, chain[0])

            v = nc.vector
            dve.wait_ge(small_in, 96)
            link(v.reciprocal(cf[:, 2:3], sc6[:, 2:3]))
            v.memset(cf[:, 10:11], -(ROUND + HALF)).then_inc(tanh_rdy, 1)
            link(v.reciprocal(cf[:, 3:4], sc6[:, 0:1]))
            link(v.tensor_scalar(cf[:, 8:9], sc6[:, 1:2], -1.0, HALF, ALU.mult, ALU.add))
            link(v.tensor_scalar(cf[:, 9:10], sc6[:, 3:4], -1.0, HALF, ALU.mult, ALU.add))
            dve.wait_ge(tanh_rdy, 2)
            link(v.tensor_scalar(cf[:, 4:5], cf[:, 0:1], sc6[:, 0:1], sc6[:, 2:3], ALU.mult, ALU.mult))
            link(v.tensor_scalar(cf[:, 5:6], cf[:, 4:5], cf[:, 8:9], None, ALU.mult))
            link(v.tensor_scalar(cf[:, 7:8], cf[:, 4:5], cf[:, 9:10], None, ALU.mult))
            link(v.tensor_scalar(cf[:, 6:7], cf[:, 5:6], cf[:, 9:10], float(D), ALU.mult, ALU.mult))
            link(v.tensor_scalar(cf[:, 11:12], cf[:, 1:2], 1.0 / DNS, None, ALU.mult))
            link(v.memset(areaH[0:64, 0:SI + D], 0.0))
            v.memset(SEL[:, 2, :], 0.0).then_inc(bs_zero, 1)

            norms = [0]

            def bn(i):
                for h in range(2):
                    ins = v.bn_stats(stats[:, i, 6 * h:6 * h + 6], X[:, i, h * 512:(h + 1) * 512])
                link(ins)
                v.bn_aggr(mv[:, i, :], stats[:, i, :]).then_inc(mv_rdy, 1)

            def coefs(lo, n, scale_ap, scale, off_ap, done=None):
                sl = slice(lo, lo + n)
                norms[0] += 1
                dve.wait_ge(rstd_rdy, norms[0])
                link(v.tensor_scalar(lnA[:, sl], lnR[:, sl], scale_ap if scale_ap is not None else scale, None, ALU.mult))
                link(v.scalar_tensor_tensor(lnB[:, sl], mv[:, sl, 0], -1.0, lnA[:, sl], ALU.mult, ALU.mult))
                if off_ap is not None:
                    v.tensor_scalar(lnB[:, sl], lnB[:, sl], off_ap, None, ALU.add).then_inc(done, 1)

            def ln1(b):
                for i in range(b * TB, b * TB + TB):
                    dve.wait_ge(x_in[i], 16)
                    bn(i)
                coefs(b * TB, TB, cf[:, 3:4], None, sc6[:, 1:2], coef1)

            def round_x(i):
                dve.wait_ge(y_relu, i + 1)
                v.tensor_scalar(rows[:, i % 2, :], rows[:, i % 2, :], QMAX, ROUND, ALU.min, ALU.add).then_inc(y_rnd, 1)

            def round_ctx(b, k):
                r = RING_AT["ctx", b, k]
                dve.wait_ge(c_relu, b * KC + k + 1)
                v.tensor_scalar(ring[:, r % 4, :], ring[:, r % 4, :], QMAX, ROUND, ALU.min, ALU.add).then_inc(c_rnd, 1)

            def lo_chunk(kind, k):
                r = RING_AT[kind, 0, k]
                dve.wait_ge(sw_hi, (k if kind == "sw" else KC + k) + 1)
                W = SW if kind == "sw" else SW3
                v.scalar_tensor_tensor(W[:, 1, k, :], ring[:, r % 4, :], WS, W[:, 0, k, :], ALU.mult,
                                       ALU.subtract).then_inc(sw_lo, 1)

            def column_terms(b):
                dve.wait_ge(r1_done, b + 1)
                link(v.tensor_scalar(r1[:, :], PS[:, 2, 0:TB], cf[:, 7:8], None, ALU.mult))
                dve.wait_ge(col_done, b + 1)
                v.tensor_scalar(CT.rearrange("p (h n) -> p h n", h=2), PS[:, 6:8, :], cf[:, 5:6], cf[:, 6:7],
                                ALU.mult, ALU.add).then_inc(col_read, 1)
                dve.wait_ge(col_read, b + 1)

            def attend(i):
                v.scalar_tensor_tensor(X[:, i, :], CT, r1[:, i % TB:i % TB + 1], X[:, i, :], ALU.add, ALU.add)\
                    .then_inc(v_chain, 1)
                chain[0] += 1
                dve.wait_ge(at_done, i + 1)
                dve.wait_ge(v_chain, chain[0])
                pb = 4 * (i % 2)
                v.scalar_tensor_tensor(X[:, i, :].rearrange("p (h n) -> p h n", h=2), PS[:, pb:pb + 2, :], cf[:, 4:5],
                                       X[:, i, :].rearrange("p (h n) -> p h n", h=2), ALU.mult, ALU.add)\
                    .then_inc(at_read, 1)
                dve.wait_ge(at_read, i + 1)
                bn(i)

            def ln2_xs(i):
                v.tensor_scalar(rows[:, i % 2, :], X[:, i, :], lnA[:, i:i + 1], lnB[:, i:i + 1], ALU.mult,
                                ALU.add).then_inc(ln_xs, 1)

            def ln2_lo(i):
                dve.wait_ge(ln_hi, i + 1)
                v.tensor_tensor(wrow[:, i % 2, D:2 * D], rows[:, i % 2, :], wrow[:, i % 2, 0:D], ALU.subtract)\
                    .then_inc(ln_lo, 1)

            def tk_hi_evac(i):
                dve.wait_ge(tk_T, 2 * i + 1)
                v.tensor_copy(XT[:, 0, :, i * P:(i + 1) * P], bank16(2)).then_inc(tk_hi, 1)

            def ln2(b):
                for q in range(2):
                    lo = b * TB + 2 * q
                    attend(lo)
                    attend(lo + 1)
                    coefs(lo, 2, None, XS, None)
                    for i in (lo, lo + 1):
                        if i >= 2:
                            dve.wait_ge(ln_hi, i - 1)
                        if i % TB < 2:
                            dve.wait_ge(q1_T, 2 * TB * (b + 1))
                        ln2_xs(i)
                    for i in (lo, lo + 1):
                        ln2_lo(i)
                        if i > b * TB:
                            tk_hi_evac(i - 1)
                tk_hi_evac(b * TB + TB - 1)

            def su_dve(u):
                dve.wait_ge(su_silu, u + 1)
                v.scalar_tensor_tensor(SA[:, u % 2, :], PS[:, 5 + 2 * (u % 2), :], sbT[:, 1, u % SC:u % SC + 1],
                                       SA[:, u % 2, :], ALU.add, ALU.mult).then_inc(su_hf, 1)
                dve.wait_ge(su_hi, u + 1)
                v.scalar_tensor_tensor(HT[:, 1, u % SC, :], SA[:, u % 2, :], HS / UPS, HT[:, 0, u % SC, :], ALU.mult,
                                       ALU.subtract).then_inc(su_lo, 1)

            def sd_evac(i):
                dve.wait_ge(sd_done, i + 1)
                pb = 2 * (i % 2)
                Xi = X[:, i, :].rearrange("p (h n) -> p h n", h=2)
                v.scalar_tensor_tensor(Xi, PS[:, pb:pb + 2, :], cf[:, 11:12], Xi, ALU.mult, ALU.add)\
                    .then_inc(sd_read, 1)

            def small_work():
                dve.wait_ge(bs_hi, 2)
                v.scalar_tensor_tensor(BS[32:64, 0:SI], areaH[32:64, 0:SI], UPS / SELV, BS[32:64, 0:SI], ALU.mult,
                                       ALU.subtract).then_inc(bs_lo, 1)
                v.scalar_tensor_tensor(BS[32:64, SI:], areaH[32:64, SI:SI + D], DNS / SELV, BS[32:64, SI:], ALU.mult,
                                       ALU.subtract).then_inc(bs_lo, 1)
                dve.wait_ge(rw_hi, 1)
                v.scalar_tensor_tensor(RW[:, :, 1, :], RW32[:, :, :], WS, RW[:, :, 0, :], ALU.mult, ALU.subtract)\
                    .then_inc(rw_lo, 1)
                link(v.tensor_scalar(sbT[:, 1, :], sbT[:, 1, :], UPS, None, ALU.mult))
                link(v.tensor_scalar(lnR[0:64, 0:1], pcol[0:64, 0:1], float(E), None, ALU.is_equal))
                link(v.tensor_scalar(lnR[0:64, 1:2], pcol[0:64, 0:1], float(32 + E), None, ALU.is_equal))
                link(v.tensor_tensor(lnR[0:64, 0:1], lnR[0:64, 0:1], lnR[0:64, 1:2], ALU.add))
                v.tensor_scalar(SEL[:, 2, :], onesh[0:64, :], lnR[0:64, 0:1], SELV, ALU.mult, ALU.mult)\
                    .then_inc(bs_lo, 1)

            def bc(ap, n):
                return ap.unsqueeze(2).to_broadcast([P, NT, n])

            def over_tiles(ap, n):
                return ap.unsqueeze(1).to_broadcast([P, NT, n])

            def top1(onehot, val, tmp, n):
                link(v.tensor_reduce(m8, val, AX, ALU.max))
                link(v.tensor_tensor(tmp, val, bc(m8, n), ALU.is_equal))
                link(v.tensor_tensor(tmp, tmp, over_tiles(desc[:, E - n:E], n), ALU.mult))
                link(v.tensor_reduce(m8, tmp, AX, ALU.max))
                link(v.tensor_tensor(onehot, over_tiles(desc[:, E - n:E], n), bc(m8, n), ALU.is_equal))

            def route():
                dve.wait_ge(lg_done, 1)
                dve.wait_ge(bias_in, 16 * 13)
                pl = PS[:, 7, 0:2 * P].rearrange("p (t h e) -> p t h e", t=NT, h=2)
                link(v.tensor_copy(lg, pl[:, :, 0, :]))
                v.tensor_tensor(lg, lg, pl[:, :, 1, :], ALU.add).then_inc(lg_read, 1)
                dve.wait_ge(lg_read, 1)
                link(v.scalar_tensor_tensor(lg, lg, 1.0 / UPS, over_tiles(rb[:, 0, :], E), ALU.mult, ALU.add))
                link(v.tensor_reduce(m8, lg, AX, ALU.max))
                v.tensor_tensor(lg, lg, bc(m8, E), ALU.subtract).then_inc(lg_sub, 1)
                dve.wait_ge(lg_exp, 1)
                link(v.tensor_reduce(m8, t1, AX, ALU.add))
                link(v.reciprocal(m8, m8))
                link(v.tensor_tensor(sco, t1, bc(m8, E), ALU.mult))
                link(v.tensor_tensor(sco, sco, over_tiles(rb[:, 1, :], E), ALU.add))
                link(v.tensor_reduce(gm.rearrange("p t g -> p (t g)"),
                                     sco.rearrange("p t (g e) -> p (t g) e", g=GROUPS), AX, ALU.max))
                top1(go[0], gm, gt, GROUPS)
                link(v.scalar_tensor_tensor(gm, go[0], -BIG, gm, ALU.mult, ALU.add))
                top1(go[1], gm, gt, GROUPS)
                link(v.tensor_tensor(go[0], go[0], go[1], ALU.add))
                keep = go[0].rearrange("p t g -> p (t g)").unsqueeze(2).to_broadcast([P, NT * GROUPS, E // GROUPS])
                G4 = "p t (g e) -> p (t g) e"
                link(v.tensor_tensor(t2.rearrange(G4, g=GROUPS), sco.rearrange(G4, g=GROUPS), keep, ALU.mult))
                link(v.tensor_scalar(go[1], go[0], 1.0, BIG, ALU.subtract, ALU.mult))
                drop = go[1].rearrange("p t g -> p (t g)").unsqueeze(2).to_broadcast([P, NT * GROUPS, E // GROUPS])
                link(v.tensor_tensor(t2.rearrange(G4, g=GROUPS), t2.rearrange(G4, g=GROUPS), drop, ALU.add))
                top1(oh[0], t2, t1, E)
                link(v.scalar_tensor_tensor(t2, oh[0], -2.0 * BIG, t2, ALU.mult, ALU.add))
                top1(oh[1], t2, t1, E)
                for c in range(2):
                    link(v.tensor_tensor(t1, sco, oh[c], ALU.mult))
                    link(v.tensor_reduce(m8, t1, AX, ALU.add))
                    link(v.tensor_scalar(CV[:, c, :], m8, cf[:, 1:2], None, ALU.mult))
                v.tensor_tensor(Mh, oh[0], oh[1], ALU.add).then_inc(m_rdy, 1)

            def place():
                dve.wait_ge(rank_done, 1)
                cnt = PS[:, 7, 0:P].rearrange(TE, t=NT)
                rank = PS[:, 7, P:2 * P].rearrange(TE, t=NT)
                link(v.memset(run[:, 0, :], 0.0))
                for t in range(NT):
                    link(v.tensor_tensor(run[:, t + 1, :], run[:, t, :], cnt[:, t, :], ALU.add))
                v.tensor_tensor(lg, rank, run[:, 0:NT, :], ALU.add).then_inc(rank_read, 1)
                n8 = big[:, 0:P].rearrange("p (e t) -> p e t", e=E)
                link(v.tensor_scalar(m8, iota[:, 0:NT], float(P), None, ALU.mult))
                link(v.tensor_tensor(n8, run[:, NT, :].unsqueeze(2).to_broadcast([P, E, NT]),
                                     m8.unsqueeze(1).to_broadcast([P, E, NT]), ALU.is_gt))
                link(v.tensor_reduce(ntl, n8, AX, ALU.add))
                link(v.memset(sA, 0.0))
                link(v.memset(sB, 0.0))
                link(v.tensor_copy(sA[:, 8:], ntl))
                src, dst = sA, sB
                for s in (1, 2, 4, 8):
                    link(v.tensor_tensor(dst[:, 8:], src[:, 8:], src[:, 8 - s:8 + E - s], ALU.add))
                    src, dst = dst, src
                tend = src[:, 8:]
                link(v.tensor_tensor(base, tend, ntl, ALU.subtract))
                link(v.tensor_scalar(base, base, float(P), None, ALU.mult))
                ec = ECM[:, 0:32 * E].rearrange("p (a e) -> p a e", e=E)
                ef = stats[:, :, :].rearrange("p a b -> p (a b)")
                link(v.tensor_tensor(ec, iota[:, 0:32].unsqueeze(2).to_broadcast([P, 32, E]),
                                     tend.unsqueeze(1).to_broadcast([P, 32, E]), ALU.is_ge))
                link(v.memset(ef[:, 0:COLS], float(E - 1)))
                link(v.tensor_reduce(ef[:, 0:32], ec, AX, ALU.add))
                link(v.tensor_scalar(ef[:, 0:32], ef[:, 0:32], float(E - 1), None, ALU.min))
                link(v.tensor_copy(EL[:, :], ef[:, 0:COLS]))
                link(v.tensor_scalar(ef[32:64, 0:COLS], ef[32:64, 0:COLS], 32.0, None, ALU.add))
                link(v.tensor_copy(ntiles[:, :], tend[:, E - 1:E]))
                v.tensor_scalar(SELQ[:, :], ef[0:64, 0:COLS], pcol[0:64, 0:1], SELV, ALU.is_equal, ALU.mult)\
                    .then_inc(el_rdy, 1)
                dve.wait_ge(rank_read, 1)
                link(v.tensor_tensor(lg, lg, base.unsqueeze(1).to_broadcast([P, NT, E]), ALU.add))
                for c in range(2):
                    link(v.tensor_tensor(t1, lg, oh[c], ALU.mult))
                    link(v.tensor_reduce(pos[:, c, :], t1, AX, ALU.add))
                link(v.tensor_copy(PI[:, :], pos.rearrange("p j t -> p (j t)")))
                link(v.tensor_scalar(ef[:, 40:73], iota[:, 0:33], float(P), None, ALU.mult))
                G = GE.rearrange("p j t a -> p (j t) a")
                pf = pos.rearrange("p j t -> p (j t)")
                link(v.tensor_tensor(G, pf.unsqueeze(2).to_broadcast([P, 2 * NT, 33]),
                                     ef[:, 40:73].unsqueeze(1).to_broadcast([P, 2 * NT, 33]), ALU.is_ge))
                af = aa.rearrange("p j t -> p (j t)")
                bf = bb.rearrange("p j t -> p (j t)")
                link(v.tensor_reduce(af, G, AX, ALU.add))
                link(v.tensor_scalar(af, af, 1.0, -float(P), ALU.subtract, ALU.mult))
                link(v.tensor_tensor(bf, pf, af, ALU.add))
                A = OA.rearrange("p j t a -> p (j t) a")
                link(v.tensor_tensor(A, G[:, :, 0:32], G[:, :, 1:33], ALU.subtract))
                tk = pcol[:, 0:NT].unsqueeze(2).to_broadcast([P, NT, 32])
                for c in range(2):
                    link(v.tensor_tensor(OA[:, c, :, :], OA[:, c, :, :], tk, ALU.mult))
                v.tensor_tensor(OB.rearrange("p j t s -> p (j t) s"), bf.unsqueeze(2).to_broadcast([P, 2 * NT, P]),
                                iota[:, :].unsqueeze(1).to_broadcast([P, 2 * NT, P]), ALU.is_equal).then_inc(slot_rdy, 1)

            def count_loads():
                pad = 32
                sums = [big[:, 0:pad + COLS], big[:, 128:128 + pad + COLS]]
                expert, load = big[:, 256:256 + COLS], big[:, 320:320 + COLS]
                nt = big[:, 384:385]
                link(v.memset(big[:, 0:256], 0.0))
                link(v.tensor_copy(expert, EL[:, :]))
                link(v.tensor_copy(nt, ntiles[:, :]))
                link(v.tensor_tensor(load[:, 2:], expert[:, 2:], expert[:, 0:COLS - 2], ALU.not_equal))
                link(v.memset(load[:, 0:2], 1.0))
                link(v.scalar_tensor_tensor(sums[0][:, pad:], iota[:, 0:COLS], nt, load, ALU.is_lt, ALU.mult))
                for q, sh in enumerate((1, 2, 4, 8, 16, 32)):
                    src, dst = sums[q % 2], sums[1 - q % 2]
                    link(v.tensor_tensor(dst[:, pad:], src[:, pad:], src[:, pad - sh:pad + COLS - sh], ALU.add))
                v.tensor_copy(LC[:, :], sums[0][:, pad:]).then_inc(lc_rdy, 1)

            dve.wait_ge(consts, 10)
            ln1(0)
            for i in range(TB):
                round_x(i)
                round_ctx(0, i)
            for k in range(TB, KC):
                round_ctx(0, k)
            small_work()
            for k in range(KC):
                lo_chunk("sw", k)
            column_terms(0)
            ln2(0)
            ln1(1)
            round_x(TB)
            round_x(TB + 1)
            for c in range(SC):
                round_ctx(1, 2 * c)
                round_ctx(1, 2 * c + 1)
                su_dve(c)
                if c == 1:
                    round_x(TB + 2)
                    round_x(TB + 3)
            for c in range(SC):
                lo_chunk("sw3", c)
            column_terms(1)
            for i in range(TB, NT):
                attend(i)
            coefs(TB, TB, None, XS, None)
            dve.wait_ge(q1_T, 2 * NT)

            def ln2_row(i):
                dve.wait_ge(ln_hi, i - 1)
                ln2_xs(i)
                ln2_lo(i)

            ln2_row(TB)
            ln2_row(TB + 1)
            for i in range(TB):
                sd_evac(i)
            for i in range(TB + 2, NT):
                tk_hi_evac(i - 2)
                ln2_row(i)
            tk_hi_evac(NT - 2)
            tk_hi_evac(NT - 1)
            route()
            for c in range(SC):
                su_dve(SC + c)
            place()
            sd_evac(TB)
            sd_evac(TB + 1)
            dve.wait_ge(ti_done, 1)
            v.tensor_copy(TI[:, 0:32], PS[:, 7, 0:32]).then_inc(ti_rdy, 1)
            count_loads()
            sd_evac(TB + 2)
            sd_evac(TB + 3)

            def split_up(loads, j):
                for q in range(4):
                    dve.wait_ge(w12_hi, 4 * loads + q + 1)
                    ks = slice(2 * q, 2 * q + 2)
                    v.scalar_tensor_tensor(W12S[j][:, 1, ks, :], W12F[:, ks, :], WS, W12S[j][:, 0, ks, :], ALU.mult,
                                           ALU.subtract).then_inc(w12_lo, 1)

            def tokens_high(t, j):
                dve.wait_ge(xg_T, 2 * t + 1)
                v.tensor_copy(XGT[j][:, 0, :, :], bank16(2)).then_inc(xg_hi, 1)

            split_up(1, 0)
            tokens_high(0, 0)

            def split_down(loads, j):
                for q in range(HC):
                    dve.wait_ge(w3_hi, 2 * loads + q + 1)
                    v.scalar_tensor_tensor(W3S[j][:, 1, q, :], W3F[:, q, :], WS, W3S[j][:, 0, q, :], ALU.mult,
                                           ALU.subtract).then_inc(w3_lo, 1)

            dve.wait_ge(lc_rdy, 1)
            n = tile_count(dve)

            def step(a, j):
                first = isinstance(a, int) and a == 0
                loads, loads_next = loads_before(dve, a), loads_before(dve, a + 1)
                loads_last = 0 if first else loads_before(dve, a - 1)
                if first:
                    dve.wait_ge(zero_out, 16)
                tokens_high(a + 1, 1 - j)
                if not first:
                    dve.wait_ge(hT_done, a)
                    v.tensor_copy(HTS[1 - j].rearrange("p h c t -> p (h c t)"), PS[:, 6, 0:256].bitcast(F16))\
                        .then_inc(hT_rdy, 1)
                if first:
                    split_up(2, 1)
                else:
                    with dve.If(loads_next > loads):
                        split_up(loads_next, 1 - j)
                dve.wait_ge(h_silu, a + 1)
                v.tensor_tensor(HF[j], PS[:, 4 + j, INTER:2 * INTER], HF[j], ALU.mult).then_inc(h_prod, 1)
                dve.wait_ge(h_hi, a + 1)
                v.scalar_tensor_tensor(HSP[j][:, 1, :], HF[j], HS / UPS, HSP[j][:, 0, :], ALU.mult,
                                       ALU.subtract).then_inc(h_lo, 1)
                if first:
                    split_down(1, 0)
                else:
                    with dve.If(loads > loads_last):
                        split_down(loads, j)

            step(0, 0)
            step(1, 1)
            with dve.Fori(1, MINT // 2) as it:
                step(2 * it, 0)
                step(2 * it + 1, 1)
            with dve.Fori(MINT // 2, STEPS // 2) as it:
                with dve.If(2 * it <= n):
                    step(2 * it, 0)
                with dve.If(2 * it + 1 <= n):
                    step(2 * it + 1, 1)

            for i in range(NT):
                r = 2 * (i % 2)
                dve.wait_ge(slot_in[r], 16 * (i // 2 + 1))
                v.scalar_tensor_tensor(X[:, i, :], ring[:, r, :], CV[:, 0, i:i + 1], X[:, i, :], ALU.mult, ALU.add)\
                    .then_inc(fin_half, 1)
                dve.wait_ge(slot_in[r + 1], 16 * (i // 2 + 1))
                dve.wait_ge(fin_half, i + 1)
                v.scalar_tensor_tensor(X[:, i, :], ring[:, r + 1, :], CV[:, 1, i:i + 1], X[:, i, :], ALU.mult, ALU.add)\
                    .then_inc(fin_rdy, 1)

        @block.tensor
        def _(pe):
            mm = nc.tensor.matmul
            pe.wait_ge(ident_rdy, 3)

            def transpose_q1(i):
                pe.wait_ge(y_rnd, i + 1)
                for h in range(2):
                    if i:
                        pe.wait_ge(q1_rdy, 2 * i - 1 + h)
                    for k in range(4):
                        last = nc.tensor.transpose(PS[:, 2 + h, k * P:(k + 1) * P],
                                                   rows[:, i % 2, (4 * h + k) * P:(4 * h + k + 1) * P], idf[:, :])
                    last.then_inc(q1_T, 1)

            def attention(b):
                pe.wait_ge(q1_rdy, 2 * TB * (b + 1))
                if b:
                    pe.wait_ge(tk_hi, TB)
                for j in range(TB):
                    for k in range(KC):
                        last = mm(PS[:, 2, j:j + 1], Q1T[:, j, k, :], onesb[:, 0:1], start=(k == 0), stop=(k == KC - 1))
                last.then_inc(r1_done, 1)
                pe.wait_ge(q2_rdy, KC * (b + 1))
                if b:
                    pe.wait_ge(su_hf, SC)
                for h in range(2):
                    for k in range(KC):
                        last = mm(PS[:, 6 + h, :], onesb[:, :], Q2[:, k, h * 512:(h + 1) * 512], start=(k == 0),
                                  stop=(k == KC - 1))
                last.then_inc(col_done, 1)
                for j in range(TB):
                    i = b * TB + j
                    if i >= 2:
                        pe.wait_ge(at_read, i - 1)
                    for h in range(2):
                        for k in range(KC):
                            last = mm(PS[:, 4 * (i % 2) + h, :], Q1T[:, j, k, :], Q2[:, k, h * 512:(h + 1) * 512],
                                      start=(k == 0), stop=(k == KC - 1))
                    last.then_inc(at_done, 1)

            def transpose_tokens(i):
                pe.wait_ge(ln_hi, i + 1)
                if i:
                    pe.wait_ge(tk_hi, i)
                if i == 0:
                    pe.wait_ge(q1_rdy, 2 * TB)
                    pe.wait_ge(col_read, 1)
                if i == TB:
                    pe.wait_ge(sd_read, TB)
                for k in range(KC):
                    last = nc.tensor.transpose(bank16(2)[:, k, :], wrow[:, i % 2, k * P:(k + 1) * P], idh[:, :])
                last.then_inc(tk_T, 1)
                pe.wait_ge(ln_lo, i + 1)
                if i:
                    pe.wait_ge(tk_lo, i)
                for k in range(KC):
                    last = nc.tensor.transpose(bank16(3)[:, k, :], wrow[:, i % 2, D + k * P:D + (k + 1) * P], idh[:, :])
                last.then_inc(tk_T, 1)

            def shared_up(half, turn):
                tk = slice(half * S, (half + 1) * S)
                for j in range(2):
                    if not (isinstance(turn, int) and turn == 0):
                        pe.wait_ge(su_hf, half * SC + 2 * turn + j - 1)
                    for w in range(2):
                        for k in range(KC):
                            for n, (wp, xp) in enumerate(((0, 0), (0, 1), (1, 0))):
                                last = mm(PS[:, 4 + 2 * j + w, :],
                                          SW[:, wp, k, bass.ds(2 * P * turn + w * SI + j * P, P)],
                                          XT[:, xp, k, tk], start=(k == 0 and n == 0), stop=(k == KC - 1 and n == 2))
                    last.then_inc(su_done, 1)

            def shared_down(i, t):
                for h in range(2):
                    hs = slice(h * 512, (h + 1) * 512)
                    for c in range(SC):
                        for n, (hp, wp) in enumerate(((0, 0), (1, 0), (0, 1))):
                            mm(PS[:, 2 * t + h, :], HT[:, hp, c, bass.ds(i * P, P)], SW3[:, wp, c, hs],
                               start=(c == 0 and n == 0), stop=False)
                    last = mm(PS[:, 2 * t + h, :], SEL[:, 2, :], BS[:, SI + h * 512:SI + (h + 1) * 512], start=False,
                              stop=True)
                last.then_inc(sd_done, 1)

            def router():
                pe.wait_ge(rw_lo, 1)
                pe.wait_ge(at_read, NT)
                for i in range(NT):
                    o = PS[:, 7, i * 2 * E:(i + 1) * 2 * E]
                    for k in range(KC):
                        mm(o, XT[:, 0, k, i * P:(i + 1) * P], RW[:, k, :, :].rearrange("p h e -> p (h e)"),
                           start=(k == 0), stop=False)
                        last = mm(o[:, 0:E], XT[:, 1, k, i * P:(i + 1) * P], RW[:, k, 0, :], start=False,
                                  stop=(k == KC - 1))
                last.then_inc(lg_done, 1)

            for i in range(TB):
                transpose_q1(i)
            attention(0)
            for i in range(TB):
                transpose_tokens(i)
            pe.wait_ge(tk_hi, TB)
            pe.wait_ge(tk_lo, TB)
            pe.wait_ge(sw_lo, KC)
            pe.wait_ge(at_read, TB)
            shared_up(0, 0)
            for i in range(TB, NT):
                transpose_q1(i)
            shared_up(0, 1)
            attention(1)
            pe.wait_ge(su_lo, SC)
            pe.wait_ge(sw_lo, KC + SC)
            pe.wait_ge(bs_lo, 3)
            pe.wait_ge(at_read, NT)
            pe.wait_ge(q1_rdy, 2 * NT)
            for i in range(TB):
                if i >= 2:
                    pe.wait_ge(sd_read, i - 1)
                shared_down(i, i % 2)
            for i in range(TB, NT):
                transpose_tokens(i)
            pe.wait_ge(tk_hi, NT)
            pe.wait_ge(tk_lo, NT)
            router()
            pe.wait_ge(lg_read, 1)
            for turn in range(SC // 2):
                shared_up(1, turn)
            pe.wait_ge(m_rdy, 1)
            pe.wait_ge(su_hf, 2 * SC)
            Mf = Mh.rearrange("p t e -> p (t e)")
            mm(PS[:, 7, 0:P], onesh[:, :], Mf, start=True, stop=True)
            mm(PS[:, 7, P:2 * P], tri[:, :], Mf, start=True, stop=True).then_inc(rank_done, 1)
            pe.wait_ge(su_lo, 2 * SC)
            shared_down(0, 0)
            shared_down(1, 1)
            pe.wait_ge(slot_rdy, 1)
            for n in range(2 * NT):
                c, t = n // NT, n % NT
                last = mm(PS[:, 7, 0:32], OB[:, c, t, :], OA[:, c, t, :], start=(n == 0), stop=(n == 2 * NT - 1))
            last.then_inc(ti_done, 1)
            for j in range(2):
                pe.wait_ge(sd_read, TB + 1 + j)
                shared_down(2 + j, j)
            pe.wait_ge(sd_read, NT)

            def transpose_gathered(t, par, count):
                pe.wait_ge(tok_in[par], count)
                for h in range(2):
                    if not (isinstance(t, int) and t == 0):
                        pe.wait_ge(xg_hi if h == 0 else xg_lo, t)
                    for k in range(KC):
                        last = nc.tensor.transpose(bank16(2 + h)[:, k, :], XG[par][:, h, k * P:(k + 1) * P], idh[:, :])
                    last.then_inc(xg_T, 1)

            transpose_gathered(0, 0, 16)
            pe.wait_ge(lc_rdy, 1)
            n = tile_count(pe)

            def step(a, j):
                known = isinstance(a, int)
                first = known and a == 0
                loads = loads_before(pe, a)
                loads_last = 0 if first else loads_before(pe, a - 1)
                transpose_gathered(a + 1, 1 - j, 8 * a + (16 if j == 0 else 24))
                if not first:
                    pe.wait_ge(h_hi, a)
                    pe.wait_ge(h_lo, a)
                    if not (known and a < 2):
                        pe.wait_ge(hT_rdy, a - 1)
                    ht = PS[:, 6, 0:256].bitcast(F16).rearrange("p (n t) -> p n t", n=2 * HC)
                    for n in range(2 * HC):
                        last = nc.tensor.transpose(ht[:, n, :], HSP[1 - j][:, n // HC, (n % HC) * P:(n % HC + 1) * P],
                                                   idh[:, :])
                    last.then_inc(hT_done, 1)
                pe.wait_ge(xg_hi, a + 1)
                pe.wait_ge(xg_lo, a + 1)
                pe.wait_ge(w12_lo, 4 * loads)
                pe.wait_ge(sel_rdy, a + 1)
                if not (known and a < 2):
                    pe.wait_ge(h_prod, a - 1)
                for k in range(KC):
                    for n, (xp, wp) in enumerate(((0, 0), (0, 1), (1, 0))):
                        mm(PS[:, 4 + j, :], XGT[j][:, xp, k, :], W12S[j][:, wp, k, :], start=(k == 0 and n == 0),
                           stop=False)
                mm(PS[:, 4 + j, :], SEL[:, j, :], BS[:, 0:SI], start=False, stop=True).then_inc(up_done, 1)
                if not first:
                    pe.wait_ge(hT_rdy, a)
                    pe.wait_ge(w3_lo, 2 * loads_last)
                    if not (known and a < 2):
                        pe.wait_ge(y_rdy, a - 1)
                    for h in range(2):
                        hs = slice(h * 512, (h + 1) * 512)
                        for c in range(HC):
                            for n, (hp, wp) in enumerate(((0, 0), (1, 0), (0, 1))):
                                mm(PS[:, h, :], HTS[1 - j][:, hp, c, :], W3S[1 - j][:, wp, c, hs],
                                   start=(c == 0 and n == 0), stop=False)
                        last = mm(PS[:, h, :], SEL[:, 1 - j, :], BS[:, SI + h * 512:SI + (h + 1) * 512], start=False,
                                  stop=True)
                    last.then_inc(dn_done, 1)

            step(0, 0)
            step(1, 1)
            with pe.Fori(1, MINT // 2) as it:
                step(2 * it, 0)
                step(2 * it + 1, 1)
            with pe.Fori(MINT // 2, STEPS // 2) as it:
                with pe.If(2 * it <= n):
                    step(2 * it, 0)
                with pe.If(2 * it + 1 <= n):
                    step(2 * it + 1, 1)


_INS = ["x", "ctx_4096", "g_xattn", "g_ffn", "L0_xattn_x1_scale", "L0_xattn_x1_zp", "L0_xattn_x2_scale",
        "L0_xattn_x2_zp", "L0_ffn_router_w", "L0_ffn_router_b", "L0_ffn_router_bias", "L0_ffn_ew1", "L0_ffn_eb1",
        "L0_ffn_ew2", "L0_ffn_eb2", "L0_ffn_ew3", "L0_ffn_eb3", "L0_ffn_sw1", "L0_ffn_sb1", "L0_ffn_sw2",
        "L0_ffn_sb2", "L0_ffn_sw3", "L0_ffn_sb3"]
_OUTS = [((2, 512, 1024), "float32")]


def kernel(**inputs):
    import numpy as _np
    import concourse.bacc as _bacc
    from concourse import mybir as _mybir
    from concourse.bass_utils import run_bass_kernel_spmd as _run

    nc = _bacc.Bacc("TRN2", target_bir_lowering=False, num_devices=1)
    arrays, args = {}, []
    for name in _INS:
        a = _np.ascontiguousarray(inputs[name])
        arrays[f"in_{name}_dram"] = a
        args.append(nc.dram_tensor(f"in_{name}_dram", a.shape, _mybir.dt.from_np(a.dtype), kind="ExternalInput").ap())
    for i, (shape, dtype) in enumerate(_OUTS):
        dt = _mybir.dt.from_np(_np.dtype(dtype))
        args.append(nc.dram_tensor(f"out_{i}_dram", shape, dt, kind="ExternalOutput").ap())
    build(nc, *args)
    r = _run(nc, [arrays], core_ids=[0])
    got = tuple(r.results[0][f"out_{i}_dram"] for i in range(len(_OUTS)))
    return got[0]
```

```python
import concourse.bass as bass
from concourse import mybir
from contextlib import ExitStack

F32, F16, BF16, I32 = mybir.dt.float32, mybir.dt.float16, mybir.dt.bfloat16, mybir.dt.int32
ALU = mybir.AluOpType
ACT = mybir.ActivationFunctionType
AX = mybir.AxisListType.X

P = 128
B, S, D = 2, 512, 1024
KC = D // P
NT = B * S // P
TB = NT // B
E, INTER = 16, 256
GROUPS = 4
SI = 2 * INTER
SC = SI // P
HC = INTER // P
TOPK = 2
MAXT = E + (TOPK * NT * P - E) // P
MINT = TOPK * NT
STEPS = MAXT + 1
COLS = STEPS + 4

QMAX = 255.0
HALF = 128.0
ROUND = 12582912.0
XS = 16.0
WS = 16.0
HS = 0.25
UPS = XS * WS
DNS = HS * WS
GS = 16.0
SELV = 4.0
EPS = 1e-5
BIG = 1e30


def build(nc, x, ctx_in, g_xattn, g_ffn, x1_scale, x1_zp, x2_scale, x2_zp, router_w, router_b, router_bias,
          ew1, eb1, ew2, eb2, ew3, eb3, sw1, sb1, sw2, sb2, sw3, sb3, out):
    x_t = x.rearrange("b (t p) d -> (b t) p d", p=P)
    out_t = out.rearrange("b (t p) d -> (b t) p d", p=P)
    split_dram = nc.dram_tensor("split_dram", [NT * P, 2 * D], F16, kind="Internal").ap()
    T = NT * P
    sum_dram = nc.dram_tensor("sum_dram", [T + P, D], F32, kind="Internal").ap()

    es = ExitStack()
    with es:
        def sb(name, shape, dt):
            return es.enter_context(nc.sbuf_tensor(name, shape, dt))

        sems = {}

        def sem(name):
            sems[name] = es.enter_context(nc.semaphore(name))
            return sems[name]

        X = sb("X", [P, NT, D], F32)
        areaT = sb("areaT", [P, 8192], F32)
        area2 = sb("area2", [P, 4096], F32)
        ring = sb("ring", [P, 4, D], F32)
        rows = sb("rows", [P, 2, D], F32)
        areaQ = sb("areaQ", [P, 3072], F32)
        wrow = sb("wrow", [P, 2, 2 * D], F16)
        areaW = sb("areaW", [P, 8192], F32)
        SW3 = sb("SW3", [P, 2, SC, D], F16)
        areaH = sb("areaH", [P, 2048], F32)
        SA = sb("SA", [P, 2, S], F32)

        def view(area, lo, n, dt, pat=None, **kw):
            v = area[:, lo:lo + n]
            if dt is not F32:
                v = v.bitcast(dt)
            return v.rearrange(pat, **kw) if pat else v

        XT = view(areaT, 0, 8192, F16, "p (h k t) -> p h k t", h=2, k=KC)
        Q2 = view(area2, 0, 4096, BF16, "p (k n) -> p k n", k=KC)
        Q1T = view(areaQ, 0, 2048, BF16, "p (j k t) -> p j k t", j=TB, k=KC)
        CT = view(areaQ, 2048, 1024, F32)
        SW = view(areaW, 0, 8192, F16, "p (h k n) -> p h k n", h=2, k=KC)
        HT = view(areaH, 0, 2048, F16, "p (h c t) -> p h c t", h=2, c=SC)
        bias32 = areaH[0:64, 0:1536]
        W12F = view(areaT, 0, 4096, F32, "p (k n) -> p k n", k=KC)
        W3S = [view(areaT, 4096 + 2048 * i, 2048, F16, "p (h c n) -> p h c n", h=2, c=HC) for i in range(2)]
        W3F = wrow[:, :, :].rearrange("p a n -> p (a n)").bitcast(F32).rearrange("p (c n) -> p c n", c=HC)
        W12S = [view(areaW, 4096 * i, 4096, F16, "p (h k n) -> p h k n", h=2, k=KC) for i in range(2)]
        XG = [view(area2, 1024 * i, 1024, F16, "p (h n) -> p h n", h=2) for i in range(2)]
        XGT = [view(area2, 2048 + 1024 * i, 1024, F16, "p (h k t) -> p h k t", h=2, k=KC) for i in range(2)]
        HF = [view(areaH, 256 * i, 256, F32) for i in range(2)]
        HSP = [view(areaH, 512 + 256 * i, 256, F16, "p (h n) -> p h n", h=2) for i in range(2)]
        HTS = [view(areaH, 1024 + 256 * i, 256, F16, "p (h c t) -> p h c t", h=2, c=HC) for i in range(2)]

        BS = sb("BS", [64, SI + D], F16)
        SEL = sb("SEL", [64, 3, P], F16)
        SELQ = sb("SELQ", [64, COLS], F32)
        RW32 = sb("RW32", [P, KC, E], F32)
        RW = sb("RW", [P, KC, 2, E], F16)
        rb = sb("rb", [P, 2, E], F32)
        sbT = sb("sbT", [P, 2, SC], F32)
        sc6 = sb("sc6", [P, 8], F32)
        cf = sb("cf", [P, 16], F32)
        stats = sb("stats", [P, NT, 12], F32)
        mv = sb("mv", [P, NT, 2], F32)
        lnA = sb("lnA", [P, NT], F32)
        lnB = sb("lnB", [P, NT], F32)
        lnR = sb("lnR", [P, NT], F32)
        lnV = sb("lnV", [P, NT], F32)
        mhalf = sb("mhalf", [P, TB], F32)
        r1 = sb("r1", [P, TB], F32)
        idf = sb("idf", [P, P], F32)
        idh = sb("idh", [P, P], F16)
        onesb = sb("onesb", [P, P], BF16)
        onesh = sb("onesh", [P, P], F16)
        tri = sb("tri", [P, P], F16)
        iota = sb("iota", [P, P], F32)
        pcol = sb("pcol", [P, 8], F32)
        desc = sb("desc", [P, E], F32)
        TI = sb("TI", [P, COLS], I32)
        tok1 = sb("tok1", [P, 2], I32)
        RI = sb("RI", [P, MAXT + 1], I32)
        row1 = sb("row1", [P, 2], I32)
        GT = sb("GT", [P, MAXT + 1], F32)
        EL = sb("EL", [P, COLS], I32)
        LC = sb("LC", [P, COLS], I32)
        ntiles = sb("ntiles", [P, 1], I32)
        CV = sb("CV", [P, 2, NT], F32)
        CVS = sb("CVS", [P, 2, 2 * NT], F16)

        PS = es.enter_context(nc.psum_tensor("PS", [P, 8, 512], F32))

        def bank16(b):
            return PS[:, b, :].bitcast(F16).rearrange("p (k t) -> p k t", k=KC)

        ofs = [0]

        def small(n, pat=None, dt=F32, **kw):
            lo = ofs[0]
            ofs[0] += n
            assert ofs[0] <= 3072
            return view(areaQ, lo, n, dt, pat, **kw)

        TE = "p (t e) -> p t e"
        lg = small(P, TE, t=NT)
        sco = small(P, TE, t=NT)
        t1 = small(P, TE, t=NT)
        t2 = small(P, TE, t=NT)
        oh = [small(P, TE, t=NT) for _ in range(2)]
        gm = small(NT * GROUPS, "p (t g) -> p t g", t=NT)
        gt = small(NT * GROUPS, "p (t g) -> p t g", t=NT)
        go = [small(NT * GROUPS, "p (t g) -> p t g", t=NT) for _ in range(2)]
        m8 = small(NT)
        Mh = small(P // 2, TE, dt=F16, t=NT)
        run = small((NT + 1) * E, "p (t e) -> p t e", t=NT + 1)
        sA = small(8 + E)
        sB = small(8 + E)
        ntl = small(E)
        base = small(E)
        pos = small(2 * NT, "p (j t) -> p j t", j=2)
        aa = small(2 * NT, "p (j t) -> p j t", j=2)
        bb = small(2 * NT, "p (j t) -> p j t", j=2)
        big = small(1024)
        GE = big[:, 0:2 * NT * 33].rearrange("p (j t a) -> p j t a", j=2, a=33)
        OB = view(areaQ, ofs[0] - 1024, 1024, F16, "p (j t s) -> p j t s", j=2, t=NT)
        OA = SA[:, :, :].rearrange("p a n -> p (a n)")[:, 0:768].bitcast(F16).rearrange("p (n w a) -> p n w a", w=3, a=32)
        ECM = SA[:, 1, :]

        AT_BANK = (0, 4, 2, 0)
        SD_BANK = (4, 2, 4, 2)

        x_in = [sem(f"x_in{i}") for i in range(NT)]
        ring_in = [sem(f"ring_in{i}") for i in range(4)]
        sw1_in = [sem(f"sw1_in{i}") for i in range(4)]
        small_in, bias_in = sem("small_in"), sem("bias_in")
        consts, ident_rdy, v_chain = sem("consts"), sem("ident_rdy"), sem("v_chain")
        coef1, tanh_rdy, mv_rdy, rstd_rdy = sem("coef1"), sem("tanh_rdy"), sem("mv_rdy"), sem("rstd_rdy")
        var_eps = sem("var_eps")
        y_relu, y_rnd, q1_T = sem("y_relu"), sem("y_rnd"), sem("q1_T")
        q1_rdy = [sem("q1_rdy0"), sem("q1_rdy1")]
        r1_rdy, x_r1, x_ct, coef2 = sem("r1_rdy"), sem("x_r1"), sem("x_ct"), sem("coef2")
        sw_scaled, sw_lo2 = sem("sw_scaled"), sem("sw_lo2")
        c_relu, c_rnd, q2_rdy = sem("c_relu"), sem("c_rnd"), sem("q2_rdy")
        sw_hi, sw_lo = sem("sw_hi"), sem("sw_lo")
        r1_done, r1_read, col_done, col_read = sem("r1_done"), sem("r1_read"), sem("col_done"), sem("col_read")
        at_done, at_read = sem("at_done"), sem("at_read")
        ln_xs, ln_hi, ln_lo = sem("ln_xs"), sem("ln_hi"), sem("ln_lo")
        split_out = [sem("split_out0"), sem("split_out1")]
        tk_T, tk_hi, tk_lo = sem("tk_T"), sem("tk_hi"), sem("tk_lo")
        rw_hi, rw_lo, bs_zero, bs_hi, bs_lo = sem("rw_hi"), sem("rw_lo"), sem("bs_zero"), sem("bs_hi"), sem("bs_lo")
        su_done, su_silu, su_hf, su_hi, su_lo = sem("su_done"), sem("su_silu"), sem("su_hf"), sem("su_hi"), sem("su_lo")
        sd_done, sd_read = sem("sd_done"), sem("sd_read")
        lg_done, lg_read, lg_sub, lg_exp = sem("lg_done"), sem("lg_read"), sem("lg_sub"), sem("lg_exp")
        m_rdy, rank_done, rank_read = sem("m_rdy"), sem("rank_done"), sem("rank_read")
        lc_rdy, sum_in, gt_rdy = sem("lc_rdy"), sem("sum_in"), sem("gt_rdy")
        el_rdy, slot_rdy, ti_done, ti_rdy = sem("el_rdy"), sem("slot_rdy"), sem("ti_done"), sem("ti_rdy")
        gathers, tok_rdy, tok_in = sem("gathers"), sem("tok_rdy"), [sem("tok_in0"), sem("tok_in1")]
        w12_in, w3_in = sem("w12_in"), sem("w3_in")
        w12_hi, w12_lo, w3_hi, w3_lo = sem("w12_hi"), sem("w12_lo"), sem("w3_hi"), sem("w3_lo")
        sel_rdy = sem("sel_rdy")
        xg_T, xg_hi, xg_lo = sem("xg_T"), sem("xg_hi"), sem("xg_lo")
        up_done, h_silu, h_prod, h_hi, h_lo = sem("up_done"), sem("h_silu"), sem("h_prod"), sem("h_hi"), sem("h_lo")
        hT_done, hT_rdy, dn_done, y_rdy = sem("hT_done"), sem("hT_rdy"), sem("dn_done"), sem("y_rdy")
        row_rdy, y_out, out_done = sem("row_rdy"), sem("y_out"), sem("out_done")

        block = es.enter_context(nc.Block())

        CHUNKS = ([("ctx", 0, k) for k in range(KC)] + [("sw", 0, k) for k in range(KC)]
                  + [("ctx", 1, k) for k in range(KC)] + [("sw3", 0, c) for c in range(SC)])
        RING_AT = {c: r for r, c in enumerate(CHUNKS)}

        def arrived(eng, r):
            eng.wait_ge(ring_in[r % 4], 16 * (r // 4 + 1))

        def consumed(r):
            kind, b, k = CHUNKS[r]
            if kind == "ctx":
                return q2_rdy, b * KC + k + 1
            if kind == "sw" and k >= KC // 2:
                return sw_lo2, k - KC // 2 + 1
            return sw_lo, (k if kind == "sw" else KC // 2 + k) + 1

        def tile_count(eng):
            return eng.value_load(ntiles[0:1, 0:1], min_val=MINT, max_val=MAXT)

        def loads_before(eng, t):
            return eng.value_load(LC[0:1, bass.ds(t, 1)], min_val=1, max_val=MAXT)

        @block.sync
        def _(sp):
            scalars = (x1_scale, x1_zp, x2_scale, x2_zp, g_xattn, g_ffn)
            for i in range(TB):
                sp.dma_start(X[:, i, :], x_t[i]).then_inc(x_in[i], 16)
                for n in range(2 * i, min(2 * i + 2, len(scalars))):
                    sp.dma_start(sc6[:, n:n + 1], scalars[n].partition_broadcast(P)).then_inc(small_in, 16)

            def load_chunk(r):
                kind, b, k = CHUNKS[r]
                if r >= 4:
                    sp.wait_ge(*consumed(r - 4))
                rs = slice(k * P, (k + 1) * P)
                if kind == "ctx":
                    sp.dma_start(ring[:, r % 4, :], ctx_in[b, rs, :]).then_inc(ring_in[r % 4], 16)
                elif kind == "sw3":
                    sp.dma_start(ring[:, r % 4, :], sw3[rs, :]).then_inc(ring_in[r % 4], 16)
                else:
                    sp.dma_start(ring[:, r % 4, :].rearrange("p (w n) -> p w n", w=2)[:, 0, :], sw1[rs, :])\
                        .then_inc(sw1_in[r % 4], 16)
                    sp.dma_start(ring[:, r % 4, SI:2 * SI], sw2[rs, :]).then_inc(ring_in[r % 4], 16)

            for r in range(4):
                load_chunk(r)
            sp.wait_ge(bs_zero, 2)
            for q in (0, 32):
                sp.dma_start(areaH[q:q + E, 0:INTER], eb1[:, :]).then_inc(bias_in, 16)
                sp.dma_start(areaH[q:q + E, INTER:SI], eb2[:, :]).then_inc(bias_in, 16)
                sp.dma_start(areaH[q:q + E, SI:SI + D], eb3[:, :]).then_inc(bias_in, 16)
                sp.dma_start(areaH[q + E:q + E + 1, SI:SI + D], sb3.rearrange("(a n) -> a n", a=1)).then_inc(bias_in, 16)
            sp.dma_start(rb[:, 0, :], router_b.partition_broadcast(P)).then_inc(bias_in, 16)
            sp.dma_start(rb[:, 1, :], router_bias.partition_broadcast(P)).then_inc(bias_in, 16)
            sp.dma_start(RW32[:, :, :], router_w.rearrange("(k p) e -> p k e", p=P)).then_inc(bias_in, 16)
            with nc.allow_non_contiguous_dma(reason="bias vectors laid along the partitions"):
                sp.dma_start(sbT[:, 0, :], sb1.rearrange("(c p) -> p c", p=P)).then_inc(bias_in, 16)
                sp.dma_start(sbT[:, 1, :], sb2.rearrange("(c p) -> p c", p=P)).then_inc(bias_in, 16)
            for r in range(4, 2 * KC):
                load_chunk(r)
            for i in range(TB, NT):
                sp.dma_start(X[:, i, :], x_t[i]).then_inc(x_in[i], 16)

            def store_split(i):
                sp.wait_ge(ln_hi, i + 1)
                sp.wait_ge(ln_lo, i + 1)
                sp.dma_start(split_dram[i * P:(i + 1) * P, :], wrow[:, i % 2, :]).then_inc(split_out[i % 2], 16)

            r = 2 * KC
            for i in range(TB):
                store_split(i)
                if i % 2:
                    load_chunk(r)
                    load_chunk(r + 1)
                    r += 2
            for r in range(r, len(CHUNKS)):
                load_chunk(r)
            for i in range(TB, NT):
                store_split(i)

            def expert_of(t):
                return sp.value_load(EL[0:1, bass.ds(t, 1)], min_val=0, max_val=E - 1)

            def load_up(e):
                for w, lo in ((ew1, 0), (ew2, INTER)):
                    sp.dma_start(W12F[:, :, lo:lo + INTER],
                                 w[bass.ds(e, 1), :, :].rearrange("o (k p) n -> p (o k) n", p=P)).then_inc(w12_in, 16)

            def load_down(e):
                sp.dma_start(W3F[:, :, :],
                             ew3[bass.ds(e, 1), :, :].rearrange("o (c p) n -> p (o c) n", p=P)).then_inc(w3_in, 16)

            sp.wait_ge(el_rdy, 1)
            sp.wait_ge(su_done, 2 * SC)
            load_up(expert_of(0))
            sp.wait_ge(split_out[0], 16 * NT // 2)
            sp.wait_ge(split_out[1], 16 * NT // 2)
            load_down(expert_of(0))
            sp.wait_ge(w12_lo, 4)
            load_up(expert_of(1))
            for i in range(NT):
                sp.wait_ge(sd_read, i + 1)
                sp.dma_start(sum_dram[i * P:(i + 1) * P, :], X[:, i, :]).then_inc(sum_in, 16)
            sp.dma_start(sum_dram[T:T + P, :], X[:, NT - 1, :]).then_inc(sum_in, 16)
            sp.wait_ge(lc_rdy, 1)
            n = tile_count(sp)

            def step(a, j):
                loads = [loads_before(sp, a + k) for k in range(3)]
                e_up, e_down = expert_of(a + 2), expert_of(a + 1)
                with sp.If(loads[2] > loads[1]):
                    sp.wait_ge(w12_lo, 4 * loads[1])
                    load_up(e_up)
                with sp.If(loads[1] > loads[0]):
                    sp.wait_ge(w3_lo, 2 * loads[0])
                    load_down(e_down)

            step(0, 0)
            step(1, 1)
            with sp.Fori(1, MINT // 2) as it:
                step(2 * it, 0)
                step(2 * it + 1, 1)
            with sp.Fori(MINT // 2, STEPS // 2) as it:
                with sp.If(2 * it <= n):
                    step(2 * it, 0)
                with sp.If(2 * it + 1 <= n):
                    step(2 * it + 1, 1)

            sp.wait_ge(y_out, 16 * n)
            for i in range(2):
                half = slice(i * T // 2, (i + 1) * T // 2)
                sp.dma_start(out.rearrange("b s d -> (b s) d")[half, :], sum_dram[half, :]).then_inc(out_done, 16)
            sp.wait_ge(out_done, 32)

        @block.gpsimd
        def _(pool):
            nc.gpsimd.memset(areaH[0:64, 0:SI + D], 0.0).then_inc(bs_zero, 1)
            nc.gpsimd.memset(SEL[:, 2, :], 0.0).then_inc(bs_zero, 1)
            nc.gpsimd.memset(idf[:, :], 0.0).then_inc(consts, 1)
            nc.gpsimd.memset(idh[:, :], 0.0).then_inc(consts, 1)
            nc.gpsimd.memset(tri[:, :], 1.0).then_inc(consts, 1)
            nc.gpsimd.memset(onesb[:, :], 1.0).then_inc(consts, 1)
            nc.gpsimd.memset(onesh[:, :], 1.0).then_inc(consts, 1)
            nc.gpsimd.iota(iota[:, :], pattern=[[1, P]], base=0, channel_multiplier=0,
                           allow_small_or_imprecise_dtypes=True).then_inc(consts, 1)
            nc.gpsimd.iota(pcol[:, :], pattern=[[P, 8]], base=0, channel_multiplier=1,
                           allow_small_or_imprecise_dtypes=True).then_inc(consts, 1)
            nc.gpsimd.iota(desc[:, :], pattern=[[-1, E]], base=E, channel_multiplier=0,
                           allow_small_or_imprecise_dtypes=True).then_inc(consts, 1)
            nc.gpsimd.memset(TI[:, :], 0).then_inc(consts, 1)
            nc.gpsimd.memset(mhalf[:, :], -0.5).then_inc(consts, 1)
            pool.wait_ge(consts, 10)
            for m in (idf, idh):
                nc.gpsimd.affine_select(out=m[:, :], in_=m[:, :], compare_op=ALU.not_equal, fill=1.0, base=0,
                                        pattern=[[-1, P]], channel_multiplier=1).then_inc(ident_rdy, 1)
            nc.gpsimd.affine_select(out=tri[:, :], in_=tri[:, :], compare_op=ALU.is_gt, fill=0.0, base=0,
                                    pattern=[[1, P]], channel_multiplier=-1).then_inc(ident_rdy, 1)

            powers = [0]

            def rstd(lo, n, tiles):
                pool.wait_ge(mv_rdy, tiles)
                nc.gpsimd.tensor_scalar(lnV[:, lo:lo + n], mv[:, lo:lo + n, 1], EPS, 1.0, ALU.add, ALU.mult)\
                    .then_inc(var_eps, 1)
                powers[0] += 1
                pool.wait_ge(var_eps, powers[0])
                nc.gpsimd.tensor_tensor(lnR[:, lo:lo + n], lnV[:, lo:lo + n], mhalf[:, 0:n], ALU.pow)\
                    .then_inc(rstd_rdy, 1)

            def lo_chunk(k):
                pool.wait_ge(sw_scaled, k - KC // 2 + 1)
                nc.gpsimd.tensor_tensor(SW[:, 1, k, :], ring[:, RING_AT["sw", 0, k] % 4, :], SW[:, 0, k, :],
                                        ALU.subtract).then_inc(sw_lo2, 1)

            for b in range(B):
                rstd(b * TB, TB, (TB, 3 * TB)[b])
                for k in range(KC):
                    n = b * KC + k
                    pool.wait_ge(c_rnd, n + 1)
                    if b and k == 0:
                        pool.wait_ge(at_done, TB)
                    nc.gpsimd.tensor_scalar(Q2[:, k, :], ring[:, RING_AT["ctx", b, k] % 4, :],
                                            -(ROUND + HALF), 1.0, ALU.add, ALU.mult).then_inc(q2_rdy, 1)
                pool.wait_ge(col_read, b + 1)
                for i in range(b * TB + 1, b * TB + TB):
                    pool.wait_ge(x_r1, i + 1)
                    nc.gpsimd.tensor_tensor(X[:, i, :], X[:, i, :], CT, ALU.add).then_inc(x_ct, 1)
                if b == 0:
                    rstd(0, 2, TB + 2)
                    lo_chunk(KC // 2)
                    rstd(2, 2, TB + 4)
                    lo_chunk(KC // 2 + 1)
                    lo_chunk(KC // 2 + 2)
                    lo_chunk(KC // 2 + 3)
                else:
                    rstd(TB, TB, 4 * TB)

            def gather(t, j):
                pool.wait_ge(tok_rdy, t + 1)
                pool.sem_inc(gathers, 1)
                pool.indirect_dma_start(out=XG[j].rearrange("p h n -> p (h n)"), out_offset=None,
                                        in_=split_dram[:, :],
                                        in_offset=bass.IndirectOffsetOnAxis(tok1[:, j:j + 1], 0)).then_inc(tok_in[j], 16)

            pool.wait_ge(at_done, NT)
            pool.wait_ge(split_out[0], 16 * NT // 2)
            pool.wait_ge(split_out[1], 16 * NT // 2)
            gather(0, 0)
            gather(1, 1)

            def scatter(t, j):
                pool.wait_ge(y_rdy, t + 1)
                pool.sem_inc(gathers, 1)
                if not (isinstance(t, int) and t == 0):
                    pool.wait_ge(y_out, 16 * t)
                    pool.sem_inc(gathers, 1)
                pool.indirect_dma_start(out=sum_dram[:, :], out_offset=bass.IndirectOffsetOnAxis(row1[:, j:j + 1], 0),
                                        in_=rows[:, j, :], in_offset=None, compute_op=ALU.add).then_inc(y_out, 16)

            def step(a, j):
                gather(a + 2, j)
                if not (isinstance(a, int) and a == 0):
                    if isinstance(a, int) and a == 1:
                        pool.wait_ge(sum_in, 16 * (NT + 1))
                    scatter(a - 1, 1 - j)

            pool.wait_ge(lc_rdy, 1)
            n = tile_count(pool)
            step(0, 0)
            step(1, 1)
            with pool.Fori(1, MINT // 2) as it:
                step(2 * it, 0)
                step(2 * it + 1, 1)
            with pool.Fori(MINT // 2, STEPS // 2) as it:
                with pool.If(2 * it <= n):
                    step(2 * it, 0)
                with pool.If(2 * it + 1 <= n):
                    step(2 * it + 1, 1)
            pool.wait_ge(tok_in[0], 16 * ((n >> 1) + 2))
            pool.sem_inc(gathers, 1)
            pool.wait_ge(tok_in[1], 16 * (((n + 1) >> 1) + 1))
            pool.sem_inc(gathers, 1)

        @block.scalar
        def _(act):
            act.wait_ge(small_in, 96)
            nc.scalar.activation(cf[:, 0:2], sc6[:, 4:6], ACT.Tanh).then_inc(tanh_rdy, 1)

            def relu_x(i):
                act.wait_ge(coef1, i // TB + 1)
                if i >= 2:
                    act.wait_ge(q1_T, 2 * (i - 1))
                if i in (TB, TB + 1):
                    act.wait_ge(ln_lo, i - 1)
                nc.scalar.activation(rows[:, i % 2, :], X[:, i, :], ACT.Relu, bias=lnB[:, i:i + 1],
                                     scale=lnA[:, i:i + 1]).then_inc(y_relu, 1)

            def evac_q1(i):
                act.wait_ge(q1_T, 2 * i + 1)
                nc.scalar.activation(Q1T[:, i % TB, 0:4, :].rearrange("p k t -> p (k t)"),
                                     PS[:, 2, :], ACT.Identity, bias=cf[:, 10:11]).then_inc(q1_rdy[0], 1)

            def relu_ctx(b, k):
                r = RING_AT["ctx", b, k]
                arrived(act, r)
                nc.scalar.activation(ring[:, r % 4, :], ring[:, r % 4, :], ACT.Relu, bias=sc6[:, 3:4],
                                     scale=cf[:, 2:3]).then_inc(c_relu, 1)

            def hi_chunk(kind, k):
                r = RING_AT[kind, 0, k]
                arrived(act, r)
                if kind == "sw":
                    act.wait_ge(sw1_in[r % 4], 16 * (k // 4 + 1))
                dst = SW[:, 0, k, :] if kind == "sw" else SW3[:, 0, k, :]
                nc.scalar.activation(dst, ring[:, r % 4, :], ACT.Copy, scale=WS).then_inc(sw_hi, 1)
                if kind == "sw" and k >= KC // 2:
                    nc.scalar.activation(ring[:, r % 4, :], ring[:, r % 4, :], ACT.Copy, scale=WS).then_inc(sw_scaled, 1)

            def add_r1(b):
                act.wait_ge(r1_rdy, b + 1)
                for i in range(b * TB, b * TB + TB):
                    nc.scalar.activation(X[:, i, :], X[:, i, :], ACT.Identity, bias=r1[:, i % TB:i % TB + 1])\
                        .then_inc(x_r1, 1)

            def ln_hi_row(i):
                act.wait_ge(coef2, (1, 1, 2, 2)[i] if i < TB else 3)
                if i >= 2:
                    act.wait_ge(ln_lo, i - 1)
                if i % TB < 2:
                    act.wait_ge(q1_T, 2 * TB * (i // TB + 1))
                nc.scalar.activation(rows[:, i % 2, :], X[:, i, :], ACT.Identity, bias=lnB[:, i:i + 1],
                                     scale=lnA[:, i:i + 1]).then_inc(ln_xs, 1)
                act.wait_ge(ln_xs, i + 1)
                if i >= 2:
                    act.wait_ge(split_out[i % 2], 16 * (i // 2))
                nc.scalar.activation(wrow[:, i % 2, 0:D], rows[:, i % 2, :], ACT.Copy).then_inc(ln_hi, 1)

            def tk_lo_evac(i):
                act.wait_ge(tk_T, 2 * i + 2)
                nc.scalar.activation(XT[:, 1, :, i * P:(i + 1) * P], bank16(3), ACT.Copy).then_inc(tk_lo, 1)

            def su_act(u):
                act.wait_ge(su_done, u + 1)
                if u >= 2:
                    act.wait_ge(su_lo, u - 1)
                nc.scalar.activation(SA[:, u % 2, :], PS[:, 4 + 2 * (u % 2), :], ACT.Silu,
                                     bias=sbT[:, 0, u % SC:u % SC + 1], scale=1.0 / UPS).then_inc(su_silu, 1)
                act.wait_ge(su_hf, u + 1)
                if u == SC:
                    act.wait_ge(sd_done, TB)
                nc.scalar.activation(HT[:, 0, u % SC, :], SA[:, u % 2, :], ACT.Copy, scale=HS / UPS).then_inc(su_hi, 1)

            def small_work():
                act.wait_ge(bias_in, 16 * 13)
                nc.scalar.activation(BS[:, 0:SI], areaH[0:64, 0:SI], ACT.Copy, scale=UPS / SELV).then_inc(bs_hi, 1)
                nc.scalar.activation(BS[:, SI:], areaH[0:64, SI:SI + D], ACT.Copy, scale=DNS / SELV).then_inc(bs_hi, 1)
                nc.scalar.activation(RW[:, :, 0, :], RW32[:, :, :], ACT.Copy, scale=WS).then_inc(rw_hi, 1)

            act.wait_ge(tanh_rdy, 2)
            for k in range(3):
                relu_ctx(0, k)
            relu_x(0)
            relu_x(1)
            relu_ctx(0, 3)
            for i in range(TB):
                evac_q1(i)
                if i + 2 < TB:
                    relu_x(i + 2)
                relu_ctx(0, i + 4)
            small_work()
            for k in range(KC // 2):
                hi_chunk("sw", k)
            add_r1(0)
            for k in range(KC // 2, KC):
                hi_chunk("sw", k)
            ln_hi_row(0)
            ln_hi_row(1)
            tk_lo_evac(0)
            tk_lo_evac(1)
            ln_hi_row(2)
            ln_hi_row(3)
            tk_lo_evac(2)
            tk_lo_evac(3)
            act.wait_ge(bs_lo, 2)
            relu_x(TB)
            relu_x(TB + 1)
            for c in range(SC):
                relu_ctx(1, 2 * c)
                relu_ctx(1, 2 * c + 1)
                su_act(c)
                for i in ((TB, TB + 1), (TB + 2,), (TB + 3,), ())[c]:
                    evac_q1(i)
                    if i + 2 < NT:
                        relu_x(i + 2)
            for c in range(SC):
                hi_chunk("sw3", c)
            add_r1(1)
            for i in range(TB, NT):
                ln_hi_row(i)
                if i > TB:
                    tk_lo_evac(i - 1)
            tk_lo_evac(NT - 1)
            act.wait_ge(lg_sub, 1)
            nc.scalar.activation(t1[:, :, :], lg[:, :, :], ACT.Exp).then_inc(lg_exp, 1)
            for c in range(SC):
                su_act(SC + c)

            def split_up(loads, j):
                act.wait_ge(w12_in, 32 * loads)
                for q in range(4):
                    nc.scalar.activation(W12S[j][:, 0, 2 * q:2 * q + 2, :], W12F[:, 2 * q:2 * q + 2, :], ACT.Copy,
                                         scale=WS).then_inc(w12_hi, 1)

            def select(t, j):
                nc.scalar.activation(SEL[:, j, :], SELQ[:, bass.ds(t, 1)].to_broadcast([64, P]), ACT.Copy)\
                    .then_inc(sel_rdy, 1)

            def tokens_low(t, j):
                act.wait_ge(xg_T, 2 * t + 2)
                nc.scalar.activation(XGT[j][:, 1, :, :], bank16(3), ACT.Copy).then_inc(xg_lo, 1)

            def tokens_of(t, j):
                nc.scalar.activation(tok1[:, j:j + 1], TI[:, bass.ds(t, 1)], ACT.Copy).then_inc(tok_rdy, 1)

            act.sem_inc(w12_hi, 4)
            act.sem_inc(w3_hi, 2)
            act.wait_ge(ti_rdy, 1)
            tokens_of(0, 0)
            tokens_of(1, 1)
            split_up(1, 0)
            act.wait_ge(el_rdy, 1)
            select(0, 0)
            tokens_low(0, 0)

            def split_down(loads, j):
                act.wait_ge(w3_in, 16 * loads)
                for q in range(HC):
                    nc.scalar.activation(W3S[j][:, 0, q, :], W3F[:, q, :], ACT.Copy, scale=WS).then_inc(w3_hi, 1)

            act.wait_ge(lc_rdy, 1)
            act.wait_ge(gt_rdy, 1)
            n = tile_count(act)

            def step(a, j):
                first = isinstance(a, int) and a == 0
                loads, loads_next = loads_before(act, a), loads_before(act, a + 1)
                loads_last = 0 if first else loads_before(act, a - 1)
                act.wait_ge(xg_T, 2 * a + 2)
                tokens_of(a + 2, j)
                tokens_low(a + 1, 1 - j)
                if first:
                    split_up(2, 1)
                else:
                    with act.If(loads_next > loads):
                        split_up(loads_next, 1 - j)
                act.wait_ge(up_done, a + 1)
                nc.scalar.activation(HF[j], PS[:, 4 + j, 0:INTER], ACT.Silu, scale=1.0 / UPS).then_inc(h_silu, 1)
                act.wait_ge(h_prod, a + 1)
                nc.scalar.activation(HSP[j][:, 0, :], HF[j], ACT.Copy, scale=HS / UPS).then_inc(h_hi, 1)
                if first:
                    split_down(1, 0)
                else:
                    with act.If(loads > loads_last):
                        split_down(loads, j)
                if not first:
                    if not (isinstance(a, int) and a < 2):
                        act.wait_ge(y_out, 16 * a - 16)
                    nc.scalar.activation(row1[:, 1 - j:2 - j], RI[:, bass.ds(a - 1, 1)], ACT.Copy).then_inc(row_rdy, 1)
                    act.wait_ge(dn_done, a)
                    act.wait_ge(row_rdy, a)
                    nc.scalar.activation(rows[:, 1 - j, :].rearrange("p (h n) -> p h n", h=2), PS[:, 0:2, :],
                                         ACT.Copy, scale=GT[:, bass.ds(a - 1, 1)]).then_inc(y_rdy, 1)
                select(a + 1, 1 - j)

            step(0, 0)
            step(1, 1)
            with act.Fori(1, MINT // 2) as it:
                step(2 * it, 0)
                step(2 * it + 1, 1)
            with act.Fori(MINT // 2, STEPS // 2) as it:
                with act.If(2 * it <= n):
                    step(2 * it, 0)
                with act.If(2 * it + 1 <= n):
                    step(2 * it + 1, 1)

        @block.vector
        def _(dve):
            chain = [0]

            def link(ins):
                chain[0] += 1
                ins.then_inc(v_chain, 1)
                dve.wait_ge(v_chain, chain[0])

            v = nc.vector
            norms = [0]

            def bn(i):
                for h in range(2):
                    ins = v.bn_stats(stats[:, i, 6 * h:6 * h + 6], X[:, i, h * 512:(h + 1) * 512])
                link(ins)
                v.bn_aggr(mv[:, i, :], stats[:, i, :]).then_inc(mv_rdy, 1)

            def coefs(lo, n, scale_ap, scale, off_ap):
                sl = slice(lo, lo + n)
                norms[0] += 1
                dve.wait_ge(rstd_rdy, norms[0])
                link(v.tensor_scalar(lnA[:, sl], lnR[:, sl], scale_ap if scale_ap is not None else scale, None, ALU.mult))
                ins = v.scalar_tensor_tensor(lnB[:, sl], mv[:, sl, 0], -1.0, lnA[:, sl], ALU.mult, ALU.mult)
                if off_ap is None:
                    ins.then_inc(coef2, 1)
                    return
                link(ins)
                v.tensor_scalar(lnB[:, sl], lnB[:, sl], off_ap, None, ALU.add).then_inc(coef1, 1)

            def ln1(b):
                for i in range(b * TB, b * TB + TB):
                    dve.wait_ge(x_in[i], 16)
                    bn(i)
                coefs(b * TB, TB, cf[:, 3:4], None, sc6[:, 1:2])

            def round_x(i):
                dve.wait_ge(y_relu, i + 1)
                v.tensor_scalar(rows[:, i % 2, :], rows[:, i % 2, :], QMAX, ROUND, ALU.min, ALU.add).then_inc(y_rnd, 1)

            def evac_q1(i):
                dve.wait_ge(q1_T, 2 * i + 2)
                v.tensor_scalar(Q1T[:, i % TB, 4:8, :].rearrange("p k t -> p (k t)"), PS[:, 3, :], cf[:, 10:11], None,
                                ALU.add).then_inc(q1_rdy[1], 1)

            def round_ctx(b, k):
                r = RING_AT["ctx", b, k]
                dve.wait_ge(c_relu, b * KC + k + 1)
                v.tensor_scalar(ring[:, r % 4, :], ring[:, r % 4, :], QMAX, ROUND, ALU.min, ALU.add).then_inc(c_rnd, 1)

            def lo_chunk(kind, k):
                r = RING_AT[kind, 0, k]
                dve.wait_ge(sw_hi, (k if kind == "sw" else KC + k) + 1)
                W = SW if kind == "sw" else SW3
                v.scalar_tensor_tensor(W[:, 1, k, :], ring[:, r % 4, :], WS, W[:, 0, k, :], ALU.mult,
                                       ALU.subtract).then_inc(sw_lo, 1)

            def row_terms(b):
                dve.wait_ge(r1_done, b + 1)
                v.tensor_scalar(r1[:, :], PS[:, 2, 0:TB], cf[:, 7:8], None, ALU.mult).then_inc(r1_rdy, 1)

            def column_terms(b):
                dve.wait_ge(col_done, b + 1)
                v.tensor_scalar(CT.rearrange("p (h n) -> p h n", h=2), PS[:, 6:8, :], cf[:, 5:6], cf[:, 6:7],
                                ALU.mult, ALU.add).then_inc(col_read, 1)

            def attend(i):
                if i % TB == 0:
                    dve.wait_ge(x_r1, i + 1)
                    dve.wait_ge(col_read, i // TB + 1)
                    link(v.tensor_tensor(X[:, i, :], X[:, i, :], CT, ALU.add))
                dve.wait_ge(at_done, i + 1)
                if i % TB:
                    dve.wait_ge(x_ct, (TB - 1) * (i // TB) + i % TB)
                pb = AT_BANK[i % TB]
                v.scalar_tensor_tensor(X[:, i, :].rearrange("p (h n) -> p h n", h=2), PS[:, pb:pb + 2, :], cf[:, 4:5],
                                       X[:, i, :].rearrange("p (h n) -> p h n", h=2), ALU.mult, ALU.add)\
                    .then_inc(at_read, 1)
                dve.wait_ge(at_read, i + 1)
                bn(i)

            def ln2_lo(i):
                dve.wait_ge(ln_hi, i + 1)
                v.tensor_tensor(wrow[:, i % 2, D:2 * D], rows[:, i % 2, :], wrow[:, i % 2, 0:D], ALU.subtract)\
                    .then_inc(ln_lo, 1)

            def tk_hi_evac(i):
                dve.wait_ge(tk_T, 2 * i + 1)
                v.tensor_copy(XT[:, 0, :, i * P:(i + 1) * P], bank16(2)).then_inc(tk_hi, 1)

            def ln2():
                attend(0)
                attend(1)
                attend(2)
                coefs(0, 2, None, XS, None)
                attend(3)
                ln2_lo(0)
                ln2_lo(1)
                tk_hi_evac(0)
                tk_hi_evac(1)
                coefs(2, 2, None, XS, None)
                for i in (2, 3):
                    ln2_lo(i)
                    tk_hi_evac(i)

            def su_dve(u):
                dve.wait_ge(su_silu, u + 1)
                v.scalar_tensor_tensor(SA[:, u % 2, :], PS[:, 5 + 2 * (u % 2), :], sbT[:, 1, u % SC:u % SC + 1],
                                       SA[:, u % 2, :], ALU.add, ALU.mult).then_inc(su_hf, 1)
                dve.wait_ge(su_hi, u + 1)
                v.scalar_tensor_tensor(HT[:, 1, u % SC, :], SA[:, u % 2, :], HS / UPS, HT[:, 0, u % SC, :], ALU.mult,
                                       ALU.subtract).then_inc(su_lo, 1)

            def sd_evac(i):
                dve.wait_ge(sd_done, i + 1)
                pb = SD_BANK[i % TB]
                Xi = X[:, i, :].rearrange("p (h n) -> p h n", h=2)
                v.scalar_tensor_tensor(Xi, PS[:, pb:pb + 2, :], cf[:, 11:12], Xi, ALU.mult, ALU.add)\
                    .then_inc(sd_read, 1)

            def small_work():
                dve.wait_ge(bs_hi, 2)
                v.scalar_tensor_tensor(BS[32:64, 0:SI], areaH[32:64, 0:SI], UPS / SELV, BS[32:64, 0:SI], ALU.mult,
                                       ALU.subtract).then_inc(bs_lo, 1)
                v.scalar_tensor_tensor(BS[32:64, SI:], areaH[32:64, SI:SI + D], DNS / SELV, BS[32:64, SI:], ALU.mult,
                                       ALU.subtract).then_inc(bs_lo, 1)
                dve.wait_ge(rw_hi, 1)
                v.scalar_tensor_tensor(RW[:, :, 1, :], RW32[:, :, :], WS, RW[:, :, 0, :], ALU.mult, ALU.subtract)\
                    .then_inc(rw_lo, 1)
                link(v.tensor_scalar(sbT[:, 1, :], sbT[:, 1, :], UPS, None, ALU.mult))
                link(v.tensor_scalar(lnR[0:64, 0:1], pcol[0:64, 0:1], float(E), None, ALU.is_equal))
                link(v.tensor_scalar(lnR[0:64, 1:2], pcol[0:64, 0:1], float(32 + E), None, ALU.is_equal))
                link(v.tensor_tensor(lnR[0:64, 0:1], lnR[0:64, 0:1], lnR[0:64, 1:2], ALU.add))
                v.tensor_scalar(SEL[:, 2, :], onesh[0:64, :], lnR[0:64, 0:1], SELV, ALU.mult, ALU.mult)\
                    .then_inc(bs_lo, 1)

            def bc(ap, n):
                return ap.unsqueeze(2).to_broadcast([P, NT, n])

            def over_tiles(ap, n):
                return ap.unsqueeze(1).to_broadcast([P, NT, n])

            def top1(onehot, val, tmp, n):
                link(v.tensor_reduce(m8, val, AX, ALU.max))
                link(v.tensor_tensor(tmp, val, bc(m8, n), ALU.is_equal))
                link(v.tensor_tensor(tmp, tmp, over_tiles(desc[:, E - n:E], n), ALU.mult))
                link(v.tensor_reduce(m8, tmp, AX, ALU.max))
                link(v.tensor_tensor(onehot, over_tiles(desc[:, E - n:E], n), bc(m8, n), ALU.is_equal))

            def route():
                dve.wait_ge(lg_done, 1)
                dve.wait_ge(bias_in, 16 * 13)
                pl = PS[:, 7, 0:2 * P].rearrange("p (t h e) -> p t h e", t=NT, h=2)
                link(v.tensor_copy(lg, pl[:, :, 0, :]))
                v.tensor_tensor(lg, lg, pl[:, :, 1, :], ALU.add).then_inc(lg_read, 1)
                dve.wait_ge(lg_read, 1)
                link(v.scalar_tensor_tensor(lg, lg, 1.0 / UPS, over_tiles(rb[:, 0, :], E), ALU.mult, ALU.add))
                link(v.tensor_reduce(m8, lg, AX, ALU.max))
                v.tensor_tensor(lg, lg, bc(m8, E), ALU.subtract).then_inc(lg_sub, 1)
                dve.wait_ge(lg_exp, 1)
                link(v.tensor_reduce(m8, t1, AX, ALU.add))
                link(v.reciprocal(m8, m8))
                link(v.tensor_tensor(sco, t1, bc(m8, E), ALU.mult))
                link(v.tensor_tensor(sco, sco, over_tiles(rb[:, 1, :], E), ALU.add))
                link(v.tensor_reduce(gm.rearrange("p t g -> p (t g)"),
                                     sco.rearrange("p t (g e) -> p (t g) e", g=GROUPS), AX, ALU.max))
                top1(go[0], gm, gt, GROUPS)
                link(v.scalar_tensor_tensor(gm, go[0], -BIG, gm, ALU.mult, ALU.add))
                top1(go[1], gm, gt, GROUPS)
                link(v.tensor_tensor(go[0], go[0], go[1], ALU.add))
                keep = go[0].rearrange("p t g -> p (t g)").unsqueeze(2).to_broadcast([P, NT * GROUPS, E // GROUPS])
                G4 = "p t (g e) -> p (t g) e"
                link(v.tensor_tensor(t2.rearrange(G4, g=GROUPS), sco.rearrange(G4, g=GROUPS), keep, ALU.mult))
                link(v.tensor_scalar(go[1], go[0], 1.0, BIG, ALU.subtract, ALU.mult))
                drop = go[1].rearrange("p t g -> p (t g)").unsqueeze(2).to_broadcast([P, NT * GROUPS, E // GROUPS])
                link(v.tensor_tensor(t2.rearrange(G4, g=GROUPS), t2.rearrange(G4, g=GROUPS), drop, ALU.add))
                top1(oh[0], t2, t1, E)
                link(v.scalar_tensor_tensor(t2, oh[0], -2.0 * BIG, t2, ALU.mult, ALU.add))
                top1(oh[1], t2, t1, E)
                for c in range(2):
                    link(v.tensor_tensor(t1, sco, oh[c], ALU.mult))
                    link(v.tensor_reduce(m8, t1, AX, ALU.add))
                    link(v.tensor_scalar(CV[:, c, :], m8, cf[:, 1:2], GS, ALU.mult, ALU.mult))
                CVf = CV.rearrange("p c t -> p (c t)")
                link(v.tensor_copy(CVS[:, 0, :], CVf))
                link(v.tensor_tensor(CVS[:, 1, :], CVf, CVS[:, 0, :], ALU.subtract))
                v.tensor_tensor(Mh, oh[0], oh[1], ALU.add).then_inc(m_rdy, 1)

            def place():
                dve.wait_ge(rank_done, 1)
                cnt = PS[:, 7, 0:P].rearrange(TE, t=NT)
                rank = PS[:, 7, P:2 * P].rearrange(TE, t=NT)
                link(v.memset(run[:, 0, :], 0.0))
                for t in range(NT):
                    link(v.tensor_tensor(run[:, t + 1, :], run[:, t, :], cnt[:, t, :], ALU.add))
                v.tensor_tensor(lg, rank, run[:, 0:NT, :], ALU.add).then_inc(rank_read, 1)
                n8 = big[:, 0:P].rearrange("p (e t) -> p e t", e=E)
                link(v.tensor_scalar(m8, iota[:, 0:NT], float(P), None, ALU.mult))
                link(v.tensor_tensor(n8, run[:, NT, :].unsqueeze(2).to_broadcast([P, E, NT]),
                                     m8.unsqueeze(1).to_broadcast([P, E, NT]), ALU.is_gt))
                link(v.tensor_reduce(ntl, n8, AX, ALU.add))
                link(v.memset(sA, 0.0))
                link(v.memset(sB, 0.0))
                link(v.tensor_copy(sA[:, 8:], ntl))
                src, dst = sA, sB
                for s in (1, 2, 4, 8):
                    link(v.tensor_tensor(dst[:, 8:], src[:, 8:], src[:, 8 - s:8 + E - s], ALU.add))
                    src, dst = dst, src
                tend = src[:, 8:]
                link(v.tensor_tensor(base, tend, ntl, ALU.subtract))
                link(v.tensor_scalar(base, base, float(P), None, ALU.mult))
                ec = ECM[:, 0:32 * E].rearrange("p (a e) -> p a e", e=E)
                ef = stats[:, :, :].rearrange("p a b -> p (a b)")
                link(v.tensor_tensor(ec, iota[:, 0:32].unsqueeze(2).to_broadcast([P, 32, E]),
                                     tend.unsqueeze(1).to_broadcast([P, 32, E]), ALU.is_ge))
                link(v.memset(ef[:, 0:COLS], float(E - 1)))
                link(v.tensor_reduce(ef[:, 0:32], ec, AX, ALU.add))
                link(v.tensor_scalar(ef[:, 0:32], ef[:, 0:32], float(E - 1), None, ALU.min))
                link(v.tensor_copy(EL[:, :], ef[:, 0:COLS]))
                link(v.tensor_scalar(ef[32:64, 0:COLS], ef[32:64, 0:COLS], 32.0, None, ALU.add))
                link(v.tensor_copy(ntiles[:, :], tend[:, E - 1:E]))
                v.tensor_scalar(SELQ[:, :], ef[0:64, 0:COLS], pcol[0:64, 0:1], SELV, ALU.is_equal, ALU.mult)\
                    .then_inc(el_rdy, 1)
                dve.wait_ge(rank_read, 1)
                link(v.tensor_tensor(lg, lg, base.unsqueeze(1).to_broadcast([P, NT, E]), ALU.add))
                for c in range(2):
                    link(v.tensor_tensor(t1, lg, oh[c], ALU.mult))
                    link(v.tensor_reduce(pos[:, c, :], t1, AX, ALU.add))
                link(v.tensor_scalar(ef[:, 40:73], iota[:, 0:33], float(P), None, ALU.mult))
                G = GE.rearrange("p j t a -> p (j t) a")
                pf = pos.rearrange("p j t -> p (j t)")
                link(v.tensor_tensor(G, pf.unsqueeze(2).to_broadcast([P, 2 * NT, 33]),
                                     ef[:, 40:73].unsqueeze(1).to_broadcast([P, 2 * NT, 33]), ALU.is_ge))
                af = aa.rearrange("p j t -> p (j t)")
                bf = bb.rearrange("p j t -> p (j t)")
                link(v.tensor_reduce(af, G, AX, ALU.add))
                link(v.tensor_scalar(af, af, 1.0, -float(P), ALU.subtract, ALU.mult))
                link(v.tensor_tensor(bf, pf, af, ALU.add))
                link(v.tensor_tensor(OA[:, :, 0, :], G[:, :, 0:32], G[:, :, 1:33], ALU.subtract))
                for w in range(2):
                    link(v.tensor_tensor(OA[:, :, 1 + w, :], OA[:, :, 0, :],
                                         CVS[:, w, :].unsqueeze(2).to_broadcast([P, 2 * NT, 32]), ALU.mult))
                tk = pcol[:, 0:NT].unsqueeze(2).to_broadcast([P, NT, 32])
                for c in range(2):
                    o = OA[:, c * NT:(c + 1) * NT, 0, :]
                    link(v.scalar_tensor_tensor(o, tk, -float(T), o, ALU.add, ALU.mult))
                v.tensor_tensor(OB.rearrange("p j t s -> p (j t) s"), bf.unsqueeze(2).to_broadcast([P, 2 * NT, P]),
                                iota[:, :].unsqueeze(1).to_broadcast([P, 2 * NT, P]), ALU.is_equal).then_inc(slot_rdy, 1)

            def count_loads():
                pad = 32
                sums = [big[:, 0:pad + COLS], big[:, 128:128 + pad + COLS]]
                expert, load = big[:, 256:256 + COLS], big[:, 320:320 + COLS]
                nt = big[:, 384:385]
                link(v.memset(big[:, 0:256], 0.0))
                link(v.tensor_copy(expert, EL[:, :]))
                link(v.tensor_copy(nt, ntiles[:, :]))
                link(v.tensor_tensor(load[:, 2:], expert[:, 2:], expert[:, 0:COLS - 2], ALU.not_equal))
                link(v.memset(load[:, 0:2], 1.0))
                link(v.scalar_tensor_tensor(sums[0][:, pad:], iota[:, 0:COLS], nt, load, ALU.is_lt, ALU.mult))
                for q, sh in enumerate((1, 2, 4, 8, 16, 32)):
                    src, dst = sums[q % 2], sums[1 - q % 2]
                    link(v.tensor_tensor(dst[:, pad:], src[:, pad:], src[:, pad - sh:pad + COLS - sh], ALU.add))
                v.tensor_copy(LC[:, :], sums[0][:, pad:]).then_inc(lc_rdy, 1)

            dve.wait_ge(small_in, 96)
            link(v.reciprocal(cf[:, 2:3], sc6[:, 2:3]))
            v.memset(cf[:, 10:11], -(ROUND + HALF)).then_inc(tanh_rdy, 1)
            v.reciprocal(cf[:, 3:4], sc6[:, 0:1]).then_inc(v_chain, 1)
            chain[0] += 1
            dve.wait_ge(consts, 10)
            for i in range(TB):
                dve.wait_ge(x_in[i], 16)
                bn(i)
            link(v.tensor_scalar(cf[:, 8:9], sc6[:, 1:2], -1.0, HALF, ALU.mult, ALU.add))
            link(v.tensor_scalar(cf[:, 9:10], sc6[:, 3:4], -1.0, HALF, ALU.mult, ALU.add))
            dve.wait_ge(tanh_rdy, 2)
            link(v.tensor_scalar(cf[:, 4:5], cf[:, 0:1], sc6[:, 0:1], sc6[:, 2:3], ALU.mult, ALU.mult))
            link(v.tensor_scalar(cf[:, 5:6], cf[:, 4:5], cf[:, 8:9], None, ALU.mult))
            link(v.tensor_scalar(cf[:, 7:8], cf[:, 4:5], cf[:, 9:10], None, ALU.mult))
            link(v.tensor_scalar(cf[:, 6:7], cf[:, 5:6], cf[:, 9:10], float(D), ALU.mult, ALU.mult))
            link(v.tensor_scalar(cf[:, 11:12], cf[:, 1:2], 1.0 / DNS, None, ALU.mult))
            coefs(0, TB, cf[:, 3:4], None, sc6[:, 1:2])
            for k in range(3):
                round_ctx(0, k)
            round_x(0)
            round_x(1)
            round_ctx(0, 3)
            for i in range(TB):
                evac_q1(i)
                if i + 2 < TB:
                    round_x(i + 2)
                round_ctx(0, i + 4)
            small_work()
            row_terms(0)
            for k in range(KC // 2):
                lo_chunk("sw", k)
            column_terms(0)
            ln2()

            ln1(1)
            round_x(TB)
            round_x(TB + 1)
            for c in range(SC):
                round_ctx(1, 2 * c)
                round_ctx(1, 2 * c + 1)
                su_dve(c)
                for i in ((TB, TB + 1), (TB + 2,), (TB + 3,), ())[c]:
                    evac_q1(i)
                    if i + 2 < NT:
                        round_x(i + 2)
            row_terms(1)
            for c in range(SC):
                lo_chunk("sw3", c)
            column_terms(1)
            for i in range(TB, NT):
                attend(i)
            coefs(TB, TB, None, XS, None)
            ln2_lo(TB)
            ln2_lo(TB + 1)
            for i in range(TB):
                sd_evac(i)
            for i in range(TB + 2, NT):
                tk_hi_evac(i - 2)
                ln2_lo(i)
            tk_hi_evac(NT - 2)
            tk_hi_evac(NT - 1)
            route()
            for c in range(SC):
                su_dve(SC + c)
            place()
            sd_evac(TB)
            dve.wait_ge(ti_done, 1)
            v.tensor_scalar(TI[:, 0:32], PS[:, 7, 0:32], -1.0, float(T), ALU.min, ALU.add).then_inc(ti_rdy, 1)
            sd_evac(TB + 1)
            count_loads()
            link(v.tensor_scalar(GT[:, :], PS[:, 7, 32:64], 1.0 / (GS * DNS), None, ALU.mult))
            link(v.scalar_tensor_tensor(GT[:, :], PS[:, 7, 64:96], 1.0 / (GS * DNS), GT[:, :], ALU.mult, ALU.add))
            link(v.tensor_scalar(stats[:, 0:3, :].rearrange("p a b -> p (a b)")[:, 0:32], PS[:, 7, 0:32], 0.0,
                                 pcol[:, 0:1], ALU.is_equal, ALU.mult))
            v.scalar_tensor_tensor(RI[:, :], PS[:, 7, 0:32], float(T),
                                   stats[:, 0:3, :].rearrange("p a b -> p (a b)")[:, 0:32], ALU.add, ALU.add)\
                .then_inc(gt_rdy, 1)
            sd_evac(TB + 2)
            sd_evac(TB + 3)

            def split_up(loads, j):
                for q in range(4):
                    dve.wait_ge(w12_hi, 4 * loads + q + 1)
                    ks = slice(2 * q, 2 * q + 2)
                    v.scalar_tensor_tensor(W12S[j][:, 1, ks, :], W12F[:, ks, :], WS, W12S[j][:, 0, ks, :], ALU.mult,
                                           ALU.subtract).then_inc(w12_lo, 1)

            def tokens_high(t, j):
                dve.wait_ge(xg_T, 2 * t + 1)
                v.tensor_copy(XGT[j][:, 0, :, :], bank16(2)).then_inc(xg_hi, 1)

            split_up(1, 0)
            tokens_high(0, 0)

            def split_down(loads, j):
                for q in range(HC):
                    dve.wait_ge(w3_hi, 2 * loads + q + 1)
                    v.scalar_tensor_tensor(W3S[j][:, 1, q, :], W3F[:, q, :], WS, W3S[j][:, 0, q, :], ALU.mult,
                                           ALU.subtract).then_inc(w3_lo, 1)

            dve.wait_ge(lc_rdy, 1)
            n = tile_count(dve)

            def step(a, j):
                first = isinstance(a, int) and a == 0
                loads, loads_next = loads_before(dve, a), loads_before(dve, a + 1)
                loads_last = 0 if first else loads_before(dve, a - 1)
                tokens_high(a + 1, 1 - j)
                if not first:
                    dve.wait_ge(hT_done, a)
                    v.tensor_copy(HTS[1 - j].rearrange("p h c t -> p (h c t)"), PS[:, 6, 0:256].bitcast(F16))\
                        .then_inc(hT_rdy, 1)
                if first:
                    split_up(2, 1)
                else:
                    with dve.If(loads_next > loads):
                        split_up(loads_next, 1 - j)
                dve.wait_ge(h_silu, a + 1)
                v.tensor_tensor(HF[j], PS[:, 4 + j, INTER:2 * INTER], HF[j], ALU.mult).then_inc(h_prod, 1)
                dve.wait_ge(h_hi, a + 1)
                v.scalar_tensor_tensor(HSP[j][:, 1, :], HF[j], HS / UPS, HSP[j][:, 0, :], ALU.mult,
                                       ALU.subtract).then_inc(h_lo, 1)
                if first:
                    split_down(1, 0)
                else:
                    with dve.If(loads > loads_last):
                        split_down(loads, j)

            step(0, 0)
            step(1, 1)
            with dve.Fori(1, MINT // 2) as it:
                step(2 * it, 0)
                step(2 * it + 1, 1)
            with dve.Fori(MINT // 2, STEPS // 2) as it:
                with dve.If(2 * it <= n):
                    step(2 * it, 0)
                with dve.If(2 * it + 1 <= n):
                    step(2 * it + 1, 1)

        @block.tensor
        def _(pe):
            mm = nc.tensor.matmul
            pe.wait_ge(ident_rdy, 3)

            def transpose_q1(i):
                pe.wait_ge(y_rnd, i + 1)
                for h in range(2):
                    if i:
                        pe.wait_ge(q1_rdy[h], i)
                    for k in range(4):
                        last = nc.tensor.transpose(PS[:, 2 + h, k * P:(k + 1) * P],
                                                   rows[:, i % 2, (4 * h + k) * P:(4 * h + k + 1) * P], idf[:, :])
                    last.then_inc(q1_T, 1)

            def attention(b):
                pe.wait_ge(q1_rdy[0], TB * (b + 1))
                pe.wait_ge(q1_rdy[1], TB * (b + 1))
                if b:
                    pe.wait_ge(tk_hi, TB)
                for j in range(TB):
                    for k in range(KC):
                        last = mm(PS[:, 2, j:j + 1], Q1T[:, j, k, :], onesb[:, 0:1], start=(k == 0), stop=(k == KC - 1))
                last.then_inc(r1_done, 1)
                if b:
                    pe.wait_ge(su_hf, SC)
                lo = b * TB

                def product(i, h, k):
                    return mm(PS[:, AT_BANK[i - lo] + h, :], Q1T[:, i - lo, k, :], Q2[:, k, h * 512:(h + 1) * 512],
                              start=(k == 0), stop=(k == KC - 1))

                for k in range(KC):
                    pe.wait_ge(q2_rdy, KC * b + k + 1)
                    for h in range(2):
                        last = mm(PS[:, 6 + h, :], onesb[:, :], Q2[:, k, h * 512:(h + 1) * 512], start=(k == 0),
                                  stop=(k == KC - 1))
                    if k == KC - 1:
                        last.then_inc(col_done, 1)
                    for i in (lo, lo + 1):
                        last = product(i, 0, k)
                        last = product(i, 1, k)
                        if k == KC - 1:
                            last.then_inc(at_done, 1)
                pe.wait_ge(r1_rdy, b + 1)
                for i in (lo + 2, lo + 3):
                    if i == lo + 3:
                        pe.wait_ge(at_read, lo + 1)
                    for h in range(2):
                        for k in range(KC):
                            last = product(i, h, k)
                    last.then_inc(at_done, 1)

            def transpose_tokens(i):
                pe.wait_ge(ln_hi, i + 1)
                if i:
                    pe.wait_ge(tk_hi, i)
                if i == 0:
                    pe.wait_ge(at_read, TB - 1)
                if i == TB:
                    pe.wait_ge(sd_read, TB)
                for k in range(KC):
                    last = nc.tensor.transpose(bank16(2)[:, k, :], wrow[:, i % 2, k * P:(k + 1) * P], idh[:, :])
                last.then_inc(tk_T, 1)
                pe.wait_ge(ln_lo, i + 1)
                if i:
                    pe.wait_ge(tk_lo, i)
                for k in range(KC):
                    last = nc.tensor.transpose(bank16(3)[:, k, :], wrow[:, i % 2, D + k * P:D + (k + 1) * P], idh[:, :])
                last.then_inc(tk_T, 1)

            def shared_up(half, c, w):
                tk = slice(half * S, (half + 1) * S)
                if c >= 2:
                    pe.wait_ge(su_hf, half * SC + c - 1)
                for k in range(KC):
                    for n, (wp, xp) in enumerate(((0, 0), (0, 1), (1, 0))):
                        last = mm(PS[:, 4 + 2 * (c % 2) + w, :], SW[:, wp, k, w * SI + c * P:w * SI + (c + 1) * P],
                                  XT[:, xp, k, tk], start=(k == 0 and n == 0), stop=(k == KC - 1 and n == 2))
                if w == 1:
                    last.then_inc(su_done, 1)

            def shared_down(i):
                pb = SD_BANK[i]
                for h in range(2):
                    hs = slice(h * 512, (h + 1) * 512)
                    for c in range(SC):
                        for n, (hp, wp) in enumerate(((0, 0), (1, 0), (0, 1))):
                            mm(PS[:, pb + h, :], HT[:, hp, c, i * P:(i + 1) * P], SW3[:, wp, c, hs],
                               start=(c == 0 and n == 0), stop=False)
                    last = mm(PS[:, pb + h, :], SEL[:, 2, :], BS[:, SI + h * 512:SI + (h + 1) * 512], start=False,
                              stop=True)
                last.then_inc(sd_done, 1)

            def router():
                pe.wait_ge(rw_lo, 1)
                pe.wait_ge(at_read, NT)
                for i in range(NT):
                    o = PS[:, 7, i * 2 * E:(i + 1) * 2 * E]
                    for k in range(KC):
                        mm(o, XT[:, 0, k, i * P:(i + 1) * P], RW[:, k, :, :].rearrange("p h e -> p (h e)"),
                           start=(k == 0), stop=False)
                        last = mm(o[:, 0:E], XT[:, 1, k, i * P:(i + 1) * P], RW[:, k, 0, :], start=False,
                                  stop=(k == KC - 1))
                last.then_inc(lg_done, 1)

            for i in range(TB):
                transpose_q1(i)
            attention(0)
            for i in range(TB):
                transpose_tokens(i)
            pe.wait_ge(tk_hi, TB)
            pe.wait_ge(tk_lo, TB)
            pe.wait_ge(sw_lo, KC // 2)
            pe.wait_ge(sw_lo2, KC // 2)
            pe.wait_ge(at_read, TB)
            for c in range(SC):
                shared_up(0, c, 0)
                if c:
                    transpose_q1(TB + c)
                shared_up(0, c, 1)
                if c == 0:
                    transpose_q1(TB)
            attention(1)
            pe.wait_ge(su_lo, SC)
            pe.wait_ge(sw_lo, KC // 2 + SC)
            pe.wait_ge(bs_lo, 3)
            pe.wait_ge(q1_rdy[0], NT)
            pe.wait_ge(q1_rdy[1], NT)
            pe.wait_ge(r1_rdy, B)
            for i in range(TB):
                if i < 2:
                    pe.wait_ge(at_read, TB + 2 + i)
                else:
                    pe.wait_ge(sd_read, i - 1)
                shared_down(i)
            for i in range(TB, NT):
                transpose_tokens(i)
            pe.wait_ge(tk_hi, NT)
            pe.wait_ge(tk_lo, NT)
            router()
            pe.wait_ge(lg_read, 1)
            for c in range(SC):
                shared_up(1, c, 0)
                shared_up(1, c, 1)
            pe.wait_ge(m_rdy, 1)
            pe.wait_ge(su_hf, 2 * SC)
            Mf = Mh.rearrange("p t e -> p (t e)")
            mm(PS[:, 7, 0:P], onesh[:, :], Mf, start=True, stop=True)
            mm(PS[:, 7, P:2 * P], tri[:, :], Mf, start=True, stop=True).then_inc(rank_done, 1)
            pe.wait_ge(su_lo, 2 * SC)
            shared_down(0)
            shared_down(1)
            pe.wait_ge(slot_rdy, 1)
            for n in range(2 * NT):
                c, t = n // NT, n % NT
                last = mm(PS[:, 7, 0:96], OB[:, c, t, :], OA[:, n, :, :].rearrange("p w a -> p (w a)"), start=(n == 0),
                          stop=(n == 2 * NT - 1))
            last.then_inc(ti_done, 1)
            for j in range(2):
                pe.wait_ge(sd_read, TB + 1 + j)
                shared_down(2 + j)
            pe.wait_ge(sd_read, NT)

            def transpose_gathered(t, par, count):
                pe.wait_ge(tok_in[par], count)
                for h in range(2):
                    if not (isinstance(t, int) and t == 0):
                        pe.wait_ge(xg_hi if h == 0 else xg_lo, t)
                    for k in range(KC):
                        last = nc.tensor.transpose(bank16(2 + h)[:, k, :], XG[par][:, h, k * P:(k + 1) * P], idh[:, :])
                    last.then_inc(xg_T, 1)

            transpose_gathered(0, 0, 16)
            pe.wait_ge(lc_rdy, 1)
            n = tile_count(pe)

            def step(a, j):
                known = isinstance(a, int)
                first = known and a == 0
                loads = loads_before(pe, a)
                loads_last = 0 if first else loads_before(pe, a - 1)
                transpose_gathered(a + 1, 1 - j, 8 * a + (16 if j == 0 else 24))
                if not first:
                    pe.wait_ge(h_hi, a)
                    pe.wait_ge(h_lo, a)
                    if not (known and a < 2):
                        pe.wait_ge(hT_rdy, a - 1)
                    ht = PS[:, 6, 0:256].bitcast(F16).rearrange("p (n t) -> p n t", n=2 * HC)
                    for n in range(2 * HC):
                        last = nc.tensor.transpose(ht[:, n, :], HSP[1 - j][:, n // HC, (n % HC) * P:(n % HC + 1) * P],
                                                   idh[:, :])
                    last.then_inc(hT_done, 1)
                pe.wait_ge(xg_hi, a + 1)
                pe.wait_ge(xg_lo, a + 1)
                pe.wait_ge(w12_lo, 4 * loads)
                pe.wait_ge(sel_rdy, a + 1)
                if not (known and a < 2):
                    pe.wait_ge(h_prod, a - 1)
                for k in range(KC):
                    for n, (xp, wp) in enumerate(((0, 0), (0, 1), (1, 0))):
                        mm(PS[:, 4 + j, :], XGT[j][:, xp, k, :], W12S[j][:, wp, k, :], start=(k == 0 and n == 0),
                           stop=False)
                mm(PS[:, 4 + j, :], SEL[:, j, :], BS[:, 0:SI], start=False, stop=True).then_inc(up_done, 1)
                if not first:
                    pe.wait_ge(hT_rdy, a)
                    pe.wait_ge(w3_lo, 2 * loads_last)
                    if not (known and a < 2):
                        pe.wait_ge(y_rdy, a - 1)
                    for h in range(2):
                        hs = slice(h * 512, (h + 1) * 512)
                        for c in range(HC):
                            for n, (hp, wp) in enumerate(((0, 0), (1, 0), (0, 1))):
                                mm(PS[:, h, :], HTS[1 - j][:, hp, c, :], W3S[1 - j][:, wp, c, hs],
                                   start=(c == 0 and n == 0), stop=False)
                        last = mm(PS[:, h, :], SEL[:, 1 - j, :], BS[:, SI + h * 512:SI + (h + 1) * 512], start=False,
                                  stop=True)
                    last.then_inc(dn_done, 1)

            step(0, 0)
            step(1, 1)
            with pe.Fori(1, MINT // 2) as it:
                step(2 * it, 0)
                step(2 * it + 1, 1)
            with pe.Fori(MINT // 2, STEPS // 2) as it:
                with pe.If(2 * it <= n):
                    step(2 * it, 0)
                with pe.If(2 * it + 1 <= n):
                    step(2 * it + 1, 1)


_INS = ["x", "ctx_4096", "g_xattn", "g_ffn", "L0_xattn_x1_scale", "L0_xattn_x1_zp", "L0_xattn_x2_scale",
        "L0_xattn_x2_zp", "L0_ffn_router_w", "L0_ffn_router_b", "L0_ffn_router_bias", "L0_ffn_ew1", "L0_ffn_eb1",
        "L0_ffn_ew2", "L0_ffn_eb2", "L0_ffn_ew3", "L0_ffn_eb3", "L0_ffn_sw1", "L0_ffn_sb1", "L0_ffn_sw2",
        "L0_ffn_sb2", "L0_ffn_sw3", "L0_ffn_sb3"]
_OUTS = [((2, 512, 1024), "float32")]


def kernel(**inputs):
    import numpy as _np
    import concourse.bacc as _bacc
    from concourse import mybir as _mybir
    from concourse.bass_utils import run_bass_kernel_spmd as _run

    nc = _bacc.Bacc("TRN2", target_bir_lowering=False, num_devices=1)
    arrays, args = {}, []
    for name in _INS:
        a = _np.ascontiguousarray(inputs[name])
        arrays[f"in_{name}_dram"] = a
        args.append(nc.dram_tensor(f"in_{name}_dram", a.shape, _mybir.dt.from_np(a.dtype), kind="ExternalInput").ap())
    for i, (shape, dtype) in enumerate(_OUTS):
        dt = _mybir.dt.from_np(_np.dtype(dtype))
        args.append(nc.dram_tensor(f"out_{i}_dram", shape, dt, kind="ExternalOutput").ap())
    build(nc, *args)
    r = _run(nc, [arrays], core_ids=[0])
    got = tuple(r.results[0][f"out_{i}_dram"] for i in range(len(_OUTS)))
    return got[0]
```

```python
import concourse.bass as bass
from concourse import mybir
from contextlib import ExitStack

F32, F16, BF16, I32 = mybir.dt.float32, mybir.dt.float16, mybir.dt.bfloat16, mybir.dt.int32
ALU = mybir.AluOpType
ACT = mybir.ActivationFunctionType
AX = mybir.AxisListType.X

P = 128
B, S, D = 2, 512, 1024
KC = D // P
NT = B * S // P
TB = NT // B
E, INTER = 16, 256
GROUPS = 4
SI = 2 * INTER
SC = SI // P
HC = INTER // P
TOPK = 2
MAXT = E + (TOPK * NT * P - E) // P
MINT = TOPK * NT
STEPS = MAXT + 1
COLS = STEPS + 4

QMAX = 255.0
HALF = 128.0
ROUND = 12582912.0
XS = 16.0
WS = 16.0
HS = 0.25
UPS = XS * WS
DNS = HS * WS
GS = 16.0
SELV = 4.0
EPS = 1e-5
BIG = 1e30


def build(nc, x, ctx_in, g_xattn, g_ffn, x1_scale, x1_zp, x2_scale, x2_zp, router_w, router_b, router_bias,
          ew1, eb1, ew2, eb2, ew3, eb3, sw1, sb1, sw2, sb2, sw3, sb3, out):
    x_t = x.rearrange("b (t p) d -> (b t) p d", p=P)
    split_dram = nc.dram_tensor("split_dram", [NT * P, 2 * D], F16, kind="Internal").ap()
    out_rows = out.rearrange("b s d -> (b s) d")
    T = NT * P

    es = ExitStack()
    with es:
        def sb(name, shape, dt):
            return es.enter_context(nc.sbuf_tensor(name, shape, dt))

        sems = {}

        def sem(name):
            sems[name] = es.enter_context(nc.semaphore(name))
            return sems[name]

        X = sb("X", [P, NT, D], F32)
        areaT = sb("areaT", [P, 8192], F32)
        area2 = sb("area2", [P, 4096], F32)
        ring = sb("ring", [P, 4, D], F32)
        rows = sb("rows", [P, 2, D], F32)
        areaQ = sb("areaQ", [P, 3072], F32)
        wrow = sb("wrow", [P, 2, 2 * D], F16)
        areaW = sb("areaW", [P, 8192], F32)
        SW3 = sb("SW3", [P, 2, SC, D], F16)
        areaH = sb("areaH", [P, 2048], F32)
        SA = sb("SA", [P, 2, S], F32)

        def view(area, lo, n, dt, pat=None, **kw):
            v = area[:, lo:lo + n]
            if dt is not F32:
                v = v.bitcast(dt)
            return v.rearrange(pat, **kw) if pat else v

        XT = view(areaT, 0, 8192, F16, "p (h k t) -> p h k t", h=2, k=KC)
        Q2 = view(area2, 0, 4096, BF16, "p (k n) -> p k n", k=KC)
        Q1T = view(areaQ, 0, 2048, BF16, "p (j k t) -> p j k t", j=TB, k=KC)
        CT = view(areaQ, 2048, 1024, F32)
        SW = view(areaW, 0, 8192, F16, "p (h k n) -> p h k n", h=2, k=KC)
        HT = view(areaH, 0, 2048, F16, "p (h c t) -> p h c t", h=2, c=SC)
        bias32 = areaH[0:64, 0:1536]
        W12F = [view(areaT, 0, 4096, F32, "p (k n) -> p k n", k=KC),
                ring[:, :, :].rearrange("p a n -> p (a n)").rearrange("p (k n) -> p k n", k=KC)]
        W3S = [view(areaT, 4096 + 2048 * i, 2048, F16, "p (h c n) -> p h c n", h=2, c=HC) for i in range(2)]
        FILL = view(areaT, 6144, 2048, F16, "p (a s) -> p a s", a=32)
        W3F = wrow[:, :, :].rearrange("p a n -> p (a n)").bitcast(F32).rearrange("p (c n) -> p c n", c=HC)
        W12S = [view(areaW, 4096 * i, 4096, F16, "p (h k n) -> p h k n", h=2, k=KC) for i in range(2)]
        XG = [view(area2, 1024 * i, 1024, F16, "p (h n) -> p h n", h=2) for i in range(2)]
        XGT = [view(area2, 2048 + 1024 * i, 1024, F16, "p (h k t) -> p h k t", h=2, k=KC) for i in range(2)]
        HF = [view(areaH, 256 * i, 256, F32) for i in range(2)]
        HSP = [view(areaH, 512 + 256 * i, 256, F16, "p (h n) -> p h n", h=2) for i in range(2)]
        HTS = [view(areaH, 1024 + 256 * i, 256, F16, "p (h c t) -> p h c t", h=2, c=HC) for i in range(2)]

        BS = sb("BS", [64, SI + D], F16)
        SEL = sb("SEL", [64, 3, P], F16)
        SELQ = sb("SELQ", [64, COLS], F32)
        RW32 = sb("RW32", [P, KC, E], F32)
        RW = sb("RW", [P, KC, 2, E], F16)
        rb = sb("rb", [P, 2, E], F32)
        sbT = sb("sbT", [P, 2, SC], F32)
        sc6 = sb("sc6", [P, 8], F32)
        cf = sb("cf", [P, 16], F32)
        stats = sb("stats", [P, NT, 12], F32)
        mv = sb("mv", [P, NT, 2], F32)
        lnA = sb("lnA", [P, NT], F32)
        lnB = sb("lnB", [P, NT], F32)
        lnR = sb("lnR", [P, NT], F32)
        lnV = sb("lnV", [P, NT], F32)
        mhalf = sb("mhalf", [P, TB], F32)
        r1 = sb("r1", [P, TB], F32)
        idf = sb("idf", [P, P], F32)
        idh = sb("idh", [P, P], F16)
        slots = sb("slots", [P, P], F32)
        rown = sb("rown", [P, 1], F16)
        lack = sb("lack", [P, 32], F16)
        empty = sb("empty", [P, 32], F16)
        spare = sb("spare", [P, 32], F32)
        onesb = sb("onesb", [P, P], BF16)
        onesh = sb("onesh", [P, P], F16)
        tri = sb("tri", [P, P], F16)
        iota = sb("iota", [P, P], F32)
        pcol = sb("pcol", [P, 8], F32)
        desc = sb("desc", [P, E], F32)
        TI = sb("TI", [P, COLS], I32)
        tok1 = sb("tok1", [P, 2], I32)
        RI = sb("RI", [P, MAXT + 1], I32)
        row1 = sb("row1", [P, 2], I32)
        GT = sb("GT", [P, MAXT + 1], F32)
        EL = sb("EL", [P, COLS], I32)
        LC = sb("LC", [P, COLS], I32)
        ntiles = sb("ntiles", [P, 1], I32)
        CV = sb("CV", [P, 2, NT], F32)
        CVS = sb("CVS", [P, 2, 2 * NT], F16)

        PS = es.enter_context(nc.psum_tensor("PS", [P, 8, 512], F32))

        def bank16(b):
            return PS[:, b, :].bitcast(F16).rearrange("p (k t) -> p k t", k=KC)

        ofs = [0]

        def small(n, pat=None, dt=F32, **kw):
            lo = ofs[0]
            ofs[0] += n
            assert ofs[0] <= 3072
            return view(areaQ, lo, n, dt, pat, **kw)

        TE = "p (t e) -> p t e"
        lg = small(P, TE, t=NT)
        sco = small(P, TE, t=NT)
        t1 = small(P, TE, t=NT)
        t2 = small(P, TE, t=NT)
        oh = [small(P, TE, t=NT) for _ in range(2)]
        gm = small(NT * GROUPS, "p (t g) -> p t g", t=NT)
        gt = small(NT * GROUPS, "p (t g) -> p t g", t=NT)
        go = [small(NT * GROUPS, "p (t g) -> p t g", t=NT) for _ in range(2)]
        m8 = small(NT)
        Mh = small(P // 2, TE, dt=F16, t=NT)
        run = small((NT + 1) * E, "p (t e) -> p t e", t=NT + 1)
        sA = small(8 + E)
        sB = small(8 + E)
        ntl = small(E)
        base = small(E)
        pos = small(2 * NT, "p (j t) -> p j t", j=2)
        aa = small(2 * NT, "p (j t) -> p j t", j=2)
        bb = small(2 * NT, "p (j t) -> p j t", j=2)
        big = small(1024)
        GE = big[:, 0:2 * NT * 33].rearrange("p (j t a) -> p j t a", j=2, a=33)
        OB = view(areaQ, ofs[0] - 1024, 1024, F16, "p (j t s) -> p j t s", j=2, t=NT)
        OA = SA[:, :, :].rearrange("p a n -> p (a n)")[:, 0:768].bitcast(F16).rearrange("p (n w a) -> p n w a", w=3, a=32)
        ECM = SA[:, 1, :]

        AT_BANK = (0, 4, 2, 0)
        SD_BANK = (4, 2, 6, 0, 4, 2, 0, 4)

        WROW = [wrow[:, i % 2, :] for i in range(NT)]
        for q in range(2):
            WROW[2 + q] = SW3[:, 0, 2 * q:2 * q + 2, :].rearrange("p a n -> p (a n)")
            WROW[TB + 2 + q] = ring[:, q, :].bitcast(F16)

        x_in = [sem(f"x_in{i}") for i in range(NT)]
        ring_in = [sem(f"ring_in{i}") for i in range(4)]
        sw1_in = [sem(f"sw1_in{i}") for i in range(4)]
        small_in, bias_in = sem("small_in"), sem("bias_in")
        consts, ident_rdy, v_chain = sem("consts"), sem("ident_rdy"), sem("v_chain")
        coef1, tanh_rdy, mv_rdy, rstd_rdy = sem("coef1"), sem("tanh_rdy"), sem("mv_rdy"), sem("rstd_rdy")
        var_eps = sem("var_eps")
        y_relu, y_rnd, q1_T = sem("y_relu"), sem("y_rnd"), sem("q1_T")
        q1_rdy = [sem("q1_rdy0"), sem("q1_rdy1")]
        r1_rdy, x_r1, x_ct, coef2 = sem("r1_rdy"), sem("x_r1"), sem("x_ct"), sem("coef2")
        sw_scaled, sw_lo2 = sem("sw_scaled"), sem("sw_lo2")
        c_relu, c_rnd, q2_rdy = sem("c_relu"), sem("c_rnd"), sem("q2_rdy")
        sw_hi, sw_lo = sem("sw_hi"), sem("sw_lo")
        r1_done, r1_read, col_done, col_read = sem("r1_done"), sem("r1_read"), sem("col_done"), sem("col_read")
        at_done, at_read = sem("at_done"), sem("at_read")
        ln_xs, ln_hi, ln_lo = sem("ln_xs"), sem("ln_hi"), sem("ln_lo")
        split_out = [sem("split_out0"), sem("split_out1")]
        tk_T, tk_hi, tk_lo = sem("tk_T"), sem("tk_hi"), sem("tk_lo")
        rw_hi, rw_lo, bs_zero, bs_hi, bs_lo = sem("rw_hi"), sem("rw_lo"), sem("bs_zero"), sem("bs_hi"), sem("bs_lo")
        su_done, su_silu, su_hf, su_hi, su_lo = sem("su_done"), sem("su_silu"), sem("su_hf"), sem("su_hi"), sem("su_lo")
        sd_done, sd_read, sd_copied, sd_sum = sem("sd_done"), sem("sd_read"), sem("sd_copied"), sem("sd_sum")
        lg_done, lg_read, lg_sub, lg_exp = sem("lg_done"), sem("lg_read"), sem("lg_sub"), sem("lg_exp")
        m_rdy, rank_done, rank_read = sem("m_rdy"), sem("rank_done"), sem("rank_read")
        lc_rdy, sum_in, gt_rdy = sem("lc_rdy"), sem("sum_in"), sem("gt_rdy")
        el_rdy, slot_rdy, ti_done, ti_rdy = sem("el_rdy"), sem("slot_rdy"), sem("ti_done"), sem("ti_rdy")
        gathers, tok_rdy, tok_in = sem("gathers"), sem("tok_rdy"), [sem("tok_in0"), sem("tok_in1")]
        w12_in, w3_in = [sem("w12_in0"), sem("w12_in1")], [sem("w3_in0"), sem("w3_in1")]
        w12_hi, w12_lo = [sem("w12_hi0"), sem("w12_hi1")], [sem("w12_lo0"), sem("w12_lo1")]
        w3_hi, w3_lo = [sem("w3_hi0"), sem("w3_hi1")], [sem("w3_lo0"), sem("w3_lo1")]
        sel_rdy = sem("sel_rdy")
        xg_T, xg_hi, xg_lo = sem("xg_T"), sem("xg_hi"), sem("xg_lo")
        up_done, h_silu, h_prod, h_hi, h_lo = sem("up_done"), sem("h_silu"), sem("h_prod"), sem("h_hi"), sem("h_lo")
        hT_done, hT_rdy, dn_done, y_rdy = sem("hT_done"), sem("hT_rdy"), sem("dn_done"), sem("y_rdy")
        waited = sem("waited")
        empty_rdy, empty_done, fill_rdy = sem("empty_rdy"), sem("empty_done"), sem("fill_rdy")
        fill_done, ri_rdy = sem("fill_done"), sem("ri_rdy")
        row_rdy, y_out, out_done = sem("row_rdy"), sem("y_out"), sem("out_done")

        block = es.enter_context(nc.Block())

        CHUNKS = ([("ctx", 0, k) for k in range(KC)] + [("sw", 0, k) for k in range(KC)]
                  + [("ctx", 1, k) for k in range(KC)] + [("sw3", 0, c) for c in range(SC)])
        RING_AT = {c: r for r, c in enumerate(CHUNKS)}

        def arrived(eng, r):
            eng.wait_ge(ring_in[r % 4], 16 * (r // 4 + 1))

        def consumed(r):
            kind, b, k = CHUNKS[r]
            if kind == "ctx":
                return q2_rdy, b * KC + k + 1
            if kind == "sw" and k >= KC // 2:
                return sw_lo2, k - KC // 2 + 1
            return sw_lo, (k if kind == "sw" else KC // 2 + k) + 1

        def tile_count(eng):
            return eng.value_load(ntiles[0:1, 0:1], min_val=MINT, max_val=MAXT)

        def loads_before(eng, t):
            return eng.value_load(LC[0:1, bass.ds(t, 1)], min_val=1, max_val=MAXT)

        @block.sync
        def _(sp):
            scalars = (x1_scale, x1_zp, x2_scale, x2_zp, g_xattn, g_ffn)
            for i in range(TB):
                sp.dma_start(X[:, i, :], x_t[i]).then_inc(x_in[i], 16)
                for n in range(2 * i, min(2 * i + 2, len(scalars))):
                    sp.dma_start(sc6[:, n:n + 1], scalars[n].partition_broadcast(P)).then_inc(small_in, 16)

            def load_chunk(r):
                kind, b, k = CHUNKS[r]
                if r >= 4:
                    sp.wait_ge(*consumed(r - 4))
                rs = slice(k * P, (k + 1) * P)
                if kind == "ctx":
                    sp.dma_start(ring[:, r % 4, :], ctx_in[b, rs, :]).then_inc(ring_in[r % 4], 16)
                elif kind == "sw3":
                    sp.dma_start(ring[:, r % 4, :], sw3[rs, :]).then_inc(ring_in[r % 4], 16)
                else:
                    sp.dma_start(ring[:, r % 4, :].rearrange("p (w n) -> p w n", w=2)[:, 0, :], sw1[rs, :])\
                        .then_inc(sw1_in[r % 4], 16)
                    sp.dma_start(ring[:, r % 4, SI:2 * SI], sw2[rs, :]).then_inc(ring_in[r % 4], 16)

            for r in range(4):
                load_chunk(r)
            sp.wait_ge(bs_zero, 2)
            for q in (0, 32):
                sp.dma_start(areaH[q:q + E, 0:INTER], eb1[:, :]).then_inc(bias_in, 16)
                sp.dma_start(areaH[q:q + E, INTER:SI], eb2[:, :]).then_inc(bias_in, 16)
                sp.dma_start(areaH[q:q + E, SI:SI + D], eb3[:, :]).then_inc(bias_in, 16)
                sp.dma_start(areaH[q + E:q + E + 1, SI:SI + D], sb3.rearrange("(a n) -> a n", a=1)).then_inc(bias_in, 16)
            sp.dma_start(rb[:, 0, :], router_b.partition_broadcast(P)).then_inc(bias_in, 16)
            sp.dma_start(rb[:, 1, :], router_bias.partition_broadcast(P)).then_inc(bias_in, 16)
            sp.dma_start(RW32[:, :, :], router_w.rearrange("(k p) e -> p k e", p=P)).then_inc(bias_in, 16)
            with nc.allow_non_contiguous_dma(reason="bias vectors laid along the partitions"):
                sp.dma_start(sbT[:, 0, :], sb1.rearrange("(c p) -> p c", p=P)).then_inc(bias_in, 16)
                sp.dma_start(sbT[:, 1, :], sb2.rearrange("(c p) -> p c", p=P)).then_inc(bias_in, 16)
            for r in range(4, 2 * KC):
                load_chunk(r)
            for i in range(TB, NT):
                sp.dma_start(X[:, i, :], x_t[i]).then_inc(x_in[i], 16)

            def store_split(i):
                sp.wait_ge(ln_hi, i + 1)
                sp.wait_ge(ln_lo, i + 1)
                sp.dma_start(split_dram[i * P:(i + 1) * P, :], WROW[i]).then_inc(split_out[i % 2], 16)

            r = 2 * KC
            for i in range(TB):
                store_split(i)
                if i % 2:
                    load_chunk(r)
                    load_chunk(r + 1)
                    r += 2
            for r in range(r, len(CHUNKS)):
                load_chunk(r)
            for i in range(TB, NT):
                store_split(i)

            def expert_of(t):
                return sp.value_load(EL[0:1, bass.ds(t, 1)], min_val=0, max_val=E - 1)

            def load_up(e, j):
                for w, lo in ((ew1, 0), (ew2, INTER)):
                    sp.dma_start(W12F[j][:, :, lo:lo + INTER],
                                 w[bass.ds(e, 1), :, :].rearrange("o (k p) n -> p (o k) n", p=P)).then_inc(w12_in[j], 16)

            def load_down(e, j):
                sp.dma_start(W3F[:, :, :],
                             ew3[bass.ds(e, 1), :, :].rearrange("o (c p) n -> p (o c) n", p=P)).then_inc(w3_in[j], 16)

            def store_sum(i):
                sp.dma_start(out_rows[i * P:(i + 1) * P, :], X[:, i, :]).then_inc(sum_in, 16)

            for i in range(TB):
                sp.wait_ge(sd_read, i + 1)
                store_sum(i)
            sp.wait_ge(sw_lo, KC // 2 + SC)
            sp.wait_ge(el_rdy, 1)
            sp.wait_ge(su_done, 2 * SC)
            load_up(expert_of(0), 0)
            sp.wait_ge(split_out[0], 16 * NT // 2)
            sp.wait_ge(split_out[1], 16 * NT // 2)
            load_down(expert_of(0), 0)
            e1 = expert_of(1)
            sp.wait_ge(tok_in[0], 16)
            load_up(e1, 1)
            sp.wait_ge(tok_in[0], 32)
            for i in range(TB, NT):
                sp.wait_ge(sd_sum, i - TB + 1)
                store_sum(i)
            sp.wait_ge(lc_rdy, 1)
            n = tile_count(sp)

            def step(a, j):
                first = isinstance(a, int) and a == 0
                loads = loads_before(sp, a)
                e_up, loads_up = expert_of(a + 2), loads_before(sp, a + 2)
                with sp.If(loads_up > loads):
                    sp.wait_ge(w12_lo[j], 4 * loads + 4)
                    sp.sem_inc(waited, 1)
                    sp.wait_ge(tok_in[1 - j], 8 * a + (16 if j == 0 else 24))
                    load_up(e_up, j)
                e_down = expert_of(a + 1)
                if first:
                    sp.wait_ge(w3_lo[0], 2)
                    load_down(e_down, 1)
                else:
                    loads_last, loads_down = loads_before(sp, a - 1), loads_before(sp, a + 1)
                    with sp.If(loads_down > loads_last):
                        sp.wait_ge(w3_lo[j], 2 * loads)
                        sp.sem_inc(waited, 1)
                        sp.wait_ge(w3_lo[1 - j], 2 * loads_last)
                        sp.sem_inc(waited, 1)
                        sp.wait_ge(tok_in[j], 8 * a + (32 if j == 0 else 24))
                        load_down(e_down, 1 - j)

            step(0, 0)
            step(1, 1)
            with sp.Fori(1, MINT // 2) as it:
                step(2 * it, 0)
                step(2 * it + 1, 1)
            with sp.Fori(MINT // 2, STEPS // 2) as it:
                with sp.If(2 * it < n):
                    step(2 * it, 0)
                with sp.If(2 * it + 1 < n):
                    step(2 * it + 1, 1)

            sp.wait_ge(sum_in, 16 * NT)
            sp.wait_ge(y_out, 16 * n)
            sp.sem_inc(waited, 1)

        @block.gpsimd
        def _(pool):
            nc.gpsimd.memset(areaH[0:64, 0:SI + D], 0.0).then_inc(bs_zero, 1)
            nc.gpsimd.memset(SEL[:, 2, :], 0.0).then_inc(bs_zero, 1)
            nc.gpsimd.memset(idf[:, :], 0.0).then_inc(consts, 1)
            nc.gpsimd.memset(idh[:, :], 0.0).then_inc(consts, 1)
            nc.gpsimd.memset(tri[:, :], 1.0).then_inc(consts, 1)
            nc.gpsimd.memset(onesb[:, :], 1.0).then_inc(consts, 1)
            nc.gpsimd.memset(onesh[:, :], 1.0).then_inc(consts, 1)
            nc.gpsimd.iota(iota[:, :], pattern=[[1, P]], base=0, channel_multiplier=0,
                           allow_small_or_imprecise_dtypes=True).then_inc(consts, 1)
            nc.gpsimd.iota(pcol[:, :], pattern=[[P, 8]], base=0, channel_multiplier=1,
                           allow_small_or_imprecise_dtypes=True).then_inc(consts, 1)
            nc.gpsimd.iota(desc[:, :], pattern=[[-1, E]], base=E, channel_multiplier=0,
                           allow_small_or_imprecise_dtypes=True).then_inc(consts, 1)
            nc.gpsimd.memset(TI[:, :], 0).then_inc(consts, 1)
            nc.gpsimd.memset(mhalf[:, :], -0.5).then_inc(consts, 1)
            pool.wait_ge(consts, 10)
            for m in (idf, idh):
                nc.gpsimd.affine_select(out=m[:, :], in_=m[:, :], compare_op=ALU.not_equal, fill=1.0, base=0,
                                        pattern=[[-1, P]], channel_multiplier=1).then_inc(ident_rdy, 1)
            nc.gpsimd.affine_select(out=tri[:, :], in_=tri[:, :], compare_op=ALU.is_gt, fill=0.0, base=0,
                                    pattern=[[1, P]], channel_multiplier=-1).then_inc(ident_rdy, 1)

            powers = [0]

            def rstd(lo, n, tiles):
                pool.wait_ge(mv_rdy, tiles)
                nc.gpsimd.tensor_scalar(lnV[:, lo:lo + n], mv[:, lo:lo + n, 1], EPS, 1.0, ALU.add, ALU.mult)\
                    .then_inc(var_eps, 1)
                powers[0] += 1
                pool.wait_ge(var_eps, powers[0])
                nc.gpsimd.tensor_tensor(lnR[:, lo:lo + n], lnV[:, lo:lo + n], mhalf[:, 0:n], ALU.pow)\
                    .then_inc(rstd_rdy, 1)

            def lo_chunk(k):
                pool.wait_ge(sw_scaled, k - KC // 2 + 1)
                nc.gpsimd.tensor_tensor(SW[:, 1, k, :], ring[:, RING_AT["sw", 0, k] % 4, :], SW[:, 0, k, :],
                                        ALU.subtract).then_inc(sw_lo2, 1)

            for b in range(B):
                if b == 0:
                    rstd(0, 2, 2)
                    rstd(2, 2, TB)
                else:
                    rstd(TB, TB, 3 * TB)
                for k in range(KC):
                    n = b * KC + k
                    pool.wait_ge(c_rnd, n + 1)
                    if b and k == 0:
                        pool.wait_ge(at_done, TB)
                    nc.gpsimd.tensor_scalar(Q2[:, k, :], ring[:, RING_AT["ctx", b, k] % 4, :],
                                            -(ROUND + HALF), 1.0, ALU.add, ALU.mult).then_inc(q2_rdy, 1)
                pool.wait_ge(col_read, b + 1)
                for i in range(b * TB + 1, b * TB + TB):
                    pool.wait_ge(x_r1, i + 1)
                    nc.gpsimd.tensor_tensor(X[:, i, :], X[:, i, :], CT, ALU.add).then_inc(x_ct, 1)
                if b == 0:
                    rstd(0, 2, TB + 2)
                    lo_chunk(KC // 2)
                    rstd(2, 2, TB + 4)
                    lo_chunk(KC // 2 + 1)
                    lo_chunk(KC // 2 + 2)
                    lo_chunk(KC // 2 + 3)
                else:
                    rstd(TB, TB, 4 * TB)

            def gather(t, j):
                pool.wait_ge(tok_rdy, t + 1)
                pool.sem_inc(gathers, 1)
                pool.indirect_dma_start(out=XG[j].rearrange("p h n -> p (h n)"), out_offset=None,
                                        in_=split_dram[:, :],
                                        in_offset=bass.IndirectOffsetOnAxis(tok1[:, j:j + 1], 0)).then_inc(tok_in[j], 16)

            pool.wait_ge(at_done, NT)
            pool.wait_ge(split_out[0], 16 * NT // 2)
            pool.wait_ge(split_out[1], 16 * NT // 2)

            def add_shared(i):
                pool.wait_ge(sd_copied, i + 1)
                nc.gpsimd.tensor_tensor(X[:, TB + i, :], X[:, TB + i, :], rows[:, i % 2, :], ALU.add).then_inc(sd_sum, 1)

            add_shared(0)
            add_shared(1)
            gather(0, 0)
            gather(1, 1)
            add_shared(2)
            add_shared(3)

            def scatter(t, j):
                pool.wait_ge(y_rdy, t + 1)
                pool.sem_inc(gathers, 1)
                if not (isinstance(t, int) and t == 0):
                    pool.wait_ge(y_out, 16 * t)
                    pool.sem_inc(gathers, 1)
                pool.indirect_dma_start(out=out_rows[:, :], out_offset=bass.IndirectOffsetOnAxis(row1[:, j:j + 1], 0),
                                        in_=rows[:, j, :], in_offset=None, compute_op=ALU.add).then_inc(y_out, 16)

            def step(a, j):
                gather(a + 2, j)
                if not (isinstance(a, int) and a == 0):
                    if isinstance(a, int) and a == 1:
                        pool.wait_ge(sum_in, 16 * NT)
                    scatter(a - 1, 1 - j)

            def last_step(a, j):
                scatter(a - 1, 1 - j)

            pool.wait_ge(lc_rdy, 1)
            n = tile_count(pool)
            step(0, 0)
            step(1, 1)
            with pool.Fori(1, MINT // 2) as it:
                step(2 * it, 0)
                step(2 * it + 1, 1)
            with pool.Fori(MINT // 2, STEPS // 2) as it:
                with pool.If(2 * it <= n):
                    with pool.If(2 * it < n):
                        step(2 * it, 0)
                    with pool.If(2 * it >= n):
                        last_step(2 * it, 0)
                with pool.If(2 * it + 1 <= n):
                    with pool.If(2 * it + 1 < n):
                        step(2 * it + 1, 1)
                    with pool.If(2 * it + 1 >= n):
                        last_step(2 * it + 1, 1)
            pool.wait_ge(tok_in[0], 16 * (((n + 1) >> 1) + 1))
            pool.sem_inc(gathers, 1)
            pool.wait_ge(tok_in[1], 16 * ((n >> 1) + 1))
            pool.sem_inc(gathers, 1)

        @block.scalar
        def _(act):
            act.wait_ge(small_in, 96)
            nc.scalar.activation(cf[:, 0:2], sc6[:, 4:6], ACT.Tanh).then_inc(tanh_rdy, 1)

            def relu_x(i):
                act.wait_ge(coef1, (1, 1, 2, 2)[i] if i < TB else 3)
                if i >= 2:
                    act.wait_ge(q1_T, 2 * (i - 1))
                if i in (TB, TB + 1):
                    act.wait_ge(ln_lo, i - 1)
                nc.scalar.activation(rows[:, i % 2, :], X[:, i, :], ACT.Relu, bias=lnB[:, i:i + 1],
                                     scale=lnA[:, i:i + 1]).then_inc(y_relu, 1)

            def evac_q1(i):
                act.wait_ge(q1_T, 2 * i + 1)
                nc.scalar.activation(Q1T[:, i % TB, 0:4, :].rearrange("p k t -> p (k t)"),
                                     PS[:, 2, :], ACT.Identity, bias=cf[:, 10:11]).then_inc(q1_rdy[0], 1)

            def relu_ctx(b, k):
                r = RING_AT["ctx", b, k]
                arrived(act, r)
                nc.scalar.activation(ring[:, r % 4, :], ring[:, r % 4, :], ACT.Relu, bias=sc6[:, 3:4],
                                     scale=cf[:, 2:3]).then_inc(c_relu, 1)

            def hi_chunk(kind, k):
                r = RING_AT[kind, 0, k]
                arrived(act, r)
                if kind == "sw":
                    act.wait_ge(sw1_in[r % 4], 16 * (k // 4 + 1))
                dst = SW[:, 0, k, :] if kind == "sw" else SW3[:, 0, k, :]
                nc.scalar.activation(dst, ring[:, r % 4, :], ACT.Copy, scale=WS).then_inc(sw_hi, 1)
                if kind == "sw" and k >= KC // 2:
                    nc.scalar.activation(ring[:, r % 4, :], ring[:, r % 4, :], ACT.Copy, scale=WS).then_inc(sw_scaled, 1)

            def add_r1(b):
                act.wait_ge(r1_rdy, b + 1)
                for i in range(b * TB, b * TB + TB):
                    nc.scalar.activation(X[:, i, :], X[:, i, :], ACT.Identity, bias=r1[:, i % TB:i % TB + 1])\
                        .then_inc(x_r1, 1)

            def ln_hi_row(i):
                act.wait_ge(coef2, (1, 1, 2, 2)[i] if i < TB else 3)
                if i >= 2:
                    act.wait_ge(ln_lo, i - 1)
                if i % TB < 2:
                    act.wait_ge(q1_T, 2 * TB * (i // TB + 1))
                nc.scalar.activation(rows[:, i % 2, :], X[:, i, :], ACT.Identity, bias=lnB[:, i:i + 1],
                                     scale=lnA[:, i:i + 1]).then_inc(ln_xs, 1)
                act.wait_ge(ln_xs, i + 1)
                if i in (TB, TB + 1):
                    act.wait_ge(split_out[i % 2], 16 * TB // 2)
                if i >= TB + 2:
                    act.wait_ge(sw_lo, KC // 2 + SC)
                nc.scalar.activation(WROW[i][:, 0:D], rows[:, i % 2, :], ACT.Copy).then_inc(ln_hi, 1)

            def tk_lo_evac(i):
                act.wait_ge(tk_T, 2 * i + 2)
                nc.scalar.activation(XT[:, 1, :, i * P:(i + 1) * P], bank16(3), ACT.Copy).then_inc(tk_lo, 1)

            def su_act(u):
                act.wait_ge(su_done, u + 1)
                if u >= 2:
                    act.wait_ge(su_lo, u - 1)
                nc.scalar.activation(SA[:, u % 2, :], PS[:, 4 + 2 * (u % 2), :], ACT.Silu,
                                     bias=sbT[:, 0, u % SC:u % SC + 1], scale=1.0 / UPS).then_inc(su_silu, 1)
                act.wait_ge(su_hf, u + 1)
                if u == SC:
                    act.wait_ge(sd_done, TB)
                nc.scalar.activation(HT[:, 0, u % SC, :], SA[:, u % 2, :], ACT.Copy, scale=HS / UPS).then_inc(su_hi, 1)

            def small_work():
                act.wait_ge(bias_in, 16 * 13)
                nc.scalar.activation(BS[:, 0:SI], areaH[0:64, 0:SI], ACT.Copy, scale=UPS / SELV).then_inc(bs_hi, 1)
                nc.scalar.activation(BS[:, SI:], areaH[0:64, SI:SI + D], ACT.Copy, scale=DNS / SELV).then_inc(bs_hi, 1)
                nc.scalar.activation(RW[:, :, 0, :], RW32[:, :, :], ACT.Copy, scale=WS).then_inc(rw_hi, 1)

            act.wait_ge(tanh_rdy, 2)
            relu_ctx(0, 0)
            relu_x(0)
            relu_x(1)
            for k in range(1, 4):
                relu_ctx(0, k)
            for i in range(TB):
                evac_q1(i)
                if i + 2 < TB:
                    relu_x(i + 2)
                if i:
                    relu_ctx(0, i + 3)
            relu_ctx(0, KC - 1)
            small_work()
            for k in range(KC // 2):
                hi_chunk("sw", k)
            add_r1(0)
            for k in range(KC // 2, KC):
                hi_chunk("sw", k)
            ln_hi_row(0)
            ln_hi_row(1)
            ln_hi_row(2)
            tk_lo_evac(0)
            ln_hi_row(3)
            for i in range(1, TB):
                tk_lo_evac(i)
            act.wait_ge(bs_lo, 2)
            relu_x(TB)
            relu_x(TB + 1)
            for c in range(SC):
                relu_ctx(1, 2 * c)
                relu_ctx(1, 2 * c + 1)
                su_act(c)
                for i in ((TB, TB + 1), (TB + 2,), (TB + 3,), ())[c]:
                    evac_q1(i)
                    if i + 2 < NT:
                        relu_x(i + 2)
            for j in range(2):
                act.wait_ge(split_out[j], 16 * TB // 2)
            for c in range(SC):
                hi_chunk("sw3", c)
            add_r1(1)
            for i in range(TB, NT):
                ln_hi_row(i)
            for i in range(TB, NT):
                tk_lo_evac(i)
            act.wait_ge(lg_sub, 1)
            nc.scalar.activation(t1[:, :, :], lg[:, :, :], ACT.Exp).then_inc(lg_exp, 1)
            for c in range(SC):
                su_act(SC + c)

            def split_up(loads, j):
                act.wait_ge(w12_in[j], 32 * loads)
                for q in range(4):
                    nc.scalar.activation(W12S[j][:, 0, 2 * q:2 * q + 2, :], W12F[j][:, 2 * q:2 * q + 2, :], ACT.Copy,
                                         scale=WS).then_inc(w12_hi[j], 1)

            def select(t, j):
                nc.scalar.activation(SEL[:, j, :], SELQ[:, bass.ds(t, 1)].to_broadcast([64, P]), ACT.Copy)\
                    .then_inc(sel_rdy, 1)

            def tokens_low(t, j):
                act.wait_ge(xg_T, 2 * t + 2)
                nc.scalar.activation(XGT[j][:, 1, :, :], bank16(3), ACT.Copy).then_inc(xg_lo, 1)

            def tokens_of(t, j):
                nc.scalar.activation(tok1[:, j:j + 1], TI[:, bass.ds(t, 1)], ACT.Copy).then_inc(tok_rdy, 1)

            def copy_shared(i):
                act.wait_ge(sd_done, TB + i + 1)
                act.wait_ge(ln_lo, NT)
                if i >= 2:
                    act.wait_ge(sd_sum, i - 1)
                pb = SD_BANK[TB + i]
                nc.scalar.activation(rows[:, i % 2, :].rearrange("p (h n) -> p h n", h=2), PS[:, pb:pb + 2, :],
                                     ACT.Copy, scale=cf[:, 11:12]).then_inc(sd_copied, 1)

            for i in range(TB - 1):
                copy_shared(i)
            for j in range(2):
                act.sem_inc(w12_hi[j], 4)
                act.sem_inc(w3_hi[j], 2)
            act.wait_ge(ti_rdy, 1)
            tokens_of(0, 0)
            tokens_of(1, 1)
            split_up(1, 0)
            copy_shared(TB - 1)
            act.wait_ge(el_rdy, 1)
            select(0, 0)
            tokens_low(0, 0)

            def split_down(loads, j):
                act.wait_ge(w3_in[j], 16 * loads)
                for q in range(HC):
                    nc.scalar.activation(W3S[j][:, 0, q, :], W3F[:, q, :], ACT.Copy, scale=WS).then_inc(w3_hi[j], 1)

            def last_step(a, j):
                if not (isinstance(a, int) and a < 2):
                    act.wait_ge(y_out, 16 * a - 16)
                nc.scalar.activation(row1[:, 1 - j:2 - j], RI[:, bass.ds(a - 1, 1)], ACT.Copy).then_inc(row_rdy, 1)
                act.wait_ge(dn_done, a)
                act.wait_ge(row_rdy, a)
                nc.scalar.activation(rows[:, 1 - j, :].rearrange("p (h n) -> p h n", h=2), PS[:, 0:2, :],
                                     ACT.Copy, scale=GT[:, bass.ds(a - 1, 1)]).then_inc(y_rdy, 1)

            act.wait_ge(lc_rdy, 1)
            n = tile_count(act)

            def step(a, j):
                first = isinstance(a, int) and a == 0
                second = isinstance(a, int)
                if not first:
                    loads_next, loads_last = loads_before(act, a + 1), loads_before(act, a - 1)
                if not second:
                    loads, loads_two = loads_before(act, a), loads_before(act, a - 2)
                act.wait_ge(xg_T, 2 * a + 2)
                tokens_of(a + 2, j)
                tokens_low(a + 1, 1 - j)
                if first:
                    split_up(1, 1)
                else:
                    with act.If(loads_next > loads_last):
                        split_up(loads_next, 1 - j)
                act.wait_ge(up_done, a + 1)
                nc.scalar.activation(HF[j], PS[:, 4 + j, 0:INTER], ACT.Silu, scale=1.0 / UPS).then_inc(h_silu, 1)
                act.wait_ge(h_prod, a + 1)
                nc.scalar.activation(HSP[j][:, 0, :], HF[j], ACT.Copy, scale=HS / UPS).then_inc(h_hi, 1)
                if second and not first:
                    act.wait_ge(ri_rdy, 1)
                if second:
                    split_down(1, j)
                else:
                    with act.If(loads > loads_two):
                        split_down(loads, j)
                if not first:
                    last_step(a, j)
                select(a + 1, 1 - j)

            step(0, 0)
            act.wait_ge(gt_rdy, 1)
            step(1, 1)
            with act.Fori(1, MINT // 2) as it:
                step(2 * it, 0)
                step(2 * it + 1, 1)
            with act.Fori(MINT // 2, STEPS // 2) as it:
                with act.If(2 * it <= n):
                    with act.If(2 * it < n):
                        step(2 * it, 0)
                    with act.If(2 * it >= n):
                        last_step(2 * it, 0)
                with act.If(2 * it + 1 <= n):
                    with act.If(2 * it + 1 < n):
                        step(2 * it + 1, 1)
                    with act.If(2 * it + 1 >= n):
                        last_step(2 * it + 1, 1)

        @block.vector
        def _(dve):
            chain = [0]

            def link(ins):
                chain[0] += 1
                ins.then_inc(v_chain, 1)
                dve.wait_ge(v_chain, chain[0])

            v = nc.vector
            norms = [0]

            def bn(i):
                for h in range(2):
                    ins = v.bn_stats(stats[:, i, 6 * h:6 * h + 6], X[:, i, h * 512:(h + 1) * 512])
                link(ins)
                v.bn_aggr(mv[:, i, :], stats[:, i, :]).then_inc(mv_rdy, 1)

            def coefs(lo, n, scale_ap, scale, off_ap):
                sl = slice(lo, lo + n)
                norms[0] += 1
                dve.wait_ge(rstd_rdy, norms[0])
                link(v.tensor_scalar(lnA[:, sl], lnR[:, sl], scale_ap if scale_ap is not None else scale, None, ALU.mult))
                ins = v.scalar_tensor_tensor(lnB[:, sl], mv[:, sl, 0], -1.0, lnA[:, sl], ALU.mult, ALU.mult)
                if off_ap is None:
                    ins.then_inc(coef2, 1)
                    return
                link(ins)
                v.tensor_scalar(lnB[:, sl], lnB[:, sl], off_ap, None, ALU.add).then_inc(coef1, 1)

            def ln1_second():
                for i in range(TB, NT):
                    dve.wait_ge(x_in[i], 16)
                    bn(i)
                coefs(TB, TB, cf[:, 3:4], None, sc6[:, 1:2])

            def round_x(i):
                dve.wait_ge(y_relu, i + 1)
                v.tensor_scalar(rows[:, i % 2, :], rows[:, i % 2, :], QMAX, ROUND, ALU.min, ALU.add).then_inc(y_rnd, 1)

            def evac_q1(i):
                dve.wait_ge(q1_T, 2 * i + 2)
                v.tensor_scalar(Q1T[:, i % TB, 4:8, :].rearrange("p k t -> p (k t)"), PS[:, 3, :], cf[:, 10:11], None,
                                ALU.add).then_inc(q1_rdy[1], 1)

            def round_ctx(b, k):
                r = RING_AT["ctx", b, k]
                dve.wait_ge(c_relu, b * KC + k + 1)
                v.tensor_scalar(ring[:, r % 4, :], ring[:, r % 4, :], QMAX, ROUND, ALU.min, ALU.add).then_inc(c_rnd, 1)

            def lo_chunk(kind, k):
                r = RING_AT[kind, 0, k]
                dve.wait_ge(sw_hi, (k if kind == "sw" else KC + k) + 1)
                W = SW if kind == "sw" else SW3
                v.scalar_tensor_tensor(W[:, 1, k, :], ring[:, r % 4, :], WS, W[:, 0, k, :], ALU.mult,
                                       ALU.subtract).then_inc(sw_lo, 1)

            def row_terms(b):
                dve.wait_ge(r1_done, b + 1)
                v.tensor_scalar(r1[:, :], PS[:, 2, 0:TB], cf[:, 7:8], None, ALU.mult).then_inc(r1_rdy, 1)

            def column_terms(b):
                dve.wait_ge(col_done, b + 1)
                v.tensor_scalar(CT.rearrange("p (h n) -> p h n", h=2), PS[:, 6:8, :], cf[:, 5:6], cf[:, 6:7],
                                ALU.mult, ALU.add).then_inc(col_read, 1)

            def attend(i):
                if i % TB == 0:
                    dve.wait_ge(x_r1, i + 1)
                    dve.wait_ge(col_read, i // TB + 1)
                    link(v.tensor_tensor(X[:, i, :], X[:, i, :], CT, ALU.add))
                dve.wait_ge(at_done, i + 1)
                if i % TB:
                    dve.wait_ge(x_ct, (TB - 1) * (i // TB) + i % TB)
                pb = AT_BANK[i % TB]
                v.scalar_tensor_tensor(X[:, i, :].rearrange("p (h n) -> p h n", h=2), PS[:, pb:pb + 2, :], cf[:, 4:5],
                                       X[:, i, :].rearrange("p (h n) -> p h n", h=2), ALU.mult, ALU.add)\
                    .then_inc(at_read, 1)
                dve.wait_ge(at_read, i + 1)
                bn(i)

            def ln2_lo(i):
                dve.wait_ge(ln_hi, i + 1)
                v.tensor_tensor(WROW[i][:, D:2 * D], rows[:, i % 2, :], WROW[i][:, 0:D], ALU.subtract)\
                    .then_inc(ln_lo, 1)

            def tk_hi_evac(i):
                dve.wait_ge(tk_T, 2 * i + 1)
                v.tensor_copy(XT[:, 0, :, i * P:(i + 1) * P], bank16(2)).then_inc(tk_hi, 1)

            def ln2():
                attend(0)
                attend(1)
                attend(2)
                coefs(0, 2, None, XS, None)
                attend(3)
                ln2_lo(0)
                coefs(2, 2, None, XS, None)
                for i in range(1, TB):
                    ln2_lo(i)
                    tk_hi_evac(i - 1)
                ln1_second()
                tk_hi_evac(TB - 1)

            def su_dve(u):
                dve.wait_ge(su_silu, u + 1)
                v.scalar_tensor_tensor(SA[:, u % 2, :], PS[:, 5 + 2 * (u % 2), :], sbT[:, 1, u % SC:u % SC + 1],
                                       SA[:, u % 2, :], ALU.add, ALU.mult).then_inc(su_hf, 1)
                dve.wait_ge(su_hi, u + 1)
                v.scalar_tensor_tensor(HT[:, 1, u % SC, :], SA[:, u % 2, :], HS / UPS, HT[:, 0, u % SC, :], ALU.mult,
                                       ALU.subtract).then_inc(su_lo, 1)

            def sd_evac(i):
                dve.wait_ge(sd_done, i + 1)
                pb = SD_BANK[i]
                Xi = X[:, i, :].rearrange("p (h n) -> p h n", h=2)
                v.scalar_tensor_tensor(Xi, PS[:, pb:pb + 2, :], cf[:, 11:12], Xi, ALU.mult, ALU.add)\
                    .then_inc(sd_read, 1)

            def small_work():
                dve.wait_ge(bs_hi, 2)
                v.scalar_tensor_tensor(BS[32:64, 0:SI], areaH[32:64, 0:SI], UPS / SELV, BS[32:64, 0:SI], ALU.mult,
                                       ALU.subtract).then_inc(bs_lo, 1)
                v.scalar_tensor_tensor(BS[32:64, SI:], areaH[32:64, SI:SI + D], DNS / SELV, BS[32:64, SI:], ALU.mult,
                                       ALU.subtract).then_inc(bs_lo, 1)
                dve.wait_ge(rw_hi, 1)
                v.scalar_tensor_tensor(RW[:, :, 1, :], RW32[:, :, :], WS, RW[:, :, 0, :], ALU.mult, ALU.subtract)\
                    .then_inc(rw_lo, 1)
                link(v.tensor_copy(rown[:, :], pcol[:, 0:1]))
                link(v.tensor_scalar(sbT[:, 1, :], sbT[:, 1, :], UPS, None, ALU.mult))
                link(v.tensor_scalar(lnR[0:64, 0:1], pcol[0:64, 0:1], float(E), None, ALU.is_equal))
                link(v.tensor_scalar(lnR[0:64, 1:2], pcol[0:64, 0:1], float(32 + E), None, ALU.is_equal))
                link(v.tensor_tensor(lnR[0:64, 0:1], lnR[0:64, 0:1], lnR[0:64, 1:2], ALU.add))
                v.tensor_scalar(SEL[:, 2, :], onesh[0:64, :], lnR[0:64, 0:1], SELV, ALU.mult, ALU.mult)\
                    .then_inc(bs_lo, 1)

            def bc(ap, n):
                return ap.unsqueeze(2).to_broadcast([P, NT, n])

            def over_tiles(ap, n):
                return ap.unsqueeze(1).to_broadcast([P, NT, n])

            def top1(onehot, val, tmp, n):
                link(v.tensor_reduce(m8, val, AX, ALU.max))
                link(v.tensor_tensor(tmp, val, bc(m8, n), ALU.is_equal))
                link(v.tensor_tensor(tmp, tmp, over_tiles(desc[:, E - n:E], n), ALU.mult))
                link(v.tensor_reduce(m8, tmp, AX, ALU.max))
                link(v.tensor_tensor(onehot, over_tiles(desc[:, E - n:E], n), bc(m8, n), ALU.is_equal))

            def route():
                dve.wait_ge(lg_done, 1)
                dve.wait_ge(bias_in, 16 * 13)
                pl = PS[:, 7, 0:2 * P].rearrange("p (t h e) -> p t h e", t=NT, h=2)
                link(v.tensor_copy(lg, pl[:, :, 0, :]))
                v.tensor_tensor(lg, lg, pl[:, :, 1, :], ALU.add).then_inc(lg_read, 1)
                dve.wait_ge(lg_read, 1)
                link(v.scalar_tensor_tensor(lg, lg, 1.0 / UPS, over_tiles(rb[:, 0, :], E), ALU.mult, ALU.add))
                link(v.tensor_reduce(m8, lg, AX, ALU.max))
                v.tensor_tensor(lg, lg, bc(m8, E), ALU.subtract).then_inc(lg_sub, 1)
                dve.wait_ge(lg_exp, 1)
                link(v.tensor_reduce(m8, t1, AX, ALU.add))
                link(v.reciprocal(m8, m8))
                link(v.tensor_tensor(sco, t1, bc(m8, E), ALU.mult))
                link(v.tensor_tensor(sco, sco, over_tiles(rb[:, 1, :], E), ALU.add))
                link(v.tensor_reduce(gm.rearrange("p t g -> p (t g)"),
                                     sco.rearrange("p t (g e) -> p (t g) e", g=GROUPS), AX, ALU.max))
                top1(go[0], gm, gt, GROUPS)
                link(v.scalar_tensor_tensor(gm, go[0], -BIG, gm, ALU.mult, ALU.add))
                top1(go[1], gm, gt, GROUPS)
                link(v.tensor_tensor(go[0], go[0], go[1], ALU.add))
                keep = go[0].rearrange("p t g -> p (t g)").unsqueeze(2).to_broadcast([P, NT * GROUPS, E // GROUPS])
                G4 = "p t (g e) -> p (t g) e"
                link(v.tensor_tensor(t2.rearrange(G4, g=GROUPS), sco.rearrange(G4, g=GROUPS), keep, ALU.mult))
                link(v.tensor_scalar(go[1], go[0], 1.0, BIG, ALU.subtract, ALU.mult))
                drop = go[1].rearrange("p t g -> p (t g)").unsqueeze(2).to_broadcast([P, NT * GROUPS, E // GROUPS])
                link(v.tensor_tensor(t2.rearrange(G4, g=GROUPS), t2.rearrange(G4, g=GROUPS), drop, ALU.add))
                top1(oh[0], t2, t1, E)
                link(v.scalar_tensor_tensor(t2, oh[0], -2.0 * BIG, t2, ALU.mult, ALU.add))
                top1(oh[1], t2, t1, E)
                for c in range(2):
                    link(v.tensor_tensor(t1, sco, oh[c], ALU.mult))
                    link(v.tensor_reduce(m8, t1, AX, ALU.add))
                    link(v.tensor_scalar(CV[:, c, :], m8, cf[:, 1:2], GS, ALU.mult, ALU.mult))
                CVf = CV.rearrange("p c t -> p (c t)")
                link(v.tensor_copy(CVS[:, 0, :], CVf))
                link(v.tensor_tensor(CVS[:, 1, :], CVf, CVS[:, 0, :], ALU.subtract))
                v.tensor_tensor(Mh, oh[0], oh[1], ALU.add).then_inc(m_rdy, 1)

            def place():
                dve.wait_ge(rank_done, 1)
                cnt = PS[:, 7, 0:P].rearrange(TE, t=NT)
                rank = PS[:, 7, P:2 * P].rearrange(TE, t=NT)
                link(v.memset(run[:, 0, :], 0.0))
                for t in range(NT):
                    link(v.tensor_tensor(run[:, t + 1, :], run[:, t, :], cnt[:, t, :], ALU.add))
                v.tensor_tensor(lg, rank, run[:, 0:NT, :], ALU.add).then_inc(rank_read, 1)
                n8 = big[:, 0:P].rearrange("p (e t) -> p e t", e=E)
                link(v.tensor_scalar(m8, iota[:, 0:NT], float(P), None, ALU.mult))
                link(v.tensor_tensor(n8, run[:, NT, :].unsqueeze(2).to_broadcast([P, E, NT]),
                                     m8.unsqueeze(1).to_broadcast([P, E, NT]), ALU.is_gt))
                link(v.tensor_reduce(ntl, n8, AX, ALU.add))
                link(v.memset(sA, 0.0))
                link(v.memset(sB, 0.0))
                link(v.tensor_copy(sA[:, 8:], ntl))
                src, dst = sA, sB
                for s in (1, 2, 4, 8):
                    link(v.tensor_tensor(dst[:, 8:], src[:, 8:], src[:, 8 - s:8 + E - s], ALU.add))
                    src, dst = dst, src
                tend = src[:, 8:]
                link(v.tensor_tensor(base, tend, ntl, ALU.subtract))
                link(v.tensor_scalar(base, base, float(P), None, ALU.mult))
                ec = ECM[:, 0:32 * E].rearrange("p (a e) -> p a e", e=E)
                ef = stats[:, :, :].rearrange("p a b -> p (a b)")
                link(v.tensor_tensor(ec, iota[:, 0:32].unsqueeze(2).to_broadcast([P, 32, E]),
                                     tend.unsqueeze(1).to_broadcast([P, 32, E]), ALU.is_ge))
                link(v.memset(ef[:, 0:COLS], float(E - 1)))
                link(v.tensor_reduce(ef[:, 0:32], ec, AX, ALU.add))
                link(v.tensor_scalar(ef[:, 0:32], ef[:, 0:32], float(E - 1), None, ALU.min))
                link(v.tensor_copy(EL[:, :], ef[:, 0:COLS]))
                link(v.tensor_scalar(ef[32:64, 0:COLS], ef[32:64, 0:COLS], 32.0, None, ALU.add))
                link(v.tensor_copy(ntiles[:, :], tend[:, E - 1:E]))
                v.tensor_scalar(SELQ[:, :], ef[0:64, 0:COLS], pcol[0:64, 0:1], SELV, ALU.is_equal, ALU.mult)\
                    .then_inc(el_rdy, 1)
                dve.wait_ge(rank_read, 1)
                link(v.tensor_tensor(lg, lg, base.unsqueeze(1).to_broadcast([P, NT, E]), ALU.add))
                for c in range(2):
                    link(v.tensor_tensor(t1, lg, oh[c], ALU.mult))
                    link(v.tensor_reduce(pos[:, c, :], t1, AX, ALU.add))
                link(v.tensor_scalar(ef[:, 40:73], iota[:, 0:33], float(P), None, ALU.mult))
                G = GE.rearrange("p j t a -> p (j t) a")
                pf = pos.rearrange("p j t -> p (j t)")
                link(v.tensor_tensor(G, pf.unsqueeze(2).to_broadcast([P, 2 * NT, 33]),
                                     ef[:, 40:73].unsqueeze(1).to_broadcast([P, 2 * NT, 33]), ALU.is_ge))
                af = aa.rearrange("p j t -> p (j t)")
                bf = bb.rearrange("p j t -> p (j t)")
                link(v.tensor_reduce(af, G, AX, ALU.add))
                link(v.tensor_scalar(af, af, 1.0, -float(P), ALU.subtract, ALU.mult))
                link(v.tensor_tensor(bf, pf, af, ALU.add))
                link(v.tensor_tensor(OA[:, :, 0, :], G[:, :, 0:32], G[:, :, 1:33], ALU.subtract))
                link(v.tensor_scalar(lack[:, :], OA[:, 0, 0, :], -1.0, 1.0, ALU.mult, ALU.add))
                link(v.tensor_tensor(lack[:, :], lack[:, :], OA[:, NT, 0, :], ALU.subtract))
                for w in range(2):
                    link(v.tensor_tensor(OA[:, :, 1 + w, :], OA[:, :, 0, :],
                                         CVS[:, w, :].unsqueeze(2).to_broadcast([P, 2 * NT, 32]), ALU.mult))
                tk = pcol[:, 0:NT].unsqueeze(2).to_broadcast([P, NT, 32])
                for c in range(2):
                    o = OA[:, c * NT:(c + 1) * NT, 0, :]
                    link(v.scalar_tensor_tensor(o, tk, -float(T), o, ALU.add, ALU.mult))
                v.tensor_tensor(OB.rearrange("p j t s -> p (j t) s"), bf.unsqueeze(2).to_broadcast([P, 2 * NT, P]),
                                iota[:, :].unsqueeze(1).to_broadcast([P, 2 * NT, P]), ALU.is_equal).then_inc(slot_rdy, 1)

            def count_loads():
                pad = 32
                sums = [big[:, 0:pad + COLS], big[:, 128:128 + pad + COLS]]
                expert, load = big[:, 256:256 + COLS], big[:, 320:320 + COLS]
                nt = big[:, 384:385]
                link(v.memset(big[:, 0:256], 0.0))
                link(v.tensor_copy(expert, EL[:, :]))
                link(v.tensor_copy(nt, ntiles[:, :]))
                link(v.tensor_tensor(load[:, 2:], expert[:, 2:], expert[:, 0:COLS - 2], ALU.not_equal))
                link(v.memset(load[:, 0:2], 1.0))
                link(v.scalar_tensor_tensor(sums[0][:, pad:], iota[:, 0:COLS], nt, load, ALU.is_lt, ALU.mult))
                for q, sh in enumerate((2, 4, 8, 16, 32)):
                    src, dst = sums[q % 2], sums[1 - q % 2]
                    link(v.tensor_tensor(dst[:, pad:], src[:, pad:], src[:, pad - sh:pad + COLS - sh], ALU.add))
                v.tensor_copy(LC[:, :], sums[1][:, pad:]).then_inc(lc_rdy, 1)

            for i in range(2):
                dve.wait_ge(x_in[i], 16)
                bn(i)
            dve.wait_ge(small_in, 96)
            link(v.reciprocal(cf[:, 2:3], sc6[:, 2:3]))
            v.memset(cf[:, 10:11], -(ROUND + HALF)).then_inc(tanh_rdy, 1)
            link(v.reciprocal(cf[:, 3:4], sc6[:, 0:1]))
            dve.wait_ge(x_in[2], 16)
            bn(2)
            coefs(0, 2, cf[:, 3:4], None, sc6[:, 1:2])
            dve.wait_ge(x_in[3], 16)
            bn(3)
            dve.wait_ge(consts, 10)
            round_ctx(0, 0)
            link(v.tensor_scalar(cf[:, 8:9], sc6[:, 1:2], -1.0, HALF, ALU.mult, ALU.add))
            link(v.tensor_scalar(cf[:, 9:10], sc6[:, 3:4], -1.0, HALF, ALU.mult, ALU.add))
            dve.wait_ge(tanh_rdy, 2)
            link(v.tensor_scalar(cf[:, 4:5], cf[:, 0:1], sc6[:, 0:1], sc6[:, 2:3], ALU.mult, ALU.mult))
            link(v.tensor_scalar(cf[:, 5:6], cf[:, 4:5], cf[:, 8:9], None, ALU.mult))
            link(v.tensor_scalar(cf[:, 7:8], cf[:, 4:5], cf[:, 9:10], None, ALU.mult))
            link(v.tensor_scalar(cf[:, 6:7], cf[:, 5:6], cf[:, 9:10], float(D), ALU.mult, ALU.mult))
            link(v.tensor_scalar(cf[:, 11:12], cf[:, 1:2], 1.0 / DNS, None, ALU.mult))
            coefs(2, 2, cf[:, 3:4], None, sc6[:, 1:2])
            round_x(0)
            round_x(1)
            for k in range(1, 4):
                round_ctx(0, k)
            for i in range(TB):
                evac_q1(i)
                if i + 2 < TB:
                    round_x(i + 2)
                if i:
                    round_ctx(0, i + 3)
            round_ctx(0, KC - 1)
            small_work()
            row_terms(0)
            for k in range(KC // 2):
                lo_chunk("sw", k)
            column_terms(0)
            ln2()

            round_x(TB)
            round_x(TB + 1)
            for c in range(SC):
                round_ctx(1, 2 * c)
                round_ctx(1, 2 * c + 1)
                su_dve(c)
                for i in ((TB, TB + 1), (TB + 2,), (TB + 3,), ())[c]:
                    evac_q1(i)
                    if i + 2 < NT:
                        round_x(i + 2)
            row_terms(1)
            for c in range(SC):
                lo_chunk("sw3", c)
            column_terms(1)
            for i in range(TB, NT):
                attend(i)
            coefs(TB, TB, None, XS, None)
            for i in range(TB):
                ln2_lo(TB + i)
                if i % 2:
                    sd_evac(i - 1)
                    sd_evac(i)
            for i in range(TB, NT):
                tk_hi_evac(i)
            route()
            for c in range(SC):
                su_dve(SC + c)
            place()
            dve.wait_ge(ti_done, 1)
            v.tensor_scalar(TI[:, 0:32], PS[:, 7, 0:32], -1.0, float(T), ALU.min, ALU.add).then_inc(ti_rdy, 1)
            link(v.tensor_copy(slots[:, :], PS[:, 7, 0:P]))
            v.tensor_scalar(empty[:, :], slots[:, 0:32], 0.0, None, ALU.is_equal).then_inc(empty_rdy, 1)
            count_loads()

            def split_up(loads, j, quarters=range(4)):
                for q in quarters:
                    dve.wait_ge(w12_hi[j], 4 * loads + q + 1)
                    ks = slice(2 * q, 2 * q + 2)
                    v.scalar_tensor_tensor(W12S[j][:, 1, ks, :], W12F[j][:, ks, :], WS, W12S[j][:, 0, ks, :], ALU.mult,
                                           ALU.subtract).then_inc(w12_lo[j], 1)

            def tokens_high(t, j):
                dve.wait_ge(xg_T, 2 * t + 1)
                v.tensor_copy(XGT[j][:, 0, :, :], bank16(2)).then_inc(xg_hi, 1)

            for j in range(2):
                dve.sem_inc(w12_lo[j], 4)
            split_up(1, 0)
            tokens_high(0, 0)

            def split_down(loads, j):
                for q in range(HC):
                    dve.wait_ge(w3_hi[j], 2 * loads + q + 1)
                    v.scalar_tensor_tensor(W3S[j][:, 1, q, :], W3F[:, q, :], WS, W3S[j][:, 0, q, :], ALU.mult,
                                           ALU.subtract).then_inc(w3_lo[j], 1)

            def last_step(a, j):
                dve.wait_ge(hT_done, a)
                v.tensor_copy(HTS[1 - j].rearrange("p h c t -> p (h c t)"), PS[:, 6, 0:256].bitcast(F16))\
                    .then_inc(hT_rdy, 1)

            def gates_and_rows():
                dve.wait_ge(empty_done, 1)
                link(v.tensor_tensor(spare[:, :], slots[:, 96:128], PS[:, 7, 128:160], ALU.subtract))
                link(v.scalar_tensor_tensor(spare[:, :], spare[:, :], float(P + 1), lack[:, :], ALU.add, ALU.mult))
                link(v.tensor_scalar(spare[:, :], spare[:, :], -1.0, None, ALU.add))
                link(v.tensor_scalar(GT[:, :], slots[:, 32:64], 1.0 / (GS * DNS), None, ALU.mult))
                v.scalar_tensor_tensor(GT[:, :], slots[:, 64:96], 1.0 / (GS * DNS), GT[:, :], ALU.mult, ALU.add)\
                    .then_inc(gt_rdy, 1)
                link(v.scalar_tensor_tensor(slots[:, 0:32], empty[:, :], -float(T), slots[:, 0:32], ALU.mult, ALU.add))

            def fill(t):
                v.tensor_tensor(FILL[:, t:t + 16, :], spare[:, t:t + 16].unsqueeze(2).to_broadcast([P, 16, P]),
                                iota[:, :].unsqueeze(1).to_broadcast([P, 16, P]), ALU.is_equal).then_inc(fill_rdy, 1)

            dve.wait_ge(lc_rdy, 1)
            n = tile_count(dve)

            def step(a, j):
                first = isinstance(a, int) and a == 0
                second = isinstance(a, int)
                if not first:
                    loads_next, loads_last = loads_before(dve, a + 1), loads_before(dve, a - 1)
                if not second:
                    loads, loads_two = loads_before(dve, a), loads_before(dve, a - 2)
                tokens_high(a + 1, 1 - j)
                if first:
                    gates_and_rows()
                    fill(0)
                if not first:
                    last_step(a, j)
                if second and not first:
                    fill(16)
                if first:
                    split_up(1, 1)
                else:
                    with dve.If(loads_next > loads_last):
                        split_up(loads_next, 1 - j, range(2))
                dve.wait_ge(h_silu, a + 1)
                v.tensor_tensor(HF[j], PS[:, 4 + j, INTER:2 * INTER], HF[j], ALU.mult).then_inc(h_prod, 1)
                dve.wait_ge(h_hi, a + 1)
                v.scalar_tensor_tensor(HSP[j][:, 1, :], HF[j], HS / UPS, HSP[j][:, 0, :], ALU.mult,
                                       ALU.subtract).then_inc(h_lo, 1)
                if not first:
                    with dve.If(loads_next > loads_last):
                        split_up(loads_next, 1 - j, range(2, 4))
                if second and not first:
                    dve.wait_ge(fill_done, 1)
                    v.scalar_tensor_tensor(RI[:, :], PS[:, 7, 160:192], float(T), slots[:, 0:32], ALU.add, ALU.add)\
                        .then_inc(ri_rdy, 1)
                if second:
                    split_down(1, j)
                else:
                    with dve.If(loads > loads_two):
                        split_down(loads, j)

            step(0, 0)
            step(1, 1)
            with dve.Fori(1, MINT // 2) as it:
                step(2 * it, 0)
                step(2 * it + 1, 1)
            with dve.Fori(MINT // 2, STEPS // 2) as it:
                with dve.If(2 * it <= n):
                    with dve.If(2 * it < n):
                        step(2 * it, 0)
                    with dve.If(2 * it >= n):
                        last_step(2 * it, 0)
                with dve.If(2 * it + 1 <= n):
                    with dve.If(2 * it + 1 < n):
                        step(2 * it + 1, 1)
                    with dve.If(2 * it + 1 >= n):
                        last_step(2 * it + 1, 1)

        @block.tensor
        def _(pe):
            mm = nc.tensor.matmul
            pe.wait_ge(ident_rdy, 3)

            def transpose_q1(i):
                pe.wait_ge(y_rnd, i + 1)
                for h in range(2):
                    if i:
                        pe.wait_ge(q1_rdy[h], i)
                    for k in range(4):
                        last = nc.tensor.transpose(PS[:, 2 + h, k * P:(k + 1) * P],
                                                   rows[:, i % 2, (4 * h + k) * P:(4 * h + k + 1) * P], idf[:, :])
                    last.then_inc(q1_T, 1)

            def product(i, h, k):
                return mm(PS[:, AT_BANK[i % TB] + h, :], Q1T[:, i % TB, k, :], Q2[:, k, h * 512:(h + 1) * 512],
                          start=(k == 0), stop=(k == KC - 1))

            def attention_chunk(b, k):
                if k == 0:
                    for q in range(2):
                        pe.wait_ge(q1_rdy[q], TB * b + 2)
                    if b:
                        pe.wait_ge(su_hf, SC)
                pe.wait_ge(q2_rdy, KC * b + k + 1)
                for h in range(2):
                    last = mm(PS[:, 6 + h, :], onesb[:, :], Q2[:, k, h * 512:(h + 1) * 512], start=(k == 0),
                              stop=(k == KC - 1))
                if k == KC - 1:
                    last.then_inc(col_done, 1)
                for i in (b * TB, b * TB + 1):
                    for h in range(2):
                        last = product(i, h, k)
                    if k == KC - 1:
                        last.then_inc(at_done, 1)

            def row_sums(b):
                for q in range(2):
                    pe.wait_ge(q1_rdy[q], TB * (b + 1))
                for j in range(TB):
                    for k in range(KC):
                        last = mm(PS[:, 2, j:j + 1], Q1T[:, j, k, :], onesb[:, 0:1], start=(k == 0), stop=(k == KC - 1))
                last.then_inc(r1_done, 1)

            def attention_rest(b):
                pe.wait_ge(r1_rdy, b + 1)
                for i in (b * TB + 2, b * TB + 3):
                    if i % TB == 3:
                        pe.wait_ge(at_read, b * TB + 1)
                    for h in range(2):
                        for k in range(KC):
                            last = product(i, h, k)
                    last.then_inc(at_done, 1)

            def transpose_tokens(i):
                pe.wait_ge(ln_hi, i + 1)
                if i:
                    pe.wait_ge(tk_hi, i)
                if i == 0:
                    pe.wait_ge(at_read, TB - 1)
                if i == TB:
                    pe.wait_ge(sd_read, 2)
                for k in range(KC):
                    last = nc.tensor.transpose(bank16(2)[:, k, :], WROW[i][:, k * P:(k + 1) * P], idh[:, :])
                last.then_inc(tk_T, 1)
                pe.wait_ge(ln_lo, i + 1)
                if i:
                    pe.wait_ge(tk_lo, i)
                for k in range(KC):
                    last = nc.tensor.transpose(bank16(3)[:, k, :], WROW[i][:, D + k * P:D + (k + 1) * P], idh[:, :])
                last.then_inc(tk_T, 1)

            def shared_up(half, c, w, lo=0, hi=S):
                tk = slice(half * S + lo, half * S + hi)
                if c >= 2:
                    pe.wait_ge(su_hf, half * SC + c - 1)
                for k in range(KC):
                    if half == 0 and c == 0 and w == 0 and lo == 0 and k >= KC // 2:
                        pe.wait_ge(sw_lo2, k - KC // 2 + 1)
                    for n, (wp, xp) in enumerate(((0, 0), (0, 1), (1, 0))):
                        last = mm(PS[:, 4 + 2 * (c % 2) + w, lo:hi], SW[:, wp, k, w * SI + c * P:w * SI + (c + 1) * P],
                                  XT[:, xp, k, tk], start=(k == 0 and n == 0), stop=(k == KC - 1 and n == 2))
                if w == 1 and hi == S:
                    last.then_inc(su_done, 1)

            def shared_down(tile):
                pb, i = SD_BANK[tile], tile % TB
                for h in range(2):
                    hs = slice(h * 512, (h + 1) * 512)
                    for c in range(SC):
                        for n, (hp, wp) in enumerate(((0, 0), (1, 0), (0, 1))):
                            mm(PS[:, pb + h, :], HT[:, hp, c, i * P:(i + 1) * P], SW3[:, wp, c, hs],
                               start=(c == 0 and n == 0), stop=False)
                    last = mm(PS[:, pb + h, :], SEL[:, 2, :], BS[:, SI + h * 512:SI + (h + 1) * 512], start=False,
                              stop=True)
                last.then_inc(sd_done, 1)

            def router(i):
                o = PS[:, 7, i * 2 * E:(i + 1) * 2 * E]
                for k in range(KC):
                    mm(o, XT[:, 0, k, i * P:(i + 1) * P], RW[:, k, :, :].rearrange("p h e -> p (h e)"),
                       start=(k == 0), stop=False)
                    last = mm(o[:, 0:E], XT[:, 1, k, i * P:(i + 1) * P], RW[:, k, 0, :], start=False,
                              stop=(k == KC - 1))
                if i == NT - 1:
                    last.then_inc(lg_done, 1)

            for i in range(TB - 1):
                transpose_q1(i)
            attention_chunk(0, 0)
            transpose_q1(TB - 1)
            for k in range(1, KC):
                attention_chunk(0, k)
                if k == 2:
                    row_sums(0)
            attention_rest(0)
            for i in range(TB - 1):
                transpose_tokens(i)
            pe.wait_ge(tk_hi, 2)
            pe.wait_ge(tk_lo, 2)
            pe.wait_ge(sw_lo, KC // 2)
            pe.wait_ge(at_read, 2)
            shared_up(0, 0, 0, 0, S // 2)
            transpose_tokens(TB - 1)
            shared_up(0, 0, 1, 0, S // 2)
            pe.wait_ge(tk_hi, TB)
            pe.wait_ge(tk_lo, TB)
            shared_up(0, 0, 0, S // 2, S)
            shared_up(0, 0, 1, S // 2, S)
            transpose_q1(TB)
            for c in range(1, SC):
                shared_up(0, c, 0)
                transpose_q1(TB + c)
                shared_up(0, c, 1)
            row_sums(1)
            for k in range(KC):
                attention_chunk(1, k)
            attention_rest(1)
            pe.wait_ge(su_lo, SC)
            pe.wait_ge(sw_lo, KC // 2 + SC)
            pe.wait_ge(bs_lo, 3)
            pe.wait_ge(q1_rdy[0], NT)
            pe.wait_ge(q1_rdy[1], NT)
            pe.wait_ge(r1_rdy, B)
            for i in range(TB):
                if i == 2:
                    pe.wait_ge(col_read, B)
                else:
                    pe.wait_ge(at_read, TB + (2, 3, None, TB)[i])
                shared_down(i)
            pe.wait_ge(rw_lo, 1)
            for i in range(TB, NT):
                transpose_tokens(i)
                if i == TB:
                    pe.wait_ge(sd_read, TB - 1)
                router(i - TB)
                if i > TB:
                    pe.wait_ge(tk_hi, i)
                    pe.wait_ge(tk_lo, i)
                    router(i - 1)
            pe.wait_ge(tk_hi, NT)
            pe.wait_ge(tk_lo, NT)
            router(NT - 1)
            for c in range(SC):
                if c == 1:
                    pe.wait_ge(lg_read, 1)
                shared_up(1, c, 0)
                shared_up(1, c, 1)
            pe.wait_ge(m_rdy, 1)
            pe.wait_ge(su_hf, 2 * SC)
            Mf = Mh.rearrange("p t e -> p (t e)")
            mm(PS[:, 7, 0:P], onesh[:, :], Mf, start=True, stop=True)
            mm(PS[:, 7, P:2 * P], tri[:, :], Mf, start=True, stop=True).then_inc(rank_done, 1)
            pe.wait_ge(su_lo, 2 * SC)
            for i in range(TB - 1):
                shared_down(TB + i)
            pe.wait_ge(slot_rdy, 1)
            for n in range(2 * NT):
                c, t = n // NT, n % NT
                last = mm(PS[:, 7, 0:96], OB[:, c, t, :], OA[:, n, :, :].rearrange("p w a -> p (w a)"), start=(n == 0),
                          stop=(n == 2 * NT - 1))
            mm(PS[:, 7, 96:128], tri[:, :], lack[:, :], start=True, stop=True).then_inc(ti_done, 1)
            pe.wait_ge(sd_copied, 1)
            shared_down(NT - 1)
            pe.wait_ge(empty_rdy, 1)
            mm(PS[:, 7, 128:160], onesh[:, :], empty[:, :], start=True, stop=True).then_inc(empty_done, 1)
            pe.wait_ge(sd_copied, 2)

            def transpose_gathered(t, par, count):
                pe.wait_ge(tok_in[par], count)
                for h in range(2):
                    if not (isinstance(t, int) and t == 0):
                        pe.wait_ge(xg_hi if h == 0 else xg_lo, t)
                    for k in range(KC):
                        last = nc.tensor.transpose(bank16(2 + h)[:, k, :], XG[par][:, h, k * P:(k + 1) * P], idh[:, :])
                    last.then_inc(xg_T, 1)

            transpose_gathered(0, 0, 16)
            pe.wait_ge(lc_rdy, 1)
            n = tile_count(pe)
            pe.wait_ge(sd_copied, TB)

            def transpose_inner(a, j):
                pe.wait_ge(h_hi, a)
                pe.wait_ge(h_lo, a)
                if not (isinstance(a, int) and a < 2):
                    pe.wait_ge(hT_rdy, a - 1)
                ht = PS[:, 6, 0:256].bitcast(F16).rearrange("p (n t) -> p n t", n=2 * HC)
                for n in range(2 * HC):
                    last = nc.tensor.transpose(ht[:, n, :], HSP[1 - j][:, n // HC, (n % HC) * P:(n % HC + 1) * P],
                                               idh[:, :])
                last.then_inc(hT_done, 1)

            def down(a, j, loads_last):
                pe.wait_ge(hT_rdy, a)
                pe.wait_ge(w3_lo[1 - j], 2 * loads_last)
                if not (isinstance(a, int) and a < 2):
                    pe.wait_ge(y_rdy, a - 1)
                for h in range(2):
                    hs = slice(h * 512, (h + 1) * 512)
                    for c in range(HC):
                        for n, (hp, wp) in enumerate(((0, 0), (1, 0), (0, 1))):
                            mm(PS[:, h, :], HTS[1 - j][:, hp, c, :], W3S[1 - j][:, wp, c, hs],
                               start=(c == 0 and n == 0), stop=False)
                    last = mm(PS[:, h, :], SEL[:, 1 - j, :], BS[:, SI + h * 512:SI + (h + 1) * 512], start=False,
                              stop=True)
                last.then_inc(dn_done, 1)

            def step(a, j):
                known = isinstance(a, int)
                first = known and a == 0
                loads = loads_before(pe, a)
                loads_last = 0 if first else loads_before(pe, a - 1)
                transpose_gathered(a + 1, 1 - j, 8 * a + (16 if j == 0 else 24))
                second = known and a == 1
                if not first and not second:
                    transpose_inner(a, j)
                pe.wait_ge(xg_hi, a + 1)
                pe.wait_ge(xg_lo, a + 1)
                if not (known and a < 2):
                    pe.wait_ge(h_prod, a - 1)
                for k in range(KC):
                    if k % 2 == 0:
                        pe.wait_ge(w12_lo[j], 4 * loads + 1 + k // 2)
                    for n, (xp, wp) in enumerate(((0, 0), (0, 1), (1, 0))):
                        mm(PS[:, 4 + j, :], XGT[j][:, xp, k, :], W12S[j][:, wp, k, :], start=(k == 0 and n == 0),
                           stop=False)
                pe.wait_ge(sel_rdy, a + 1)
                mm(PS[:, 4 + j, :], SEL[:, j, :], BS[:, 0:SI], start=False, stop=True).then_inc(up_done, 1)
                if second:
                    transpose_inner(a, j)
                if not first:
                    down(a, j, loads_last)
                if second:
                    pe.wait_ge(fill_rdy, 2)
                    for t in range(32):
                        last = mm(PS[:, 7, 160 + t:161 + t], FILL[:, t, :], rown[:, 0:1], start=True, stop=True)
                    last.then_inc(fill_done, 1)

            def last_step(a, j):
                loads_last = loads_before(pe, a - 1)
                transpose_inner(a, j)
                down(a, j, loads_last)

            step(0, 0)
            step(1, 1)
            with pe.Fori(1, MINT // 2) as it:
                step(2 * it, 0)
                step(2 * it + 1, 1)
            with pe.Fori(MINT // 2, STEPS // 2) as it:
                with pe.If(2 * it <= n):
                    with pe.If(2 * it < n):
                        step(2 * it, 0)
                    with pe.If(2 * it >= n):
                        last_step(2 * it, 0)
                with pe.If(2 * it + 1 <= n):
                    with pe.If(2 * it + 1 < n):
                        step(2 * it + 1, 1)
                    with pe.If(2 * it + 1 >= n):
                        last_step(2 * it + 1, 1)


_INS = ["x", "ctx_4096", "g_xattn", "g_ffn", "L0_xattn_x1_scale", "L0_xattn_x1_zp", "L0_xattn_x2_scale",
        "L0_xattn_x2_zp", "L0_ffn_router_w", "L0_ffn_router_b", "L0_ffn_router_bias", "L0_ffn_ew1", "L0_ffn_eb1",
        "L0_ffn_ew2", "L0_ffn_eb2", "L0_ffn_ew3", "L0_ffn_eb3", "L0_ffn_sw1", "L0_ffn_sb1", "L0_ffn_sw2",
        "L0_ffn_sb2", "L0_ffn_sw3", "L0_ffn_sb3"]
_OUTS = [((2, 512, 1024), "float32")]


def kernel(**inputs):
    import numpy as _np
    import concourse.bacc as _bacc
    from concourse import mybir as _mybir
    from concourse.bass_utils import run_bass_kernel_spmd as _run

    nc = _bacc.Bacc("TRN2", target_bir_lowering=False, num_devices=1)
    arrays, args = {}, []
    for name in _INS:
        a = _np.ascontiguousarray(inputs[name])
        arrays[f"in_{name}_dram"] = a
        args.append(nc.dram_tensor(f"in_{name}_dram", a.shape, _mybir.dt.from_np(a.dtype), kind="ExternalInput").ap())
    for i, (shape, dtype) in enumerate(_OUTS):
        dt = _mybir.dt.from_np(_np.dtype(dtype))
        args.append(nc.dram_tensor(f"out_{i}_dram", shape, dt, kind="ExternalOutput").ap())
    build(nc, *args)
    r = _run(nc, [arrays], core_ids=[0])
    got = tuple(r.results[0][f"out_{i}_dram"] for i in range(len(_OUTS)))
    return got[0]
```
